# Optimizing a Trainium2 kernel written in Bass

```python
import numpy as np
import jax
import jax.numpy as jnp

def _softmax(x, axis=-1):
    return jax.nn.softmax(x, axis=axis)

def _gelu(x):
    return jax.nn.gelu(x, approximate=True)

def _silu(x):
    return jax.nn.silu(x)

def _sigmoid(x):
    return jax.nn.sigmoid(x)

def _layernorm(x, axis=-1, eps=1e-05):
    m = jnp.mean(x, axis=axis, keepdims=True)
    v = jnp.var(x, axis=axis, keepdims=True)
    return (x - m) / jnp.sqrt(v + eps)

def _scatter_add(tgt, idx, src, axis=0):
    return tgt.at[idx].add(src)

def _segment_sum(src, seg, n):
    return jax.ops.segment_sum(src, seg, n)
kernel_name = 'mk_flamingo_gated_d4_seqx_r8_ca270d'

def setup_inputs(seed: int=0):
    np.random.seed(seed)
    _w = jnp.asarray

    def _rec_inputs():
        import jax
        import jax.numpy as jnp
        _rk = jax.random.key(seed)
        x = -0.0003929 + 0.9999 * jax.random.normal(jax.random.fold_in(_rk, 1), (8, 128, 256), jnp.float32)
        _lenS = 128 - jax.random.randint(jax.random.fold_in(_rk, 7), (8,), 0, max(1, 128 // 4) + 1, jnp.int32)
        _lenS2 = 128 - jax.random.randint(jax.random.fold_in(_rk, 8), (8,), 0, max(1, 128 // 4) + 1, jnp.int32)
        _ctx_1024P = jax.random.normal(jax.random.fold_in(_rk, 11), (8, 16, 128), jnp.float32)
        _ctx_1024c = jax.random.dirichlet(jax.random.fold_in(_rk, 511), 0.3 * jnp.ones((16,), jnp.float32), (8, 128))
        _ctx_1024t = jnp.einsum('bsk,bkd->bsd', _ctx_1024c, _ctx_1024P)
        _ctx_1024t = _ctx_1024t * jax.lax.rsqrt(jnp.mean(jnp.square(_ctx_1024t)) + 1e-12) * 0.953939
        ctx_1024 = 0.000227908 + 0.99994 * (_ctx_1024t + 0.3 * jax.random.normal(jax.random.fold_in(_rk, 611), (8, 128, 128), jnp.float32))
        fside_BxSx2_0 = jax.random.uniform(jax.random.fold_in(_rk, 13), (8, 128, 2), jnp.float32, 0.0, 0.999707)
        _validS = jnp.arange(128)[None, :] < _lenS[:, None]
        _validS2 = jnp.arange(128)[None, :] < _lenS2[:, None]
        _causal = jnp.tril(jnp.ones((128, 128), dtype=bool))
        mask_BxS2_bf1 = jnp.ones((8, 128), dtype=bool)
        _g = jax.random.normal(jax.random.fold_in(_rk, 9001), (2, 4), jnp.float32)
        _g = jnp.sign(_g) * jnp.maximum(jnp.abs(_g), 1.0) + (_g == 0) * 1.0
        g_xattn = _g[0]
        g_ffn = _g[1]
        return (x, ctx_1024, fside_BxSx2_0, mask_BxS2_bf1, g_xattn, g_ffn)
    x, ctx_1024, fside_BxSx2_0, mask_BxS2_bf1, g_xattn, g_ffn = _rec_inputs()

    def _L0_xattn_setup():
        import jax, jax.numpy as jnp
        import numpy as np
        EPS = 1e-05

        def rmsnorm(x, g, eps=EPS):
            var = jnp.mean(jnp.square(x), axis=-1, keepdims=True)
            return x * jax.lax.rsqrt(var + eps) * g
        key = jax.random.key(seed)
        ks = jax.random.split(key, 8)
        B, Sq, Skv = (2, 512, 64)
        dim, cdim, H, D = (256, 128, 16, 128)
        inner = H * D
        s = lambda f: 1.0 / np.sqrt(f)
        return {'hidden_states': jax.random.normal(ks[0], (B, Sq, dim), jnp.float32), 'encoder_hidden_states': jax.random.normal(ks[1], (B, Skv, cdim), jnp.float32), 'Wq': jax.random.normal(ks[2], (dim, inner), jnp.float32) * s(dim), 'Wk': jax.random.normal(ks[3], (cdim, inner), jnp.float32) * s(cdim), 'Wv': jax.random.normal(ks[4], (cdim, inner), jnp.float32) * s(cdim), 'Wo': jax.random.normal(ks[5], (inner, dim), jnp.float32) * s(inner), 'gq': jnp.ones((D,), jnp.float32), 'gk': jnp.ones((D,), jnp.float32)}
    _L0_xattn_all = _L0_xattn_setup()
    _L0_xattn_in = {k: v for k, v in _L0_xattn_all.items() if k in ('Wq', 'Wk', 'Wv', 'Wo', 'gq', 'gk')}
    del _L0_xattn_all

    def _L0_ffn_setup():
        import jax, jax.numpy as jnp
        import numpy as np
        BLOCK_SIZE = 32
        HIDDEN_SIZE = 256
        MLP_DIM = 2048
        NVFP4_LUT = jnp.array([0.0, 0.5, 1.0, 1.5, 2.0, 3.0, 4.0, 6.0, 0.0, -0.5, -1.0, -1.5, -2.0, -3.0, -4.0, -6.0], dtype=jnp.float32)

        def dequant_nvfp4(W_packed, scales, block=BLOCK_SIZE):
            N = W_packed.shape[0]
            low = W_packed & 15
            high = W_packed >> 4 & 15
            idx = jnp.stack([low, high], axis=-1).reshape(N, -1)
            vals = NVFP4_LUT[idx]
            K = vals.shape[1]
            vals = vals.reshape(N, K // block, block) * scales[:, :, None]
            return vals.reshape(N, K)
        key = jax.random.key(seed)
        ks = jax.random.split(key, 7)
        x = jax.random.normal(ks[0], (4, 32, HIDDEN_SIZE), dtype=jnp.float32)
        gate_W_packed = jax.random.randint(ks[1], (MLP_DIM, HIDDEN_SIZE // 2), 0, 32, dtype=jnp.int32)
        gate_scales = jax.random.uniform(ks[2], (MLP_DIM, HIDDEN_SIZE // BLOCK_SIZE), dtype=jnp.float32) * 0.1 + 0.001
        up_W_packed = jax.random.randint(ks[3], (MLP_DIM, HIDDEN_SIZE // 2), 0, 32, dtype=jnp.int32)
        up_scales = jax.random.uniform(ks[4], (MLP_DIM, HIDDEN_SIZE // BLOCK_SIZE), dtype=jnp.float32) * 0.1 + 0.001
        down_W_packed = jax.random.randint(ks[5], (HIDDEN_SIZE, MLP_DIM // 2), 0, 32, dtype=jnp.int32)
        down_scales = jax.random.uniform(ks[6], (HIDDEN_SIZE, MLP_DIM // BLOCK_SIZE), dtype=jnp.float32) * 0.1 + 0.001
        return {'x': x, 'gate_W_packed': gate_W_packed, 'gate_scales': gate_scales, 'up_W_packed': up_W_packed, 'up_scales': up_scales, 'down_W_packed': down_W_packed, 'down_scales': down_scales}
    _L0_ffn_all = _L0_ffn_setup()
    _L0_ffn_in = {k: v for k, v in _L0_ffn_all.items() if k in ('gate_W_packed', 'gate_scales', 'up_W_packed', 'up_scales', 'down_W_packed', 'down_scales')}
    del _L0_ffn_all

    def _L1_xattn_setup():
        import jax, jax.numpy as jnp
        import numpy as np
        B, S1, S2, DCA = (2, 256, 128, 16)
        QDIM, KDIM, H = (256, 128, 16)
        HD = QDIM // H
        SCALE = HD ** (-0.5)
        EPS = 1e-06
        DCA_WEIGHT = 1.0

        def _ln(t, w, b):
            m = jnp.mean(t, axis=-1, keepdims=True)
            v = jnp.var(t, axis=-1, keepdims=True)
            return (t - m) * jax.lax.rsqrt(v + EPS) * w + b

        def _attn(q, k, v):
            s = jnp.einsum('bhqd,bhkd->bhqk', q, k) * SCALE
            p = jax.nn.softmax(s, axis=-1)
            return jnp.einsum('bhqk,bhkd->bhqd', p, v)
        key = jax.random.key(seed)
        ks = jax.random.split(key, 8)
        w = lambda k, shape: jax.random.normal(k, shape, jnp.float32) * 0.02
        return {'x': jax.random.normal(ks[0], (B, S1, QDIM), jnp.float32), 'y': jax.random.normal(ks[1], (B, S2 + DCA, KDIM), jnp.float32), 'Wq': w(ks[2], (QDIM, QDIM)), 'bq': jnp.zeros((QDIM,), jnp.float32), 'Wk': w(ks[3], (KDIM, QDIM)), 'bk': jnp.zeros((QDIM,), jnp.float32), 'Wv': w(ks[4], (KDIM, QDIM)), 'bv': jnp.zeros((QDIM,), jnp.float32), 'Wkv_dca': w(ks[5], (KDIM, 2 * QDIM)), 'bkv_dca': jnp.zeros((2 * QDIM,), jnp.float32), 'qn_w': jnp.ones((HD,), jnp.float32), 'qn_b': jnp.zeros((HD,), jnp.float32), 'kn_w': jnp.ones((HD,), jnp.float32), 'kn_b': jnp.zeros((HD,), jnp.float32), 'kn_dca_w': jnp.ones((HD,), jnp.float32), 'kn_dca_b': jnp.zeros((HD,), jnp.float32), 'Wo': w(ks[6], (QDIM, QDIM)), 'bo': jnp.zeros((QDIM,), jnp.float32)}
    _L1_xattn_all = _L1_xattn_setup()
    _L1_xattn_in = {k: v for k, v in _L1_xattn_all.items() if k in ('Wq', 'bq', 'Wk', 'bk', 'Wv', 'bv', 'Wkv_dca', 'bkv_dca', 'qn_w', 'qn_b', 'kn_w', 'kn_b', 'kn_dca_w', 'kn_dca_b', 'Wo', 'bo')}
    del _L1_xattn_all

    def _L1_ffn_setup():
        import jax, jax.numpy as jnp
        import numpy as np
        FP8 = jnp.float8_e4m3fn
        key = jax.random.key(seed)
        k1, k2 = jax.random.split(key)
        input1 = jax.random.normal(k1, (2, 512, 256), dtype=jnp.float32)
        input2 = jax.random.normal(k2, (256, 256), dtype=jnp.float32)
        scale = jnp.array(0.5, dtype=jnp.float32)
        scale1 = jnp.array(0.5, dtype=jnp.float32)
        return {'input1': input1, 'input2': input2, 'scale': scale, 'scale1': scale1}
    _L1_ffn_all = _L1_ffn_setup()
    _L1_ffn_in = {k: v for k, v in _L1_ffn_all.items() if k in ('input2', 'scale', 'scale1')}
    del _L1_ffn_all

    def _L2_xattn_setup():
        import jax, jax.numpy as jnp
        import numpy as np
        N_HEADS = 16
        N_KV_HEADS = 8
        HEAD_DIM = 128
        D_TEXT = 256
        D_VISION = 128
        GROUPS = N_HEADS // N_KV_HEADS
        key = jax.random.key(seed)
        ks = jax.random.split(key, 6)
        B, T_text, T_vis = (4, 256, 72)
        text_hidden = jax.random.normal(ks[0], (B, T_text, D_TEXT), dtype=jnp.float32)
        vision_tokens = jax.random.normal(ks[1], (B, T_vis, D_VISION), dtype=jnp.float32)
        vision_mask = jnp.ones((B, T_vis), dtype=bool)
        s = 0.02
        Wq = jax.random.normal(ks[2], (D_TEXT, N_HEADS * HEAD_DIM), dtype=jnp.float32) * s
        Wk = jax.random.normal(ks[3], (D_VISION, N_KV_HEADS * HEAD_DIM), dtype=jnp.float32) * s
        Wv = jax.random.normal(ks[4], (D_VISION, N_KV_HEADS * HEAD_DIM), dtype=jnp.float32) * s
        Wo = jax.random.normal(ks[5], (N_HEADS * HEAD_DIM, D_TEXT), dtype=jnp.float32) * s
        return {'text_hidden': text_hidden, 'vision_tokens': vision_tokens, 'vision_mask': vision_mask, 'Wq': Wq, 'Wk': Wk, 'Wv': Wv, 'Wo': Wo}
    _L2_xattn_all = _L2_xattn_setup()
    _L2_xattn_in = {k: v for k, v in _L2_xattn_all.items() if k in ('Wq', 'Wk', 'Wv', 'Wo')}
    del _L2_xattn_all

    def _L2_ffn_setup():
        import jax, jax.numpy as jnp
        import numpy as np
        DIM = 256
        HID = 704
        ZERO_POINT = 128.0

        def _qlinear(x, wq, scale):
            W = (wq.astype(jnp.float32) - ZERO_POINT) * scale[:, None]
            return jnp.einsum('bsd,hd->bsh', x, W)
        key = jax.random.key(seed)
        ks = jax.random.split(key, 7)
        B, S = (4, 256)
        sg = jax.random.uniform(ks[1], (HID,)) * (0.02 / np.sqrt(DIM)) + 0.0001
        su = jax.random.uniform(ks[3], (HID,)) * (0.02 / np.sqrt(DIM)) + 0.0001
        sd = jax.random.uniform(ks[5], (DIM,)) * (0.02 / np.sqrt(HID)) + 0.0001
        return {'x': jax.random.normal(ks[0], (B, S, DIM), dtype=jnp.float32), 'wq_gate': jax.random.randint(ks[2], (HID, DIM), 0, 32, dtype=jnp.int32), 's_gate': sg, 'wq_up': jax.random.randint(ks[4], (HID, DIM), 0, 32, dtype=jnp.int32), 's_up': su, 'wq_down': jax.random.randint(ks[6], (DIM, HID), 0, 32, dtype=jnp.int32), 's_down': sd}
    _L2_ffn_all = _L2_ffn_setup()
    _L2_ffn_in = {k: v for k, v in _L2_ffn_all.items() if k in ('wq_gate', 's_gate', 'wq_up', 's_up', 'wq_down', 's_down')}
    del _L2_ffn_all

    def _L3_xattn_setup():
        import jax, jax.numpy as jnp
        import numpy as np
        DIM = 256
        CTX_DIM = 128
        N_HEADS = 32
        HEAD_DIM = DIM // N_HEADS
        POS_DIM = 2
        B, N, CTXN = (2, 256, 256)
        ROPE_BASE = 10000.0

        def apply_axial_rope(x, pos):
            b, n, h, d = x.shape
            p = pos.shape[-1]
            dpa = d // p
            half = dpa // 2
            freqs = ROPE_BASE ** (-jnp.arange(half, dtype=x.dtype) / half)
            ang = pos[..., :, None] * freqs
            cos = jnp.cos(ang)[:, :, None, :, :]
            sin = jnp.sin(ang)[:, :, None, :, :]
            xr = x.reshape(b, n, h, p, half, 2)
            x1, x2 = (xr[..., 0], xr[..., 1])
            out = jnp.stack([x1 * cos - x2 * sin, x1 * sin + x2 * cos], axis=-1)
            return out.reshape(b, n, h, d)
        key = jax.random.key(seed)
        ks = jax.random.split(key, 8)
        x = jax.random.normal(ks[0], (B, N, DIM), jnp.float32)
        ctx = jax.random.normal(ks[1], (B, CTXN, CTX_DIM), jnp.float32)
        pos_map = jax.random.uniform(ks[2], (B, N, POS_DIM), jnp.float32)
        ctx_pos_map = jax.random.uniform(ks[3], (B, CTXN, POS_DIM), jnp.float32)
        Wq = jax.random.normal(ks[4], (DIM, DIM), jnp.float32) / np.sqrt(DIM)
        Wkv = jax.random.normal(ks[5], (CTX_DIM, 2 * DIM), jnp.float32) / np.sqrt(CTX_DIM)
        Wout = jax.random.normal(ks[6], (DIM, DIM), jnp.float32) / np.sqrt(DIM)
        bout = jnp.zeros((DIM,), jnp.float32)
        return {'x': x, 'ctx': ctx, 'pos_map': pos_map, 'ctx_pos_map': ctx_pos_map, 'Wq': Wq, 'Wkv': Wkv, 'Wout': Wout, 'bout': bout}
    _L3_xattn_all = _L3_xattn_setup()
    _L3_xattn_in = {k: v for k, v in _L3_xattn_all.items() if k in ('Wq', 'Wkv', 'Wout', 'bout')}
    del _L3_xattn_all

    def _L3_ffn_setup():
        import jax, jax.numpy as jnp
        import numpy as np
        B, T, D, H = (4, 256, 256, 176)
        E, K = (16, 2)
        G, TKG, S = (4, 2, 1)
        SCALE = 1.0

        def _moe(x, gate_w, w1, w2, sw1, sw2):
            Bx, Tx, Dx = x.shape
            xf = x.reshape(-1, Dx)
            N = xf.shape[0]
            shared = jnp.zeros_like(xf)
            for s in range(S):
                shared = shared + jax.nn.silu(xf @ sw1[s]) @ sw2[s]
            scores = jax.nn.sigmoid(xf @ gate_w.T)
            gs = E // G
            sg = scores.reshape(N, G, gs)
            group_scores = jax.lax.top_k(sg, min(2, gs))[0].sum(axis=-1)
            _, gidx = jax.lax.top_k(group_scores, TKG)
            gmask = jax.nn.one_hot(gidx, G, dtype=scores.dtype).max(axis=1)
            masked = (sg * gmask[:, :, None]).reshape(N, E)
            tw, ti = jax.lax.top_k(masked, K)
            tw = tw / (tw.sum(axis=-1, keepdims=True) + 1e-20) * SCALE
            combine = jnp.zeros((N, E), scores.dtype).at[jnp.arange(N)[:, None], ti].add(tw)
            out = shared
            for e in range(E):
                out = out + combine[:, e:e + 1] * (jax.nn.silu(xf @ w1[e]) @ w2[e])
            return out.reshape(Bx, Tx, Dx)
        key = jax.random.key(seed)
        ks = jax.random.split(key, 6)
        x = jax.random.normal(ks[0], (B, T, D), jnp.float32)
        gate_w = jax.random.normal(ks[1], (E, D), jnp.float32) * 0.02
        w1 = jax.random.normal(ks[2], (E, D, H), jnp.float32) * 0.02
        w2 = jax.random.normal(ks[3], (E, H, D), jnp.float32) * 0.02
        sw1 = jax.random.normal(ks[4], (S, D, H), jnp.float32) * 0.02
        sw2 = jax.random.normal(ks[5], (S, H, D), jnp.float32) * 0.02
        return {'x': x, 'gate_w': gate_w, 'w1': w1, 'w2': w2, 'sw1': sw1, 'sw2': sw2}
    _L3_ffn_all = _L3_ffn_setup()
    _L3_ffn_in = {k: v for k, v in _L3_ffn_all.items() if k in ('gate_w', 'w1', 'w2', 'sw1', 'sw2')}
    del _L3_ffn_all
    return {'x': x, 'ctx_1024': ctx_1024, 'fside_BxSx2_0': fside_BxSx2_0, 'mask_BxS2_bf1': mask_BxS2_bf1, 'g_xattn': g_xattn, 'g_ffn': g_ffn, 'L0_xattn_Wq': _L0_xattn_in['Wq'], 'L0_xattn_Wk': _L0_xattn_in['Wk'], 'L0_xattn_Wv': _L0_xattn_in['Wv'], 'L0_xattn_Wo': _L0_xattn_in['Wo'], 'L0_xattn_gq': _L0_xattn_in['gq'], 'L0_xattn_gk': _L0_xattn_in['gk'], 'L0_ffn_gate_W_packed': _L0_ffn_in['gate_W_packed'], 'L0_ffn_gate_scales': _L0_ffn_in['gate_scales'], 'L0_ffn_up_W_packed': _L0_ffn_in['up_W_packed'], 'L0_ffn_up_scales': _L0_ffn_in['up_scales'], 'L0_ffn_down_W_packed': _L0_ffn_in['down_W_packed'], 'L0_ffn_down_scales': _L0_ffn_in['down_scales'], 'L1_xattn_Wq': _L1_xattn_in['Wq'], 'L1_xattn_bq': _L1_xattn_in['bq'], 'L1_xattn_Wk': _L1_xattn_in['Wk'], 'L1_xattn_bk': _L1_xattn_in['bk'], 'L1_xattn_Wv': _L1_xattn_in['Wv'], 'L1_xattn_bv': _L1_xattn_in['bv'], 'L1_xattn_Wkv_dca': _L1_xattn_in['Wkv_dca'], 'L1_xattn_bkv_dca': _L1_xattn_in['bkv_dca'], 'L1_xattn_qn_w': _L1_xattn_in['qn_w'], 'L1_xattn_qn_b': _L1_xattn_in['qn_b'], 'L1_xattn_kn_w': _L1_xattn_in['kn_w'], 'L1_xattn_kn_b': _L1_xattn_in['kn_b'], 'L1_xattn_kn_dca_w': _L1_xattn_in['kn_dca_w'], 'L1_xattn_kn_dca_b': _L1_xattn_in['kn_dca_b'], 'L1_xattn_Wo': _L1_xattn_in['Wo'], 'L1_xattn_bo': _L1_xattn_in['bo'], 'L1_ffn_input2': _L1_ffn_in['input2'], 'L1_ffn_scale': _L1_ffn_in['scale'], 'L1_ffn_scale1': _L1_ffn_in['scale1'], 'L2_xattn_Wq': _L2_xattn_in['Wq'], 'L2_xattn_Wk': _L2_xattn_in['Wk'], 'L2_xattn_Wv': _L2_xattn_in['Wv'], 'L2_xattn_Wo': _L2_xattn_in['Wo'], 'L2_ffn_wq_gate': _L2_ffn_in['wq_gate'], 'L2_ffn_s_gate': _L2_ffn_in['s_gate'], 'L2_ffn_wq_up': _L2_ffn_in['wq_up'], 'L2_ffn_s_up': _L2_ffn_in['s_up'], 'L2_ffn_wq_down': _L2_ffn_in['wq_down'], 'L2_ffn_s_down': _L2_ffn_in['s_down'], 'L3_xattn_Wq': _L3_xattn_in['Wq'], 'L3_xattn_Wkv': _L3_xattn_in['Wkv'], 'L3_xattn_Wout': _L3_xattn_in['Wout'], 'L3_xattn_bout': _L3_xattn_in['bout'], 'L3_ffn_gate_w': _L3_ffn_in['gate_w'], 'L3_ffn_w1': _L3_ffn_in['w1'], 'L3_ffn_w2': _L3_ffn_in['w2'], 'L3_ffn_sw1': _L3_ffn_in['sw1'], 'L3_ffn_sw2': _L3_ffn_in['sw2']}

def reference(x, ctx_1024, fside_BxSx2_0, mask_BxS2_bf1, g_xattn, g_ffn, L0_xattn_Wq, L0_xattn_Wk, L0_xattn_Wv, L0_xattn_Wo, L0_xattn_gq, L0_xattn_gk, L0_ffn_gate_W_packed, L0_ffn_gate_scales, L0_ffn_up_W_packed, L0_ffn_up_scales, L0_ffn_down_W_packed, L0_ffn_down_scales, L1_xattn_Wq, L1_xattn_bq, L1_xattn_Wk, L1_xattn_bk, L1_xattn_Wv, L1_xattn_bv, L1_xattn_Wkv_dca, L1_xattn_bkv_dca, L1_xattn_qn_w, L1_xattn_qn_b, L1_xattn_kn_w, L1_xattn_kn_b, L1_xattn_kn_dca_w, L1_xattn_kn_dca_b, L1_xattn_Wo, L1_xattn_bo, L1_ffn_input2, L1_ffn_scale, L1_ffn_scale1, L2_xattn_Wq, L2_xattn_Wk, L2_xattn_Wv, L2_xattn_Wo, L2_ffn_wq_gate, L2_ffn_s_gate, L2_ffn_wq_up, L2_ffn_s_up, L2_ffn_wq_down, L2_ffn_s_down, L3_xattn_Wq, L3_xattn_Wkv, L3_xattn_Wout, L3_xattn_bout, L3_ffn_gate_w, L3_ffn_w1, L3_ffn_w2, L3_ffn_sw1, L3_ffn_sw2):
    import jax
    import jax.numpy as jnp

    def _L0_xattn_ref(hidden_states, encoder_hidden_states, Wq, Wk, Wv, Wo, gq, gk):
        import jax, jax.numpy as jnp
        import numpy as np
        EPS = 1e-05

        def rmsnorm(x, g, eps=EPS):
            var = jnp.mean(jnp.square(x), axis=-1, keepdims=True)
            return x * jax.lax.rsqrt(var + eps) * g
        B, Sq, _ = hidden_states.shape
        Skv = encoder_hidden_states.shape[1]
        D = gq.shape[0]
        H = Wq.shape[1] // D
        scale = 1.0 / np.sqrt(D)
        q = (hidden_states @ Wq).reshape(B, Sq, H, D)
        k = (encoder_hidden_states @ Wk).reshape(B, Skv, H, D)
        v = (encoder_hidden_states @ Wv).reshape(B, Skv, H, D)
        q = rmsnorm(q, gq)
        k = rmsnorm(k, gk)
        scores = jnp.einsum('bqhd,bkhd->bhqk', q, k) * scale
        attn = jax.nn.softmax(scores, axis=-1)
        out = jnp.einsum('bhqk,bkhd->bqhd', attn, v)
        out = out.reshape(B, Sq, H * D)
        return out @ Wo

    def _L0_ffn_ref(x, gate_W_packed, gate_scales, up_W_packed, up_scales, down_W_packed, down_scales):
        import jax, jax.numpy as jnp
        import numpy as np
        BLOCK_SIZE = 32
        HIDDEN_SIZE = 256
        MLP_DIM = 2048
        NVFP4_LUT = jnp.array([0.0, 0.5, 1.0, 1.5, 2.0, 3.0, 4.0, 6.0, 0.0, -0.5, -1.0, -1.5, -2.0, -3.0, -4.0, -6.0], dtype=jnp.float32)

        def dequant_nvfp4(W_packed, scales, block=BLOCK_SIZE):
            N = W_packed.shape[0]
            low = W_packed & 15
            high = W_packed >> 4 & 15
            idx = jnp.stack([low, high], axis=-1).reshape(N, -1)
            vals = NVFP4_LUT[idx]
            K = vals.shape[1]
            vals = vals.reshape(N, K // block, block) * scales[:, :, None]
            return vals.reshape(N, K)
        B, S, H = x.shape
        xt = x.reshape(B * S, H)
        Wg = dequant_nvfp4(gate_W_packed, gate_scales)
        Wu = dequant_nvfp4(up_W_packed, up_scales)
        Wd = dequant_nvfp4(down_W_packed, down_scales)
        gate = jnp.einsum('th,nh->tn', xt, Wg)
        up = jnp.einsum('th,nh->tn', xt, Wu)
        gelu = jnp.tanh(0.7978845608028654 * (gate + 0.044715 * gate ** 3)) * gate * 0.5 + gate * 0.5
        inter = gelu * up
        out = jnp.einsum('tn,hn->th', inter, Wd)
        return out.reshape(B, S, H)

    def _L1_xattn_ref(x, y, Wq, bq, Wk, bk, Wv, bv, Wkv_dca, bkv_dca, qn_w, qn_b, kn_w, kn_b, kn_dca_w, kn_dca_b, Wo, bo):
        import jax, jax.numpy as jnp
        import numpy as np
        B, S1, S2, DCA = (2, 256, 128, 16)
        QDIM, KDIM, H = (256, 128, 16)
        HD = QDIM // H
        SCALE = HD ** (-0.5)
        EPS = 1e-06
        DCA_WEIGHT = 1.0

        def _ln(t, w, b):
            m = jnp.mean(t, axis=-1, keepdims=True)
            v = jnp.var(t, axis=-1, keepdims=True)
            return (t - m) * jax.lax.rsqrt(v + EPS) * w + b

        def _attn(q, k, v):
            s = jnp.einsum('bhqd,bhkd->bhqk', q, k) * SCALE
            p = jax.nn.softmax(s, axis=-1)
            return jnp.einsum('bhqk,bhkd->bhqd', p, v)
        b, s1, _ = x.shape
        y_dca = y[:, -DCA:, :]
        y_main = y[:, :-DCA, :]
        kv_dca = (y_dca @ Wkv_dca + bkv_dca).reshape(b, DCA, 2, H, HD)
        k_dca = _ln(kv_dca[:, :, 0], kn_dca_w, kn_dca_b)
        v_dca = kv_dca[:, :, 1]
        s2 = y_main.shape[1]
        q = _ln((x @ Wq + bq).reshape(b, s1, H, HD), qn_w, qn_b)
        kv = jnp.concatenate([y_main @ Wk + bk, y_main @ Wv + bv], axis=-1)
        kv = kv.reshape(b, s2, H, 2 * HD)
        k = _ln(kv[..., :HD], kn_w, kn_b)
        v = kv[..., HD:]
        qT = q.transpose(0, 2, 1, 3)
        ctx = _attn(qT, k.transpose(0, 2, 1, 3), v.transpose(0, 2, 1, 3))
        ctx = ctx.transpose(0, 2, 1, 3).reshape(b, s1, QDIM)
        ctx_dca = _attn(qT, k_dca.transpose(0, 2, 1, 3), v_dca.transpose(0, 2, 1, 3))
        ctx_dca = ctx_dca.transpose(0, 2, 1, 3).reshape(b, s1, QDIM)
        ctx = ctx + DCA_WEIGHT * ctx_dca
        return ctx @ Wo + bo

    def _L1_ffn_ref(input1, input2, scale, scale1):
        import jax, jax.numpy as jnp
        import numpy as np
        FP8 = jnp.float8_e4m3fn
        q1 = (input1 * scale).astype(FP8)
        q2 = (input2 * scale1).astype(FP8)
        d1 = q1.astype(jnp.float32) * (1.0 / scale)
        d2 = q2.astype(jnp.float32) * (1.0 / scale1)
        return jnp.einsum('bmk,kn->bmn', d1, d2)

    def _L2_xattn_ref(text_hidden, vision_tokens, vision_mask, Wq, Wk, Wv, Wo):
        import jax, jax.numpy as jnp
        import numpy as np
        N_HEADS = 16
        N_KV_HEADS = 8
        HEAD_DIM = 128
        D_TEXT = 256
        D_VISION = 128
        GROUPS = N_HEADS // N_KV_HEADS
        B, T_text, _ = text_hidden.shape
        T_vis = vision_tokens.shape[1]
        scale = jnp.float32(np.sqrt(HEAD_DIM))
        q = (text_hidden @ Wq).reshape(B, T_text, N_HEADS, HEAD_DIM).transpose(0, 2, 1, 3)
        k = (vision_tokens @ Wk).reshape(B, T_vis, N_KV_HEADS, HEAD_DIM).transpose(0, 2, 1, 3)
        v = (vision_tokens @ Wv).reshape(B, T_vis, N_KV_HEADS, HEAD_DIM).transpose(0, 2, 1, 3)
        k = jnp.repeat(k, GROUPS, axis=1)
        v = jnp.repeat(v, GROUPS, axis=1)
        scores = jnp.einsum('bhtd,bhsd->bhts', q, k) / scale
        mask = vision_mask[:, None, None, :]
        scores = jnp.where(mask, scores, -jnp.inf)
        attn = jax.nn.softmax(scores, axis=-1)
        attn = jnp.nan_to_num(attn, nan=0.0)
        out = jnp.einsum('bhts,bhsd->bhtd', attn, v)
        out = out.transpose(0, 2, 1, 3).reshape(B, T_text, N_HEADS * HEAD_DIM)
        return out @ Wo

    def _L2_ffn_ref(x, wq_gate, s_gate, wq_up, s_up, wq_down, s_down):
        import jax, jax.numpy as jnp
        import numpy as np
        DIM = 256
        HID = 704
        ZERO_POINT = 128.0

        def _qlinear(x, wq, scale):
            W = (wq.astype(jnp.float32) - ZERO_POINT) * scale[:, None]
            return jnp.einsum('bsd,hd->bsh', x, W)
        gate = _qlinear(x, wq_gate, s_gate)
        gate = jax.nn.silu(gate)
        up = _qlinear(x, wq_up, s_up)
        return _qlinear(gate * up, wq_down, s_down)

    def _L3_xattn_ref(x, ctx, pos_map, ctx_pos_map, Wq, Wkv, Wout, bout):
        import jax, jax.numpy as jnp
        import numpy as np
        DIM = 256
        CTX_DIM = 128
        N_HEADS = 32
        HEAD_DIM = DIM // N_HEADS
        POS_DIM = 2
        B, N, CTXN = (2, 256, 256)
        ROPE_BASE = 10000.0

        def apply_axial_rope(x, pos):
            b, n, h, d = x.shape
            p = pos.shape[-1]
            dpa = d // p
            half = dpa // 2
            freqs = ROPE_BASE ** (-jnp.arange(half, dtype=x.dtype) / half)
            ang = pos[..., :, None] * freqs
            cos = jnp.cos(ang)[:, :, None, :, :]
            sin = jnp.sin(ang)[:, :, None, :, :]
            xr = x.reshape(b, n, h, p, half, 2)
            x1, x2 = (xr[..., 0], xr[..., 1])
            out = jnp.stack([x1 * cos - x2 * sin, x1 * sin + x2 * cos], axis=-1)
            return out.reshape(b, n, h, d)
        b, n, _ = x.shape
        ctx_n = ctx.shape[1]
        q = (x @ Wq).reshape(b, n, N_HEADS, HEAD_DIM)
        k, v = jnp.split(ctx @ Wkv, 2, axis=-1)
        k = k.reshape(b, ctx_n, N_HEADS, HEAD_DIM)
        v = v.reshape(b, ctx_n, N_HEADS, HEAD_DIM)
        q = apply_axial_rope(q, pos_map)
        k = apply_axial_rope(k, ctx_pos_map)
        scale = 1.0 / np.sqrt(HEAD_DIM).astype(np.float32)
        logits = jnp.einsum('bqhd,bkhd->bhqk', q, k) * scale
        w = jax.nn.softmax(logits, axis=-1)
        attn = jnp.einsum('bhqk,bkhd->bqhd', w, v)
        attn = attn.reshape(b, n, N_HEADS * HEAD_DIM)
        return attn @ Wout + bout

    def _L3_ffn_ref(x, gate_w, w1, w2, sw1, sw2):
        import jax, jax.numpy as jnp
        import numpy as np
        B, T, D, H = (4, 256, 256, 176)
        E, K = (16, 2)
        G, TKG, S = (4, 2, 1)
        SCALE = 1.0

        def _moe(x, gate_w, w1, w2, sw1, sw2):
            Bx, Tx, Dx = x.shape
            xf = x.reshape(-1, Dx)
            N = xf.shape[0]
            shared = jnp.zeros_like(xf)
            for s in range(S):
                shared = shared + jax.nn.silu(xf @ sw1[s]) @ sw2[s]
            scores = jax.nn.sigmoid(xf @ gate_w.T)
            gs = E // G
            sg = scores.reshape(N, G, gs)
            group_scores = jax.lax.top_k(sg, min(2, gs))[0].sum(axis=-1)
            _, gidx = jax.lax.top_k(group_scores, TKG)
            gmask = jax.nn.one_hot(gidx, G, dtype=scores.dtype).max(axis=1)
            masked = (sg * gmask[:, :, None]).reshape(N, E)
            tw, ti = jax.lax.top_k(masked, K)
            tw = tw / (tw.sum(axis=-1, keepdims=True) + 1e-20) * SCALE
            combine = jnp.zeros((N, E), scores.dtype).at[jnp.arange(N)[:, None], ti].add(tw)
            out = shared
            for e in range(E):
                out = out + combine[:, e:e + 1] * (jax.nn.silu(xf @ w1[e]) @ w2[e])
            return out.reshape(Bx, Tx, Dx)
        return _moe(x, gate_w, w1, w2, sw1, sw2)
    x = x + jnp.tanh(g_xattn[0]) * _L0_xattn_ref(_layernorm(x, axis=-1), ctx_1024, L0_xattn_Wq, L0_xattn_Wk, L0_xattn_Wv, L0_xattn_Wo, L0_xattn_gq, L0_xattn_gk)
    x = x + jnp.tanh(g_ffn[0]) * _L0_ffn_ref(_layernorm(x, axis=-1), L0_ffn_gate_W_packed, L0_ffn_gate_scales, L0_ffn_up_W_packed, L0_ffn_up_scales, L0_ffn_down_W_packed, L0_ffn_down_scales)
    x = x + jnp.tanh(g_xattn[1]) * _L1_xattn_ref(_layernorm(x, axis=-1), ctx_1024, L1_xattn_Wq, L1_xattn_bq, L1_xattn_Wk, L1_xattn_bk, L1_xattn_Wv, L1_xattn_bv, L1_xattn_Wkv_dca, L1_xattn_bkv_dca, L1_xattn_qn_w, L1_xattn_qn_b, L1_xattn_kn_w, L1_xattn_kn_b, L1_xattn_kn_dca_w, L1_xattn_kn_dca_b, L1_xattn_Wo, L1_xattn_bo)
    x = x + jnp.tanh(g_ffn[1]) * _L1_ffn_ref(_layernorm(x, axis=-1), L1_ffn_input2, L1_ffn_scale, L1_ffn_scale1)
    x = x + jnp.tanh(g_xattn[2]) * _L2_xattn_ref(_layernorm(x, axis=-1), ctx_1024, mask_BxS2_bf1, L2_xattn_Wq, L2_xattn_Wk, L2_xattn_Wv, L2_xattn_Wo)
    x = x + jnp.tanh(g_ffn[2]) * _L2_ffn_ref(_layernorm(x, axis=-1), L2_ffn_wq_gate, L2_ffn_s_gate, L2_ffn_wq_up, L2_ffn_s_up, L2_ffn_wq_down, L2_ffn_s_down)
    x = x + jnp.tanh(g_xattn[3]) * _L3_xattn_ref(_layernorm(x, axis=-1), ctx_1024, fside_BxSx2_0, fside_BxSx2_0, L3_xattn_Wq, L3_xattn_Wkv, L3_xattn_Wout, L3_xattn_bout)
    x = x + jnp.tanh(g_ffn[3]) * _L3_ffn_ref(_layernorm(x, axis=-1), L3_ffn_gate_w, L3_ffn_w1, L3_ffn_w2, L3_ffn_sw1, L3_ffn_sw2)
    return x

_drawn_inputs = setup_inputs


def setup_inputs(seed=0):
    import zlib

    import numpy as np

    out = dict(_drawn_inputs(seed))
    spreads = {'L0_xattn_gq': (1.0, 0.2),
     'L0_xattn_gk': (1.0, 0.2),
     'L1_xattn_bq': (0.0, 0.8),
     'L1_xattn_bk': (0.0, 0.8),
     'L1_xattn_bv': (0.0, 0.8),
     'L1_xattn_bkv_dca': (0.0, 0.768),
     'L1_xattn_qn_w': (1.0, 0.6),
     'L1_xattn_qn_b': (0.0, 0.8),
     'L1_xattn_kn_w': (1.0, 0.6),
     'L1_xattn_kn_b': (0.0, 0.8),
     'L1_xattn_kn_dca_w': (1.0, 0.6),
     'L1_xattn_kn_dca_b': (0.0, 0.8),
     'L1_xattn_bo': (0.0, 0.444),
     'L3_xattn_bout': (0.0, 0.8)}
    factors = {'fside_BxSx2_0': 8.0,
     'L1_xattn_Wq': 7.979,
     'L1_xattn_Wk': 7.315,
     'L1_xattn_Wv': 7.428,
     'L1_xattn_Wkv_dca': 5.663,
     'L1_xattn_Wo': 4.284,
     'L2_xattn_Wq': 8.0,
     'L2_xattn_Wk': 8.0,
     'L2_xattn_Wv': 8.0,
     'L2_xattn_Wo': 8.0,
     'L2_ffn_s_gate': 8.0,
     'L2_ffn_s_up': 8.0,
     'L2_ffn_s_down': 8.0,
     'L3_xattn_Wq': 6.397,
     'L3_ffn_gate_w': 8.0,
     'L3_ffn_w1': 8.0,
     'L3_ffn_w2': 8.0,
     'L3_ffn_sw1': 8.0,
     'L3_ffn_sw2': 8.0}
    for name, (base, spread) in spreads.items():
        noise = np.random.default_rng([zlib.crc32(name.encode()), seed]).standard_normal(out[name].shape)
        drawn = base * np.exp(spread * noise) if base else spread * noise
        out[name] = jnp.asarray(drawn.astype(out[name].dtype))
    for name, factor in factors.items():
        out[name] = (out[name] * factor).astype(out[name].dtype)
    return out
```

```python
from contextlib import ExitStack

import concourse.bass as bass
from concourse import mybir

F32 = mybir.dt.float32
BF16 = mybir.dt.bfloat16
I32 = mybir.dt.int32
U32 = mybir.dt.uint32
U8 = mybir.dt.uint8
ALU = mybir.AluOpType
ACT = mybir.ActivationFunctionType
AX = mybir.AxisListType.X

P = 128
B = 8
CB = 4
CT = CB * P
D = 256
STAGES = 16
WIDE, FFN, NARROW, FP8 = "wide", "ffn", "narrow", "fp8"
KIND = [WIDE, FFN, NARROW, FP8, WIDE, FFN, NARROW, FFN]
HEADS = 16
MOE_H = 176
EXPERTS = 16
MOE_ALL = (EXPERTS + 1) * MOE_H
HID2 = 704
NEG = 1e30
FP4_TABLE = 0xC8643210
RSQRT_SEED = float(0x5F3759DF)


def tile_sizes(total):
    return [min(P, total - i) for i in range(0, total, P)]


TILES = {1: tile_sizes(2048), 5: tile_sizes(HID2), 7: tile_sizes(MOE_ALL)}
FFN_BASE, _n = {}, 0
for _s in range(STAGES):
    FFN_BASE[_s] = _n
    if _s // 2 in TILES:
        _n += len(TILES[_s // 2])


class Narrow:

    def __init__(self, s):
        self.s = s
        self.hd = 16 if s == 2 else 8
        self.heads = P // self.hd
        self.keys = 112 if s == 2 else 128
        self.scale = float(self.hd) ** -0.5
        self.groups = self.heads // 4
        order = [(f, g) for f in range(2) for g in range(self.groups)]
        self.order = order + [("dca", 0)] * (s == 2)
        self.n = len(self.order)
        self.batch_base = 0 if s == 2 else B
        self.group_base = 0 if s == 2 else 5 * B
        self.dcas_before = 0 if s == 2 else B

    def steps(self, chunk):
        for t in range(CB):
            for k, (f, g) in enumerate(self.order):
                yield t, f, g, k, self.group_base + (CB * chunk + t) * self.n + k


def build(nc, dram, out):
    with ExitStack() as ctx:
        def sb(name, shape, dt=F32):
            return ctx.enter_context(nc.sbuf_tensor(name, shape, dt))

        sems = {}

        def sem(name):
            sems[name] = ctx.enter_context(nc.semaphore(name))
            return sems[name]

        bank = [ctx.enter_context(nc.psum_tensor(f"bank{i}", [P, 512], F32)) for i in range(8)]

        consts = sb("consts", [P, 552])
        ident = consts[:, 0:128]
        head_mask = {6: consts[:, 128:144], 2: consts[:, 144:152]}
        dca_mask = consts[:, 152:280]
        tie16 = consts[:, 280:536].rearrange("p (e j) -> p e j", e=16)
        tie4 = consts[:, 536:552].rearrange("p (e j) -> p e j", e=4)
        ones = sb("ones", [P, P])
        fp4_table = sb("fp4_table", [P, 1], U32)
        x_sb = sb("x_sb", [P, B, D])
        xn = sb("xn", [P, 2, CB, D])
        xT = sb("xT", [P, 2, 2, CT])
        xqT = sb("xqT", [P, 2, CT], BF16)
        w8 = sb("w8", [P, 2, D], BF16)
        ctx_tok = sb("ctx_tok", [P, B, P])
        ctxT = sb("ctxT", [P, B, P])
        mask8 = sb("mask8", [P, B * P], U8)
        gates = sb("gates", [P, 8])
        tg = sb("tg", [P, 8])
        scales8 = sb("scales8", [P, 4])
        gqk = sb("gqk", [P, 3])
        fside = sb("fside", [P, B, 2])
        trig = sb("trig", [P, 6, B * 4])
        cosx = sb("cosx", [P, B, 4, 2])
        sinx = sb("sinx", [P, B, 4, 2])
        ffn2_scale = sb("ffn2_scale", [P, 2, 6])
        stats = sb("stats", [P, CB, 6])
        mv = sb("mv", [P, CB, 2])
        newton = sb("newton", [P, 3, 64])
        q_rstd = sb("q_rstd", [P, HEADS, CB])
        neg_max = sb("neg_max", [P, HEADS, CB])
        row_sum = sb("row_sum", [P, HEADS, CB])
        k_ss = sb("k_ss", [P, HEADS, CB])
        any_valid = sb("any_valid", [P, B])
        n_max = sb("n_max", [P, 4, 16])
        n_sum = sb("n_sum", [P, 4, 16])
        score = sb("score", [P, CB, 16])
        route = sb("route", [P, 8, CB * 16])

        A = sb("A", [P, 10240])
        Bw = sb("Bw", [P, 12288])
        H = sb("H", [P, 8192])
        S = sb("S", [P, 4608])
        R = sb("R", [P, 4608])
        X = sb("X", [P, 1024])

        def ring(region, off, n, cols=512):
            return [region[:, off + i * cols:off + (i + 1) * cols] for i in range(n)]

        def split(ap, pattern, **kw):
            return ap.rearrange(pattern, **kw)

        q_ring, q2_ring, p_ring, pt_ring = ring(S, 0, 2), ring(S, 1024, 2), ring(S, 2048, 3), ring(S, 3584, 2)
        heads = split(H[:, :], "p (h t) -> p h t", h=HEADS)
        L0_wq = split(A[:, 0:4096], "p (f n) -> p f n", f=2)
        L0_wk = A[:, 4096:6144]
        out_w = {0: split(A[:, 6144:10240], "p (h n) -> p h n", h=HEADS),
                 4: split(A[:, 4096:8192], "p (h n) -> p h n", h=HEADS)}
        L0_wvT = split(H[:, 0:2048], "p (h n) -> p h n", h=HEADS)
        L0_wo = split(H[:, 2048:6144], "p (h n) -> p h n", h=HEADS)
        L2_m = split(A[:, 0:4096], "p (f h n) -> p f h n", f=2, h=HEADS)
        L2_wqT = split(Bw[:, 0:4096], "p (h n) -> p h n", h=HEADS)
        L2_wkT = split(Bw[:, 4096:5120], "p (h n) -> p h n", h=8)
        L2_wvT = split(Bw[:, 5120:6144], "p (h n) -> p h n", h=8)
        L2_wo = split(Bw[:, 6144:10240], "p (h n) -> p h n", h=HEADS)
        mask_bias = R[:, 0:1024]
        act_ring, h_ring = ring(S, 0, 2), ring(S, 1024, 3)
        ff0 = [split(Bw[:, 4096 * i:4096 * (i + 1)], "p (k n) -> p k n", k=2) for i in range(3)]
        ff_gate = {1: ff0[0], 5: split(Bw[:, 0:1408], "p (k n) -> p k n", k=2),
                   7: split(A[:, 0:2 * MOE_ALL], "p (k n) -> p k n", k=2)}
        ff_up = {1: ff0[1], 5: split(Bw[:, 1408:2816], "p (k n) -> p k n", k=2)}
        ff_down = {1: split(Bw[:, 8192:12288], "p (m n) -> p m n", n=D),
                   5: split(Bw[:, 2816:4352], "p (m n) -> p m n", n=D),
                   7: split(Bw[:, 5888:12032], "p (m n) -> p m n", n=D)}
        router_w = split(Bw[:, 12032:12064], "p (k n) -> p k n", k=2)
        down_scale = R[:, 1024:1280]
        fp4_slot = [(R[:, 1024 * i:1024 * i + 512].bitcast(U32), R[:, 1024 * i + 512:1024 * i + 1024]) for i in range(3)]
        fp4_tmp = ring(R, 3072, 3)
        nq = {2: split(A[:, 0:512], "p (k n) -> p k n", k=2), 6: split(Bw[:, 4352:4864], "p (k n) -> p k n", k=2)}
        nkv = {2: A[:, 512:1024], 6: Bw[:, 4864:5376]}
        nout = {2: split(A[:, 1536:2048], "p (k n) -> p k n", k=2), 6: split(Bw[:, 5376:5888], "p (k n) -> p k n", k=2)}
        dca_w = A[:, 1024:1536]
        w8_raw = split(A[:, 2048:2560], "p (k n) -> p k n", k=2)
        w8_tmp = ring(A, 2560, 1)[0]
        kdca = split(A[:, 3072:5120], "p (f b h k) -> p f b h k", f=2, b=B, h=8)
        vdca = split(A[:, 5120:7168], "p (b n) -> p b n", b=B)
        dca_tok, dca_tmp = A[:, 7168:7424], A[:, 7424:7680]
        dca_ctx = A[:, 7680:7808]
        dca_ctx8 = split(A[:, 7808:8832], "p (b k) -> p b k", b=B)
        q_bias, kv_bias = R[:, 0:256], R[:, 256:768]
        dca_bias = R[:, 768:1280]
        ln_w, ln_b = R[:, 1280:1312], R[:, 1312:1344]
        dca_lnw, dca_lnb = R[:, 1344:1360], R[:, 1360:1376]
        out_bias = {2: R[:, 1376:1632], 6: R[:, 1280:1536]}
        cat, cat2, cat3 = S[:, 0:512], S[:, 512:1024], S[:, 1024:1536]
        v_tok = ring(S, 1536, 2, 256)
        nqT = ring(X, 0, 2, 256)
        n_out = X[:, 512:768]
        kbd = [H[:, 2048 * f:2048 * (f + 1)] for f in range(2)]
        vpad = [H[:, 4096 + 2048 * f:4096 + 2048 * (f + 1)] for f in range(2)]
        sel = R[:, 1536:1536 + MOE_ALL // 2].bitcast(BF16)
        comb_tok = split(R[:, 3072:3584], "p (b e) -> p b e", b=CB)
        combT = R[:, 3584:3840].bitcast(BF16)
        route_a = split(S[:, 2560:3584], "p (b e j) -> p b e j", b=CB, e=16)
        route_b = split(S[:, 3584:4608], "p (b e j) -> p b e j", b=CB, e=16)

        ld = {k: sem("ld_" + k) for k in (
            "const", "x", "ctx", "rows", "wq0", "wk0", "wvo0", "fp4_0", "fp4_1", "fp4_2", "L1", "L1rows",
            "L2", "late", "ff2", "moe1")}
        v_chain, tg_ready = sem("v_chain"), sem("tg_ready")
        ones_set, sel_chain, ctxT_mm, ctxT_cp, trig_arg, trig_sin = (
            sem("ones_set"), sem("sel_chain"), sem("ctxT_mm"), sem("ctxT_cp"), sem("trig_arg"), sem("trig_sin"))
        pre_mm, pre_cp = sem("pre_mm"), sem("pre_cp")
        fp4_done, ff2_cast, w8_ready = sem("fp4_done"), sem("ff2_cast"), sem("w8_ready")
        ln_done, xT_mm, xT_cp = sem("ln_done"), sem("xT_mm"), sem("xT_cp")
        y_ready, resid_done, stored = sem("y_ready"), sem("resid_done"), sem("stored")
        k_mm, k_sq, k_cp, k_red, k_rstd, k_scaled_v, k_scaled_g, kT_mm, kT_cp = (
            sem("k_mm"), sem("k_sq"), sem("k_cp"), sem("k_red"), sem("k_rstd"), sem("k_scaled_v"),
            sem("k_scaled_g"), sem("kT_mm"), sem("kT_cp"))
        q_mm, q_cp, q_sq, ss_mm, s_mm, nb, ex, rs, p_norm, pt_mm, pt_cp, ot_mm, ot_cp = (
            sem("q_mm"), sem("q_cp"), sem("q_sq"), sem("ss_mm"), sem("s_mm"), sem("nb"), sem("ex"), sem("rs"),
            sem("p_norm"), sem("pt_mm"), sem("pt_cp"), sem("ot_mm"), sem("ot_cp"))
        mask_set = sem("mask_set")
        g_mm, g_act, h_done, d_mm = sem("g_mm"), sem("g_act"), sem("h_done"), sem("d_mm")
        (n_qkv, n_tok, n_vtok, n_tr, n_qT, n_kbd, n_vpad, n_s, n_nb, n_ex, n_rs, n_pn, n_ptm, n_ptc, n_otm,
         n_otc, vpad_zero) = (
            sem("n_qkv"), sem("n_tok"), sem("n_vtok"), sem("n_tr"), sem("n_qT"), sem("n_kbd"), sem("n_vpad"),
            sem("n_s"), sem("n_nb"), sem("n_ex"), sem("n_rs"), sem("n_pn"), sem("n_ptm"), sem("n_ptc"),
            sem("n_otm"), sem("n_otc"), sem("vpad_zero"))
        dca_copied = sem("dca_copied")
        dca_mm, dca_tr, dca_norm, dca_ready = sem("dca_mm"), sem("dca_tr"), sem("dca_norm"), sem("dca_ready")
        r_mm, r_sig, r_comb, r_tr, r_combT = (
            sem("r_mm"), sem("r_sig"), sem("r_comb"), sem("r_tr"), sem("r_combT"))

        NAR = {s: Narrow(s) for s in (2, 6)}
        WIDE_INDEX = {0: 0, 1: 1, 8: 2, 9: 3}

        block = ctx.enter_context(nc.Block())

        @block.sync
        def _(sp):
            def load(dst, src, what):
                sp.dma_start(dst, src).then_inc(ld[what], 16)

            load(consts[:, :], dram["consts"], "const")
            load(x_sb[:, 0:CB, :], dram["x"][0:CB].rearrange("b p d -> p b d"), "x")
            load(x_sb[:, CB:B, :], dram["x"][CB:B].rearrange("b p d -> p b d"), "x")
            load(ctx_tok[:, :, :], dram["ctx"].rearrange("b p d -> p b d"), "ctx")
            load(H[:, 0:2048], dram["L0_wvT"], "wvo0")
            load(H[:, 2048:6144], dram["L0_wo"], "wvo0")
            load(L0_wk, dram["L0_wk"], "wk0")
            load(A[:, 0:4096], dram["L0_wq"], "wq0")
            load(gates[:, 0:4], dram["g_xattn"].partition_broadcast(P), "rows")
            load(gates[:, 4:8], dram["g_ffn"].partition_broadcast(P), "rows")
            load(gqk[:, 0:1], dram["gq"], "rows")
            load(gqk[:, 1:2], dram["gk"], "rows")
            load(mask8[:, :], dram["mask"].partition_broadcast(P), "rows")
            load(fside[:, :, :], dram["fside"].rearrange("b p d -> p b d"), "rows")
            load(scales8[:, 0:1], dram["scale"].partition_broadcast(P), "rows")
            load(scales8[:, 1:2], dram["scale1"].partition_broadcast(P), "rows")
            for p in range(12):
                if p >= 3:
                    sp.wait_ge(fp4_done, 2 * (p - 2))
                name, cols = ("gate", "up", "down")[p // 4], slice(512 * (p % 4), 512 * (p % 4) + 512)
                packed, scale = fp4_slot[p % 3]
                load(packed.bitcast(I32), dram[f"ff0_{name}"][:, cols], f"fp4_{p % 3}")
                load(scale,
                     dram[f"ff0_{name}_s"][:, cols].unsqueeze(1).broadcast_to([8, 16, 512]), f"fp4_{p % 3}")
            sp.wait_ge(fp4_done, 24)
            for dst, name in ((q_bias, "bq"), (kv_bias, "bkv"), (dca_bias, "bkv_dca"), (ln_w[:, 0:16], "qn_w"),
                              (ln_w[:, 16:32], "kn_w"), (ln_b[:, 0:16], "qn_b"), (ln_b[:, 16:32], "kn_b"),
                              (dca_lnw, "kn_dca_w"), (dca_lnb, "kn_dca_b"), (out_bias[2], "bo")):
                load(dst, dram[name].partition_broadcast(P), "L1rows")
            sp.wait_ge(y_ready, 4)
            load(A[:, 0:512], dram["L1_wq"], "L1")
            load(A[:, 512:1024], dram["L1_wkv"], "L1")
            load(A[:, 1024:1536], dram["L1_dca"], "L1")
            load(A[:, 1536:2048], dram["L1_wo"], "L1")
            load(A[:, 2048:2560], dram["w8"], "L1")
            sp.wait_ge(y_ready, 8)
            load(Bw[:, 0:4096], dram["L2_wqT"], "L2")
            load(Bw[:, 4096:5120], dram["L2_wkT"], "L2")
            load(Bw[:, 5120:6144], dram["L2_wvT"], "L2")
            load(Bw[:, 6144:10240], dram["L2_wo"], "L2")
            sp.wait_ge(resid_done, 12)
            load(down_scale, dram["s_down"].partition_broadcast(P), "late")
            load(out_bias[6], dram["bout"].partition_broadcast(P), "late")
            load(ffn2_scale[:, 0, :], dram["s_gate"], "late")
            load(ffn2_scale[:, 1, :], dram["s_up"], "late")
            sp.wait_ge(pre_mm, 24)
            load(Bw[:, 0:1408].bitcast(I32), dram["ff2_gate"], "ff2")
            load(Bw[:, 1408:2816].bitcast(I32), dram["ff2_up"], "ff2")
            load(Bw[:, 2816:4352].bitcast(I32), dram["ff2_down"], "ff2")
            load(Bw[:, 4352:4864], dram["L3_wq"], "ff2")
            load(Bw[:, 4864:5376], dram["L3_wkv"], "ff2")
            load(Bw[:, 5376:5888], dram["L3_wo"], "ff2")
            load(Bw[:, 5888:12032], dram["moe_w2"], "ff2")
            load(Bw[:, 12032:12064], dram["router"], "ff2")
            sp.wait_ge(y_ready, 20)
            load(A[:, 0:2 * MOE_ALL], dram["moe_w1"], "moe1")
            for c in range(2):
                for j in range(2):
                    sp.wait_ge(resid_done, 2 * (14 + c) + j + 1)
                    b = CB * c + 2 * j
                    sp.dma_start(out[b:b + 2].rearrange("b p d -> p b d"), x_sb[:, b:b + 2, :]).then_inc(stored, 16)
            sp.wait_ge(stored, 64)

        @block.tensor
        def _(pe):
            def transpose_x(n):
                c = n % 2
                pe.wait_ge(ln_done, n + 1)
                for f in range(2):
                    for b in range(CB):
                        src = xn[:, c, b, f::2] if n // 2 == 1 else xn[:, c, b, f * P:(f + 1) * P]
                        mm = nc.tensor.transpose(bank[f][:, b * P:(b + 1) * P], src, ident)
                mm.then_inc(xT_mm, 1)

            def weight_products(which):
                units = [("n", i) for i in range(8)] if which == 0 else [("m", i) for i in range(8)] + [("n", i) for i in range(8)]
                base = 0 if which == 0 else 8
                for u, (kind, i) in enumerate(units):
                    if base + u >= 4:
                        pe.wait_ge(pre_cp, base + u - 3)
                    dst = bank[2 + (base + u) % 4]
                    for j in range(2):
                        h = 2 * i + j
                        if kind == "n":
                            wv = L0_wvT[:, h, :] if which == 0 else L2_wvT[:, h // 2, :]
                            wo = L0_wo[:, h, :] if which == 0 else L2_wo[:, h, :]
                            mm = nc.tensor.matmul(dst[:, j * 256:(j + 1) * 256], wv, wo, start=True, stop=True)
                        else:
                            for f in range(2):
                                mm = nc.tensor.matmul(dst[:, f * 256 + j * 128:f * 256 + (j + 1) * 128],
                                                      L2_wqT[:, h, f * P:(f + 1) * P], L2_wkT[:, h // 2, :],
                                                      start=True, stop=True)
                    mm.then_inc(pre_mm, 1)

            def wide(n):
                a, c, s = WIDE_INDEX[n], n % 2, n // 2
                base = HEADS * a
                if s == 0:
                    pe.wait_ge(ld["wk0"], 16)
                    for u in range(16):
                        if u >= 2:
                            pe.wait_ge(k_cp, 16 * a + u - 1)
                        elif a == 0:
                            pe.wait_ge(pre_cp, 8)
                        nc.tensor.matmul(bank[2 + u % 2][:, :], ctxT[:, CB * c + u // 4, :],
                                         L0_wk[:, 512 * (u % 4):512 * (u % 4) + 512], start=True, stop=True)\
                            .then_inc(k_mm, 1)
                    pe.wait_ge(k_cp, 16 * a + 16)
                    pe.wait_ge(ld["wq0"], 16)
                else:
                    pe.wait_ge(pre_cp, 24)
                pe.wait_ge(xT_cp, n + 1)
                pe.wait_ge(resid_done, 2 * n)
                for i in range(HEADS + 4):
                    if i < HEADS:
                        if i:
                            pe.wait_ge(q_sq if s == 0 else q_cp, base + i)
                        for f in range(2):
                            w = L0_wq[:, f, i * P:(i + 1) * P] if s == 0 else L2_m[:, f, i, :]
                            mm = nc.tensor.matmul(bank[0][:, :], w, xT[:, c, f, :], start=(f == 0), stop=(f == 1))
                        mm.then_inc(q_mm, 1)
                        if s == 0:
                            pe.wait_ge(k_scaled_g if i % 2 else k_scaled_v, 8 * a + i // 2 + 1)
                            if i:
                                pe.wait_ge(kT_cp, base + i)
                            for b in range(CB):
                                mm = nc.tensor.transpose(bank[1][:, b * P:(b + 1) * P],
                                                         heads[:, i, b * P:(b + 1) * P], ident)
                            mm.then_inc(kT_mm, 1)
                    h = i - 1
                    if 0 <= h < HEADS:
                        qT = q_ring[h % 2]
                        if s == 0:
                            pe.wait_ge(q_sq, base + h + 1)
                            if h:
                                pe.wait_ge(nb, base + h)
                            for b in range(CB):
                                mm = nc.tensor.matmul(bank[6][:, b * P:(b + 1) * P],
                                                      q2_ring[h % 2][:, b * P:(b + 1) * P], ones[:, :],
                                                      start=True, stop=True)
                            mm.then_inc(ss_mm, 1)
                            pe.wait_ge(kT_cp, base + h + 1)
                        else:
                            pe.wait_ge(q_cp, base + h + 1)
                        if h >= 2:
                            pe.wait_ge(ex, base + h - 1)
                        for b in range(CB):
                            keys = heads[:, h, b * P:(b + 1) * P] if s == 0 else ctxT[:, CB * c + b, :]
                            mm = nc.tensor.matmul(bank[2 + h % 2][:, b * P:(b + 1) * P], qT[:, b * P:(b + 1) * P],
                                                  keys, start=True, stop=True)
                        mm.then_inc(s_mm, 1)
                    h = i - 3
                    if 0 <= h < HEADS:
                        pe.wait_ge(p_norm, base + h + 1)
                        if h:
                            pe.wait_ge(pt_cp, base + h)
                        for b in range(CB):
                            mm = nc.tensor.transpose(bank[4][:, b * P:(b + 1) * P],
                                                     p_ring[h % 3][:, b * P:(b + 1) * P], ident)
                        mm.then_inc(pt_mm, 1)
                    h = i - 4
                    if 0 <= h < HEADS:
                        pe.wait_ge(pt_cp, base + h + 1)
                        if h >= 2:
                            pe.wait_ge(ot_cp, base + h - 1)
                        for b in range(CB):
                            mm = nc.tensor.matmul(bank[5 + 2 * (h % 2)][:, b * P:(b + 1) * P],
                                                  ctx_tok[:, CB * c + b, :], pt_ring[h % 2][:, b * P:(b + 1) * P],
                                                  start=True, stop=True)
                        mm.then_inc(ot_mm, 1)
                pe.wait_ge(ot_cp, base + HEADS)
                for j in range(2):
                    for b in (2 * j, 2 * j + 1):
                        for h in range(HEADS):
                            mm = nc.tensor.matmul(bank[6 + j][:, (b % 2) * D:(b % 2 + 1) * D],
                                                  heads[:, h, b * P:(b + 1) * P], out_w[s][:, h, :],
                                                  start=(h == 0), stop=(h == HEADS - 1))
                    mm.then_inc(y_ready, 1)

            def route_pe(n):
                c = n % 2
                for b in range(CB):
                    for f in range(2):
                        mm = nc.tensor.matmul(bank[4][:, b * 16:(b + 1) * 16], xT[:, c, f, b * P:(b + 1) * P],
                                              router_w[:, f, :], start=(f == 0), stop=(f == 1))
                mm.then_inc(r_mm, 1)
                pe.wait_ge(r_comb, n - 13)
                for b in range(CB):
                    mm = nc.tensor.transpose(bank[5][:, b * P:(b + 1) * P], comb_tok[:, b, :], ident)
                mm.then_inc(r_tr, 1)
                pe.wait_ge(r_combT, n - 13)

            def ffn(n):
                s, c = n // 2, n % 2
                base, tiles = FFN_BASE[n], TILES[s]
                pe.wait_ge(xT_cp, n + 1)
                if s == 1:
                    pe.wait_ge(fp4_done, 24)
                elif s == 5:
                    pe.wait_ge(ff2_cast, 3)
                else:
                    pe.wait_ge(ld["moe1"], 16)
                    pe.wait_ge(ld["ff2"], 128)
                    route_pe(n)
                pe.wait_ge(resid_done, 2 * n)
                for i in range(len(tiles) + 1):
                    if i < len(tiles):
                        w = tiles[i]
                        if i >= 2:
                            pe.wait_ge(g_act, base + i - 1)
                        for f in range(2):
                            mm = nc.tensor.matmul(bank[i % 2][0:w, :], ff_gate[s][:, f, i * P:i * P + w],
                                                  xT[:, c, f, :], start=(f == 0), stop=(f == 1))
                        if i >= 2:
                            pe.wait_ge(h_done, base + i - 1)
                        if s == 7:
                            mm = nc.tensor.matmul(bank[2 + i % 2][0:w, :], sel[:, i * P:i * P + w], combT[:, :],
                                                  start=True, stop=True)
                        else:
                            for f in range(2):
                                mm = nc.tensor.matmul(bank[2 + i % 2][0:w, :], ff_up[s][:, f, i * P:i * P + w],
                                                      xT[:, c, f, :], start=(f == 0), stop=(f == 1))
                        mm.then_inc(g_mm, 1)
                    m = i - 1
                    if m >= 0:
                        w = tiles[m]
                        pe.wait_ge(h_done, base + m + 1)
                        for b in range(CB):
                            mm = nc.tensor.matmul(bank[6 + b // 2][:, (b % 2) * D:(b % 2 + 1) * D],
                                                  h_ring[m % 3][0:w, b * P:(b + 1) * P], ff_down[s][0:w, m, :],
                                                  start=(m == 0 and b % 2 == 0), stop=(m == len(tiles) - 1),
                                                  skip_group_check=True)
                            if m == len(tiles) - 1 and b % 2:
                                mm.then_inc(y_ready, 1)
                            elif m < len(tiles) - 1 and b == CB - 1:
                                mm.then_inc(d_mm, 1)

            def fp8(n):
                pe.wait_ge(xT_cp, n + 1)
                pe.wait_ge(w8_ready, 1)
                pe.wait_ge(resid_done, 2 * n)
                for j in range(2):
                    for b in (2 * j, 2 * j + 1):
                        for f in range(2):
                            mm = nc.tensor.matmul(bank[6 + j][:, (b % 2) * D:(b % 2 + 1) * D],
                                                  xqT[:, f, b * P:(b + 1) * P], w8[:, f, :],
                                                  start=(f == 0), stop=(f == 1))
                    mm.then_inc(y_ready, 1)

            def dca_setup():
                pe.wait_ge(ld["L1"], 80)
                pe.wait_ge(dca_copied, 2)
                nc.tensor.matmul(bank[0][:, 0:256], dca_ctx, dca_w[:, 0:256], start=True, stop=True)\
                    .then_inc(dca_mm, 1)
                for b in range(B):
                    if b >= 2:
                        pe.wait_ge(dca_ready, b - 1)
                    nc.tensor.matmul(bank[2 + b % 2][:, 0:256],
                                     dca_ctx8[:, b, :],
                                     dca_w[:, 256:512], start=True, stop=True).then_inc(dca_mm, 1)
                pe.wait_ge(dca_norm, 1)
                for f in range(2):
                    mm = nc.tensor.transpose(bank[1][:, f * P:(f + 1) * P], dca_tok[:, f * P:(f + 1) * P], ident)
                mm.then_inc(dca_tr, 1)
                pe.wait_ge(dca_ready, B + 2)

            def narrow(n):
                s, c = n // 2, n % 2
                na = NAR[s]
                pe.wait_ge(xT_cp, n + 1)
                if n == 4:
                    dca_setup()
                if s == 6:
                    pe.wait_ge(ld["ff2"], 128)
                pe.wait_ge(resid_done, 2 * n)

                def project(t):
                    bt = na.batch_base + CB * c + t
                    if bt:
                        pe.wait_ge(n_vtok, bt)
                        pe.wait_ge(n_tok, bt)
                    nc.tensor.matmul(bank[0][:, :], ctxT[:, CB * c + t, :], nkv[s], start=True, stop=True)
                    for f in range(2):
                        mm = nc.tensor.matmul(bank[1][:, 0:256], xT[:, c, f, t * P:(t + 1) * P], nq[s][:, f, :],
                                              start=(f == 0), stop=(f == 1))
                    mm.then_inc(n_qkv, 1)

                def turn(t):
                    bt = na.batch_base + CB * c + t
                    pe.wait_ge(n_tok, bt + 1)
                    if bt:
                        pe.wait_ge(n_kbd, 2 * bt)
                        pe.wait_ge(n_qT, bt)
                    for k in range(4):
                        mm = nc.tensor.transpose(bank[2][:, k * P:(k + 1) * P], cat[:, k * P:(k + 1) * P], ident)
                    mm.then_inc(n_tr, 1)

                def finish(t):
                    bt = na.batch_base + CB * c + t
                    pe.wait_ge(n_otc, bt + 1)
                    for f in range(2):
                        mm = nc.tensor.matmul(bank[6 + t // 2][:, (t % 2) * D:(t % 2 + 1) * D],
                                              n_out[:, f * P:(f + 1) * P], nout[s][:, f, :],
                                              start=(f == 0), stop=(f == 1))
                    if t % 2:
                        mm.then_inc(y_ready, 1)

                steps = list(na.steps(c))
                project(0)
                turn(0)
                for i in range(len(steps) + 4):
                    if i < len(steps):
                        t, f, g, k, gi = steps[i]
                        bt = na.batch_base + CB * c + t
                        pe.wait_ge(n_qT, bt + 1)
                        if gi >= 2:
                            pe.wait_ge(n_ex, gi - 1)
                        dst = bank[3 + gi % 2]
                        if f == "dca":
                            for ff in range(2):
                                mm = nc.tensor.matmul(dst[:, ff * P:(ff + 1) * P], nqT[bt % 2][:, ff * P:(ff + 1) * P],
                                                      kdca[:, ff, CB * c + t, :, :], start=True, stop=True)
                        else:
                            pe.wait_ge(n_kbd, 2 * bt + f + 1)
                            w = 4 * na.keys
                            mm = nc.tensor.matmul(dst[:, 0:w], nqT[bt % 2][:, f * P:(f + 1) * P],
                                                  kbd[f][:, g * w:(g + 1) * w], start=True, stop=True)
                        mm.then_inc(n_s, 1)
                        if k == 0 and t + 1 < CB:
                            project(t + 1)
                        if k == na.n // 2 and t + 1 < CB:
                            turn(t + 1)
                    if i >= 4 and steps[i - 4][3] == na.n - 1:
                        finish(steps[i - 4][0])
                    j = i - 2
                    if 0 <= j < len(steps):
                        t, f, g, k, gi = steps[j]
                        pe.wait_ge(n_pn, gi + 1)
                        if gi:
                            pe.wait_ge(n_ptc, gi)
                        for u in range(2 if f == "dca" else 4):
                            w = P if f == "dca" else na.keys
                            mm = nc.tensor.transpose(bank[5][0:w, u * P:(u + 1) * P],
                                                     p_ring[gi % 3][:, u * w:(u + 1) * w], ident)
                        mm.then_inc(n_ptm, 1)
                    j = i - 3
                    if 0 <= j < len(steps):
                        t, f, g, k, gi = steps[j]
                        bt = na.batch_base + CB * c + t
                        dst = bank[7 if t < 2 else 6]
                        pe.wait_ge(n_ptc, gi + 1)
                        if k == 0:
                            if bt:
                                pe.wait_ge(n_otc, bt)
                            if t == 2:
                                pe.wait_ge(resid_done, 2 * n + 1)
                        if f == "dca":
                            for ff in range(2):
                                mm = nc.tensor.matmul(dst[:, ff * P:(ff + 1) * P],
                                                      vdca[:, CB * c + t, ff * P:(ff + 1) * P],
                                                      pt_ring[gi % 2][:, ff * P:(ff + 1) * P],
                                                      start=False, stop=True, skip_group_check=True)
                        else:
                            pe.wait_ge(n_vpad, 2 * bt + f + 1)
                            for u in range(4):
                                h = 4 * g + u
                                mm = nc.tensor.matmul(dst[:, f * P:(f + 1) * P],
                                                      vpad[f][0:na.keys, h * P:(h + 1) * P],
                                                      pt_ring[gi % 2][0:na.keys, u * P:(u + 1) * P],
                                                      start=(k == 0 and u == 0), stop=(h == na.heads - 1),
                                                      skip_group_check=True)
                        mm.then_inc(n_otm, 1)

            pe.wait_ge(ld["const"], 16)
            pe.wait_ge(ld["ctx"], 16)
            for b in range(B):
                mm = nc.tensor.transpose(bank[4 + b // 4][:, (b % 4) * P:(b % 4 + 1) * P], ctx_tok[:, b, :], ident)
            mm.then_inc(ctxT_mm, 1)
            pe.wait_ge(ctxT_cp, 1)
            pe.wait_ge(ld["wvo0"], 32)
            weight_products(0)
            pe.wait_ge(ones_set, 1)
            for n in range(STAGES):
                if n == 8:
                    pe.wait_ge(ld["L2"], 64)
                    weight_products(4)
                transpose_x(n)
                {WIDE: wide, FFN: ffn, NARROW: narrow, FP8: fp8}[KIND[n // 2]](n)

        @block.scalar
        def _(act):
            def copy_xT(n):
                act.wait_ge(xT_mm, n + 1)
                for f in range(2):
                    dst = xqT[:, f, :] if n // 2 == 3 else xT[:, n % 2, f, :]
                    i = nc.scalar.activation(dst, bank[f][:, :], ACT.Copy)
                i.then_inc(xT_cp, 1)

            def copy_products(which):
                base = 0 if which == 0 else 8
                for u in range(8 if which == 0 else 16):
                    act.wait_ge(pre_mm, base + u + 1)
                    src = bank[2 + (base + u) % 4]
                    if which == 4 and u < 8:
                        dst = L2_m[:, :, 2 * u:2 * u + 2, :]
                        src = src[:, :].rearrange("p (f h n) -> p f h n", f=2, h=2)
                    else:
                        dst = out_w[which][:, 2 * (u % 8):2 * (u % 8) + 2, :]
                        src = src[:, :].rearrange("p (h n) -> p h n", h=2)
                    nc.scalar.activation(dst, src, ACT.Copy).then_inc(pre_cp, 1)

            def wide(n):
                a, c, s = WIDE_INDEX[n], n % 2, n // 2
                base = HEADS * a
                if s == 0:
                    for u in range(16):
                        act.wait_ge(k_mm, 16 * a + u + 1)
                        if u >= 2:
                            act.wait_ge(k_red, 16 * a + u - 1)
                        src = bank[2 + u % 2][:, :]
                        nc.scalar.activation(q2_ring[u % 2], src, ACT.Square).then_inc(k_sq, 1)
                        b, g = u // 4, u % 4
                        nc.scalar.activation(heads[:, 4 * g:4 * g + 4, b * P:(b + 1) * P],
                                             src.rearrange("p (h d) -> p h d", h=4), ACT.Copy).then_inc(k_cp, 1)
                copy_xT(n)
                if s == 0:
                    act.wait_ge(k_red, 16 * a + 16)
                for i in range(HEADS + 1):
                    if i < HEADS:
                        act.wait_ge(q_mm, base + i + 1)
                        if i >= 2:
                            act.wait_ge(s_mm, base + i - 1)
                        nc.scalar.activation(q_ring[i % 2], bank[0][:, :], ACT.Copy).then_inc(q_cp, 1)
                        if s == 0:
                            nc.scalar.activation(q2_ring[i % 2], bank[0][:, :], ACT.Square).then_inc(q_sq, 1)
                    h = i - 1
                    if h >= 0:
                        act.wait_ge(nb, base + h + 1)
                        if h >= 3:
                            act.wait_ge(pt_mm, base + h - 2)
                        for b in range(CB):
                            cols = slice(b * P, (b + 1) * P)
                            e = nc.scalar.activation(
                                p_ring[h % 3][:, cols], bank[2 + h % 2][:, cols], ACT.Exp,
                                bias=neg_max[:, h, b:b + 1],
                                scale=q_rstd[:, h, b:b + 1] if s == 0 else float(P) ** -0.5,
                                accum_out=row_sum[:, h, b:b + 1])
                        e.then_inc(ex, 1)

            def ffn(n):
                s = n // 2
                base, tiles = FFN_BASE[n], TILES[s]
                copy_xT(n)
                if s == 7:
                    act.wait_ge(r_mm, n - 13)
                    nc.scalar.activation(score[:, :, :], bank[4][:, 0:64].rearrange("p (b e) -> p b e", b=CB),
                                         ACT.Sigmoid).then_inc(r_sig, 1)
                for i, w in enumerate(tiles):
                    act.wait_ge(g_mm, base + i + 1)
                    if i >= 2:
                        act.wait_ge(h_done, base + i - 1)
                    if s == 1:
                        g = nc.scalar.activation(act_ring[i % 2][0:w, :], bank[i % 2][0:w, :], ACT.Gelu_apprx_tanh)
                    elif s == 5:
                        g = nc.scalar.activation(act_ring[i % 2][0:w, :], bank[i % 2][0:w, :], ACT.Silu,
                                                 scale=ffn2_scale[0:w, 0, i:i + 1])
                    else:
                        g = nc.scalar.activation(act_ring[i % 2][0:w, :], bank[i % 2][0:w, :], ACT.Silu)
                    g.then_inc(g_act, 1)

            def narrow(n):
                s, c = n // 2, n % 2
                na = NAR[s]
                copy_xT(n)

                def copy_qT(t):
                    bt = na.batch_base + CB * c + t
                    act.wait_ge(n_tr, bt + 1)
                    nc.scalar.activation(nqT[bt % 2], bank[2][:, 0:256], ACT.Copy).then_inc(n_qT, 1)

                steps = list(na.steps(c))
                copy_qT(0)
                for i in range(len(steps) + 3):
                    if i < len(steps):
                        t, f, g, k, gi = steps[i]
                        act.wait_ge(n_nb, gi + 1)
                        if gi >= 3:
                            act.wait_ge(n_ptm, gi - 2)
                        if f == "dca":
                            nc.scalar.activation(p_ring[gi % 3][:, 0:256], cat3[:, 0:256], ACT.Exp,
                                                 scale=na.scale).then_inc(n_ex, 1)
                        else:
                            for u in range(4):
                                cols = slice(u * na.keys, (u + 1) * na.keys)
                                e = nc.scalar.activation(p_ring[gi % 3][:, cols], bank[3 + gi % 2][:, cols], ACT.Exp,
                                                         bias=n_max[:, gi % 4, u:u + 1], scale=na.scale,
                                                         accum_out=n_sum[:, gi % 4, u:u + 1])
                            e.then_inc(n_ex, 1)
                        if k == na.n // 2 and t + 1 < CB:
                            copy_qT(t + 1)
                    j = i - 3
                    if 0 <= j and steps[j][3] == na.n - 1:
                        t, f, g, k, gi = steps[j]
                        bt = na.batch_base + CB * c + t
                        act.wait_ge(n_otm, gi + 1)
                        nc.scalar.activation(n_out, bank[7 if t < 2 else 6][:, 0:256], ACT.Copy).then_inc(n_otc, 1)

            act.wait_ge(ld["rows"], 128)
            nc.scalar.activation(tg[:, :], gates[:, :], ACT.Tanh).then_inc(tg_ready, 1)
            act.wait_ge(trig_arg, 1)
            nc.scalar.activation(trig[:, 4:6, :], trig[:, 2:4, :], ACT.Sin).then_inc(trig_sin, 1)
            act.wait_ge(ctxT_mm, 1)
            for i in range(2):
                m = nc.scalar.activation(ctxT[:, 4 * i:4 * i + 4, :].rearrange("p b k -> p (b k)"), bank[4 + i][:, :],
                                         ACT.Copy)
            m.then_inc(ctxT_cp, 1)
            copy_products(0)
            for n in range(STAGES):
                if n == 8:
                    copy_products(4)
                kind = KIND[n // 2]
                if kind == FP8:
                    copy_xT(n)
                else:
                    {WIDE: wide, FFN: ffn, NARROW: narrow}[kind](n)

        @block.gpsimd
        def _(pool):
            def broadcast(ap, shape):
                return ap.unsqueeze(2).broadcast_to(shape)

            def zero_vpad(i):
                nc.gpsimd.memset(H[:, 4096:8192], 0.0).then_inc(vpad_zero, 1)
                pool.wait_ge(vpad_zero, i)

            def selection():
                rows = sel.rearrange("p (e j) -> p e j", e=EXPERTS + 1)
                nc.gpsimd.memset(sel, 0.0).then_inc(sel_chain, 1)
                for k in range(3):
                    pool.wait_ge(sel_chain, k + 1)
                    nc.gpsimd.affine_select(out=rows, in_=rows, compare_op=ALU.not_equal, fill=1.0,
                                            base=-(EXPERTS + 1) * k, pattern=[[-1, EXPERTS + 1], [0, MOE_H]],
                                            channel_multiplier=1).then_inc(sel_chain, 1)

            def wide(n):
                a, s = WIDE_INDEX[n], n // 2
                base = HEADS * a
                if s == 0:
                    pool.wait_ge(k_rstd, a + 1)
                    pool.wait_ge(k_cp, 16 * a + 16)
                    for h in range(1, HEADS, 2):
                        v = heads[:, h, :].rearrange("p (b d) -> p b d", b=CB)
                        nc.gpsimd.tensor_tensor(v, v, broadcast(k_ss[:, h, :], [P, CB, P]), ALU.mult)\
                            .then_inc(k_scaled_g, 1)
                for h in range(HEADS):
                    pool.wait_ge(rs, base + h + 1)
                    v = p_ring[h % 3].rearrange("p (b k) -> p b k", b=CB)
                    nc.gpsimd.tensor_tensor(v, v, broadcast(row_sum[:, h, :], [P, CB, P]), ALU.mult)\
                        .then_inc(p_norm, 1)

            def narrow(n):
                s, c = n // 2, n % 2
                na = NAR[s]
                if c == 0:
                    pool.wait_ge(y_ready, 2 * n)
                    zero_vpad(1 if s == 2 else 2)

                def pad_v(t, f):
                    bt = na.batch_base + CB * c + t
                    pool.wait_ge(n_vtok, bt + 1)
                    if bt > na.batch_base:
                        last = na.group_base + (CB * c + t - 1) * na.n + (f + 1) * na.groups
                        pool.wait_ge(n_otm, last)
                    dst = bass.AP(vpad[f].tensor, vpad[f].offset,
                                  [list(vpad[f].ap[0]), [P + na.hd, na.heads], [1, na.hd]])
                    nc.gpsimd.tensor_copy(
                        dst, v_tok[bt % 2][:, f * P:(f + 1) * P].rearrange("p (h d) -> p h d", d=na.hd))\
                        .then_inc(n_vpad, 1)

                steps = list(na.steps(c))
                pad_v(0, 0)
                pad_v(0, 1)
                for i, (t, f, g, k, gi) in enumerate(steps):
                    if t and k == na.groups:
                        pad_v(t, 1)
                    pool.wait_ge(n_rs, gi + 1)
                    m, w = (16, 16) if f == "dca" else (4, na.keys)
                    v = p_ring[gi % 3][:, 0:m * w].rearrange("p (h k) -> p h k", h=m)
                    nc.gpsimd.tensor_tensor(v, v, broadcast(n_sum[:, gi % 4, 0:m], [P, m, w]), ALU.mult)\
                        .then_inc(n_pn, 1)
                    if k == na.n - 1 and t + 1 < CB:
                        pad_v(t + 1, 0)

            for n in range(STAGES):
                if n == 4:
                    pool.wait_ge(y_ready, 4)
                    dca_keys = ctxT[:, :, 112:128]
                    nc.gpsimd.tensor_copy(dca_ctx.rearrange("p (b k) -> p b k", b=B), dca_keys)\
                        .then_inc(dca_copied, 1)
                    shape = [P, B, 8, 16]
                    nc.gpsimd.tensor_copy(dca_ctx8.rearrange("p b (r k) -> p b r k", r=8),
                                          dca_keys.unsqueeze(2).broadcast_to(shape)).then_inc(dca_copied, 1)
                if n == 12:
                    pool.wait_ge(resid_done, 12)
                    selection()
                if KIND[n // 2] == WIDE:
                    wide(n)
                elif KIND[n // 2] == NARROW:
                    narrow(n)

        @block.vector
        def _(dve):
            count = [0]

            def link(ins):
                count[0] += 1
                ins.then_inc(v_chain, 1)
                dve.wait_ge(v_chain, count[0])

            def tt(o, a, b, op):
                return nc.vector.tensor_tensor(o, a, b, op)

            def ts(o, a, s1, s2, op0, op1=ALU.bypass):
                return nc.vector.tensor_scalar(o, a, s1, s2, op0, op1) if s2 is not None else \
                    nc.vector.tensor_scalar(o, a, s1, None, op0)

            def stt(o, a, s, b, op0, op1):
                return nc.vector.scalar_tensor_tensor(o, a, s, b, op0, op1)

            def rsqrt(dst, v, scale, eps, width):
                x, y, t = (newton[:, k, 0:width] for k in range(3))
                link(ts(x, v, scale, eps, ALU.mult, ALU.add))
                link(ts(t.bitcast(I32), x.bitcast(I32), 1, None, ALU.logical_shift_right))
                link(ts(y.bitcast(I32), t.bitcast(I32), -1.0, RSQRT_SEED, ALU.mult, ALU.add))
                for k in range(3):
                    link(tt(t, y, y, ALU.mult))
                    link(stt(t, t, -0.5, x, ALU.mult, ALU.mult))
                    if k < 2:
                        link(stt(y, t, 1.5, y, ALU.add, ALU.mult))
                return stt(dst, t, 1.5, y, ALU.add, ALU.mult)

            def quantise(v, t, u, scale):
                link(ts(v, v, scale, None, ALU.mult))
                link(ts(t.bitcast(U32), v.bitcast(U32), 0x7F800000, None, ALU.bitwise_and))
                link(ts(t, t, 2.0 ** -6, 1.5 * 2.0 ** 20, ALU.max, ALU.mult))
                link(tt(u, v, t, ALU.add))
                link(tt(v, u, t, ALU.subtract))
                link(ts(t, v, 1.1 * 2.0 ** 119, None, ALU.mult))
                return stt(v, t, 0.0, v, ALU.mult, ALU.add)

            def layer_norm(n):
                c = n % 2
                for b in range(CB):
                    nc.vector.bn_stats(stats[:, b, :], x_sb[:, CB * c + b, :]).then_inc(v_chain, 1)
                    count[0] += 1
                dve.wait_ge(v_chain, count[0])
                for b in range(CB):
                    nc.vector.bn_aggr(mv[:, b, :], stats[:, b, :]).then_inc(v_chain, 1)
                    count[0] += 1
                dve.wait_ge(v_chain, count[0])
                link(rsqrt(newton[:, 0, 60:64], mv[:, :, 1], 1.0, 1e-5, CB))
                if n >= 2:
                    dve.wait_ge(xT_mm, n - 1)
                for b in range(CB):
                    i = ts(xn[:, c, b, :], x_sb[:, CB * c + b, :], mv[:, b, 0:1], newton[:, 0, 60 + b:61 + b],
                           ALU.subtract, ALU.mult)
                    if b < CB - 1 or n // 2 == 3:
                        link(i)
                    else:
                        i.then_inc(ln_done, 1)
                if n // 2 == 3:
                    flat = xn[:, c, :, :].rearrange("p b d -> p (b d)")
                    quantise(flat, S[:, 0:1024], S[:, 1024:2048], scales8[:, 0:1]).then_inc(ln_done, 1)
                dve.wait_ge(ln_done, n + 1)

            def residual(n, j):
                s, c = n // 2, n % 2
                dve.wait_ge(y_ready, 2 * n + j + 1)
                x = x_sb[:, CB * c + 2 * j:CB * c + 2 * j + 2, :]
                y = bank[6 + j][:, :].rearrange("p (b d) -> p b d", b=2)
                gate = tg[:, s // 2 + 4 * (s % 2):s // 2 + 4 * (s % 2) + 1]
                if s == 3:
                    gate = scales8[:, 2:3]
                if s == 5:
                    if j:
                        dve.wait_ge(resid_done, 2 * n + 1)
                    t = X[:, 0:512].rearrange("p (b d) -> p b d", b=2)
                    link(tt(t, y, down_scale.unsqueeze(1).broadcast_to([P, 2, D]), ALU.mult))
                    i = stt(x, t, gate, x, ALU.mult, ALU.add)
                elif s in (2, 6):
                    t = X[:, 512 * 0 + 768:1024]
                    link(ts(t, out_bias[s], gate, None, ALU.mult))
                    link(tt(x, x, t.unsqueeze(1).broadcast_to([P, 2, D]), ALU.add))
                    i = stt(x, y, gate, x, ALU.mult, ALU.add)
                else:
                    i = stt(x, y, gate, x, ALU.mult, ALU.add)
                i.then_inc(resid_done, 1)

            def unpack_fp4(p, high):
                packed, scale = fp4_slot[p % 3]
                code, mag, sign = (t.bitcast(U32) for t in fp4_tmp)
                signed = fp4_tmp[0]
                if not high:
                    dve.wait_ge(ld[f"fp4_{p % 3}"], 32 * (p // 3 + 1))
                if high:
                    link(ts(code, packed, 2, 28, ALU.logical_shift_right, ALU.bitwise_and))
                else:
                    link(ts(code, packed, 2, 28, ALU.logical_shift_left, ALU.bitwise_and))
                link(tt(mag, fp4_table[:, :].broadcast_to([P, 512]), code, ALU.logical_shift_right))
                link(ts(mag, mag, 15, None, ALU.bitwise_and))
                link(ts(sign, packed, 7 if high else 3, 1, ALU.logical_shift_right, ALU.bitwise_and))
                link(stt(signed, sign, 0.5, scale, ALU.subtract, ALU.mult))
                dst = ff0[p // 4][:, int(high), 512 * (p % 4):512 * (p % 4) + 512]
                stt(dst, mag, -1.0, signed, ALU.mult, ALU.mult).then_inc(fp4_done, 1)
                dve.wait_ge(fp4_done, 2 * p + int(high) + 1)

            def wide(n):
                a, c, s = WIDE_INDEX[n], n % 2, n // 2
                base = HEADS * a
                if s == 0:
                    for u in range(16):
                        dve.wait_ge(k_sq, 16 * a + u + 1)
                        b, g = u // 4, u % 4
                        nc.vector.tensor_reduce(k_ss[:, 4 * g:4 * g + 4, b],
                                                q2_ring[u % 2].rearrange("p (h d) -> p h d", h=4), AX, ALU.add)\
                            .then_inc(k_red, 1)
                    dve.wait_ge(k_red, 16 * a + 16)
                    flat = k_ss[:, :, :].rearrange("p h b -> p (h b)")
                    rsqrt(flat, flat, 1.0 / P, 1e-5, 64).then_inc(k_rstd, 1)
                    dve.wait_ge(k_rstd, a + 1)
                    dve.wait_ge(k_cp, 16 * a + 16)
                    for h in range(0, HEADS, 2):
                        v = heads[:, h, :].rearrange("p (b d) -> p b d", b=CB)
                        tt(v, v, k_ss[:, h, :].unsqueeze(2).broadcast_to([P, CB, P]), ALU.mult)\
                            .then_inc(k_scaled_v, 1)
                elif c == 0:
                    dve.wait_ge(resid_done, 12)
                    ts(mask_bias, mask8[:, :], 1.0, NEG, ALU.subtract, ALU.mult).then_inc(mask_set, 1)
                    nc.vector.tensor_reduce(any_valid[:, :], mask8[:, :].rearrange("p (b k) -> p b k", b=B), AX,
                                            ALU.max).then_inc(mask_set, 1)
                    dve.wait_ge(mask_set, 2)
                for i in range(HEADS + 4):
                    if i < HEADS and s == 0:
                        dve.wait_ge(kT_mm, base + i + 1)
                        ts(heads[:, i, :], bank[1][:, :], gqk[:, 2:3], None, ALU.mult).then_inc(kT_cp, 1)
                    h = i - 1
                    if 0 <= h < HEADS:
                        if s == 0:
                            dve.wait_ge(ss_mm, base + h + 1)
                            ss = bank[6][:, :].rearrange("p (b k) -> p b k", b=CB)[:, :, 0]
                            link(rsqrt(q_rstd[:, h, :], ss, 1.0 / P, 1e-5, CB))
                        dve.wait_ge(s_mm, base + h + 1)
                        sc = bank[2 + h % 2][:, :]
                        if s != 0:
                            link(tt(sc, sc, mask_bias[:, CT * c:CT * (c + 1)], ALU.add))
                        link(nc.vector.tensor_reduce(neg_max[:, h, :], sc.rearrange("p (b k) -> p b k", b=CB), AX,
                                                     ALU.max))
                        if s == 0:
                            stt(neg_max[:, h, :], neg_max[:, h, :], -1.0, q_rstd[:, h, :], ALU.mult, ALU.mult)\
                                .then_inc(nb, 1)
                        else:
                            ts(neg_max[:, h, :], neg_max[:, h, :], -float(P) ** -0.5, None, ALU.mult)\
                                .then_inc(nb, 1)
                    h = i - 2
                    if 0 <= h < HEADS:
                        dve.wait_ge(ex, base + h + 1)
                        if s == 0:
                            nc.vector.reciprocal(row_sum[:, h, :], row_sum[:, h, :]).then_inc(rs, 1)
                        else:
                            link(nc.vector.reciprocal(row_sum[:, h, :], row_sum[:, h, :]))
                            tt(row_sum[:, h, :], row_sum[:, h, :], any_valid[:, CB * c:CB * c + CB], ALU.mult)\
                                .then_inc(rs, 1)
                    h = i - 3
                    if 0 <= h < HEADS:
                        dve.wait_ge(pt_mm, base + h + 1)
                        if h >= 2:
                            dve.wait_ge(ot_mm, base + h - 1)
                        nc.vector.tensor_copy(pt_ring[h % 2], bank[4][:, :]).then_inc(pt_cp, 1)
                    h = i - 4
                    if 0 <= h < HEADS:
                        dve.wait_ge(ot_mm, base + h + 1)
                        nc.vector.tensor_copy(heads[:, h, :], bank[5 + 2 * (h % 2)][:, :]).then_inc(ot_cp, 1)
                    if s == 0 and i < HEADS:
                        k = HEADS * c + i
                        if k < 24:
                            unpack_fp4(k // 2, bool(k % 2))

            def cast_ff2():
                dve.wait_ge(ld["ff2"], 128)
                for k, (lo, hi) in enumerate(((0, 1408), (1408, 2816), (2816, 4352))):
                    v = Bw[:, lo:hi]
                    ts(v, v.bitcast(I32), -128.0, None, ALU.add).then_inc(ff2_cast, 1)

            def route_dve(n):
                k = n - 13
                dve.wait_ge(r_sig, k)
                sg = score[:, :, :].rearrange("p b (g j) -> p (b g) j", j=4)
                m, top2, pair = route[:, 0, :], route[:, 1, 0:16], route[:, 1, 16:32]
                first = True
                for u in range(4):
                    for v in range(u + 1, 4):
                        if first:
                            link(tt(top2, sg[:, :, u], sg[:, :, v], ALU.add))
                        else:
                            link(tt(pair, sg[:, :, u], sg[:, :, v], ALU.add))
                            link(tt(top2, top2, pair, ALU.max))
                        first = False

                def in_top2(dst, v, tie, size, ra, rb):
                    shape = [P, CB, size, size]
                    other, own = v.unsqueeze(2).broadcast_to(shape), v.unsqueeze(3).broadcast_to(shape)
                    link(tt(ra, other, own, ALU.is_equal))
                    link(tt(ra, ra, tie.unsqueeze(1).broadcast_to(shape), ALU.mult))
                    link(tt(rb, other, own, ALU.is_gt))
                    link(tt(ra, ra, rb, ALU.add))
                    link(nc.vector.tensor_reduce(dst, ra, AX, ALU.add))
                    link(ts(dst, dst, 2.0, None, ALU.is_lt))

                gsel = route[:, 2, 0:16].rearrange("p (b g) -> p b g", b=CB)
                in_top2(gsel, top2.rearrange("p (b g) -> p b g", b=CB), tie4, 4,
                        route_a[:, :, 0:4, 0:4], route_b[:, :, 0:4, 0:4])
                masked = m.rearrange("p (b e) -> p b e", b=CB)
                link(tt(m.rearrange("p (g j) -> p g j", j=4), sg,
                        route[:, 2, 0:16].unsqueeze(2).broadcast_to([P, 16, 4]), ALU.mult))
                chosen = route[:, 3, :].rearrange("p (b e) -> p b e", b=CB)
                in_top2(chosen, masked, tie16, 16, route_a, route_b)
                link(tt(chosen, chosen, masked, ALU.mult))
                total = route[:, 4, 0:CB]
                link(nc.vector.tensor_reduce(total, chosen, AX, ALU.add))
                link(ts(total, total, 1e-20, None, ALU.add))
                link(nc.vector.reciprocal(total, total))
                if n == 14:
                    link(nc.vector.memset(comb_tok, 0.0))
                    link(nc.vector.memset(comb_tok[:, :, 16:17], 1.0))
                else:
                    dve.wait_ge(r_tr, 1)
                link(tt(chosen, chosen, total.unsqueeze(2).broadcast_to([P, CB, 16]), ALU.mult))
                part = route[:, 5, 0:32].bitcast(BF16).rearrange("p (b e) -> p b e", b=CB)
                for q in range(3):
                    link(nc.vector.tensor_copy(part, chosen))
                    dst = comb_tok[:, :, 17 * q:17 * q + 16]
                    if q < 2:
                        link(nc.vector.tensor_copy(dst, part))
                        link(tt(chosen, chosen, dst, ALU.subtract))
                    else:
                        nc.vector.tensor_copy(dst, part).then_inc(r_comb, 1)
                dve.wait_ge(r_tr, k)
                nc.vector.tensor_copy(combT, bank[5][:, :]).then_inc(r_combT, 1)

            def ffn(n):
                s = n // 2
                base, tiles = FFN_BASE[n], TILES[s]
                if s == 7:
                    route_dve(n)
                for i, w in enumerate(tiles):
                    dve.wait_ge(g_act, base + i + 1)
                    if i >= 3:
                        dve.wait_ge(d_mm, base - FFN_STAGES_BEFORE[n] + i - 2)
                    up, ga, dst = bank[2 + i % 2][0:w, :], act_ring[i % 2][0:w, :], h_ring[i % 3][0:w, :]
                    if s == 5:
                        o = stt(dst, up, ffn2_scale[0:w, 1, i:i + 1], ga, ALU.mult, ALU.mult)
                    else:
                        o = tt(dst, up, ga, ALU.mult)
                    o.then_inc(h_done, 1)

            def head_norm(v, rows, t, m, eps, w, b, shape):
                width = v.shape[-1]
                mean = newton_wide[:, 0, 0:m]
                rstd = newton_wide[:, 1, 0:m]
                link(nc.vector.tensor_reduce(mean, v, AX, ALU.add))
                link(ts(mean, mean, -1.0 / width, None, ALU.mult))
                link(tt(v, v, mean.unsqueeze(2).broadcast_to([P, m, width]), ALU.add))
                link(tt(t, v, v, ALU.mult))
                link(nc.vector.tensor_reduce(mean, t, AX, ALU.add))
                link(rsqrt(rstd, mean, 1.0 / width, eps, m))
                link(tt(v, v, rstd.unsqueeze(2).broadcast_to([P, m, width]), ALU.mult))
                link(tt(rows, rows, w.broadcast_to(shape), ALU.mult))
                return tt(rows, rows, b.broadcast_to(shape), ALU.add)

            def dca_setup():
                dve.wait_ge(ld["L1rows"], 160)
                dve.wait_ge(dca_mm, 1)
                link(tt(dca_tok, bank[0][:, 0:256], dca_bias[:, 0:256], ALU.add))
                v = dca_tok.rearrange("p (h d) -> p h d", d=16)
                head_norm(v, v, dca_tmp.rearrange("p (h d) -> p h d", d=16), 16, 1e-6,
                          dca_lnw.unsqueeze(1), dca_lnb.unsqueeze(1), [P, 16, 16]).then_inc(dca_norm, 1)
                for b in range(B):
                    dve.wait_ge(dca_mm, b + 2)
                    link(tt(vdca[:, b, :], bank[2 + b % 2][:, 0:256], dca_bias[:, 256:512], ALU.add))
                    v = vdca[:, b, :].rearrange("p (f k) -> p f k", f=2)
                    tt(v, v, dca_mask.unsqueeze(1).broadcast_to([P, 2, P]), ALU.mult).then_inc(dca_ready, 1)
                dve.wait_ge(dca_tr, 1)
                for f in range(2):
                    src = bank[1][:, f * P:(f + 1) * P].rearrange("p (b k) -> p b k", b=B)
                    shape = [P, B, 8, 16]
                    tt(kdca[:, f, :, :, :], src.unsqueeze(2).broadcast_to(shape),
                       head_mask[2].unsqueeze(1).unsqueeze(3).broadcast_to(shape), ALU.mult).then_inc(dca_ready, 1)

            def narrow(n):
                s, c = n // 2, n % 2
                na = NAR[s]
                if n == 4:
                    dca_setup()
                if n == 12:
                    dve.wait_ge(ld["late"], 64)

                def tokens(t):
                    bt = na.batch_base + CB * c + t
                    dve.wait_ge(n_qkv, bt + 1)
                    if bt:
                        dve.wait_ge(n_tr, bt)
                    if bt >= na.batch_base + 2:
                        dve.wait_ge(n_vpad, 2 * (bt - 1))
                    if s == 2:
                        kv = bank[0][:, :].rearrange("p (h z d) -> p h z d", z=2, d=16)
                        bias = kv_bias.rearrange("p (h z d) -> p h z d", z=2, d=16)
                        link(tt(cat[:, 0:256], bank[1][:, 0:256], q_bias, ALU.add))
                        link(tt(cat[:, 256:512].rearrange("p (h d) -> p h d", d=16), kv[:, :, 0, :], bias[:, :, 0, :],
                                ALU.add))
                        tt(v_tok[bt % 2].rearrange("p (h d) -> p h d", d=16), kv[:, :, 1, :], bias[:, :, 1, :],
                           ALU.add).then_inc(n_vtok, 1)
                        v = cat.rearrange("p (h d) -> p h d", d=16)
                        rows = cat.rearrange("p (z h d) -> p z h d", z=2, d=16)
                        head_norm(v, rows, cat2.rearrange("p (h d) -> p h d", d=16), 32, 1e-6,
                                  ln_w.rearrange("p (z d) -> p z d", z=2).unsqueeze(2),
                                  ln_b.rearrange("p (z d) -> p z d", z=2).unsqueeze(2), [P, 2, 16, 16])\
                            .then_inc(n_tok, 1)
                    else:
                        b = CB * c + t
                        nc.vector.tensor_copy(v_tok[bt % 2], bank[0][:, 256:512]).then_inc(n_vtok, 1)
                        for z, src in ((0, bank[1][:, 0:256]), (1, bank[0][:, 0:256])):
                            cols = slice(z * 256, (z + 1) * 256)
                            pairs = src.rearrange("p (h q e) -> p h q e", q=4, e=2)
                            link(tt(cat[:, cols].rearrange("p (h q) -> p h q", q=8),
                                    src.rearrange("p (h q) -> p h q", q=8),
                                    cosx[:, b, :, :].rearrange("p q e -> p (q e)").unsqueeze(1)
                                    .broadcast_to([P, 32, 8]), ALU.mult))
                            dst = cat2[:, cols].rearrange("p (h q e) -> p h q e", q=4, e=2)
                            for e in range(2):
                                link(tt(dst[:, :, :, e], pairs[:, :, :, 1 - e],
                                        sinx[:, b, :, e].unsqueeze(1).broadcast_to([P, 32, 4]), ALU.mult))
                        tt(cat, cat, cat2, ALU.add).then_inc(n_tok, 1)
                    dve.wait_ge(n_tok, bt + 1)

                def spread_k(t, f):
                    bt = na.batch_base + CB * c + t
                    dve.wait_ge(n_qT, bt + 1)
                    if bt > na.batch_base:
                        last = na.group_base + (CB * c + t - 1) * na.n + (f + 1) * na.groups
                        dve.wait_ge(n_s, last)
                    shape = [P, na.heads, na.keys]
                    src = bank[2][:, 256 + f * P:256 + f * P + na.keys]
                    tt(kbd[f][:, 0:na.heads * na.keys].rearrange("p (h k) -> p h k", h=na.heads),
                       src.unsqueeze(1).broadcast_to(shape),
                       head_mask[s].unsqueeze(2).broadcast_to(shape), ALU.mult).then_inc(n_kbd, 1)

                steps = list(na.steps(c))
                tokens(0)
                spread_k(0, 0)
                spread_k(0, 1)
                for i in range(len(steps) + 4):
                    if i < len(steps):
                        t, f, g, k, gi = steps[i]
                        dve.wait_ge(n_s, gi + 1)
                        m, w = (16, 16) if f == "dca" else (4, na.keys)
                        sc = bank[3 + gi % 2][:, 0:m * w].rearrange("p (h k) -> p h k", h=m)
                        top = n_max[:, gi % 4, 0:m]
                        link(nc.vector.tensor_reduce(top, sc, AX, ALU.max))
                        if f == "dca":
                            tt(cat3[:, 0:256].rearrange("p (h k) -> p h k", h=16), sc,
                               top.unsqueeze(2).broadcast_to([P, 16, 16]), ALU.subtract).then_inc(n_nb, 1)
                        else:
                            ts(top, top, -na.scale, None, ALU.mult).then_inc(n_nb, 1)
                    j = i - 1
                    if 0 <= j < len(steps):
                        t, f, g, k, gi = steps[j]
                        dve.wait_ge(n_ex, gi + 1)
                        m = 16 if f == "dca" else 4
                        total = n_sum[:, gi % 4, 0:m]
                        if f == "dca":
                            link(nc.vector.tensor_reduce(
                                total, p_ring[gi % 3][:, 0:256].rearrange("p (h k) -> p h k", h=16), AX, ALU.add))
                        nc.vector.reciprocal(total, total).then_inc(n_rs, 1)
                    if i >= 4 and steps[i - 4][3] == na.n - 1 and steps[i - 4][0] == 1:
                        residual(n, 0)
                    j = i - 2
                    if 0 <= j < len(steps):
                        t, f, g, k, gi = steps[j]
                        dve.wait_ge(n_ptm, gi + 1)
                        if gi >= 2:
                            dve.wait_ge(n_otm, gi - 1)
                        w, m = (P, 256) if f == "dca" else (na.keys, 512)
                        nc.vector.tensor_copy(pt_ring[gi % 2][0:w, 0:m], bank[5][0:w, 0:m]).then_inc(n_ptc, 1)
                    if i < len(steps):
                        t, f, g, k, gi = steps[i]
                        if t + 1 < CB:
                            if k == 0:
                                tokens(t + 1)
                            if k == na.n // 2:
                                spread_k(t + 1, 0)
                            if k == na.n - 1:
                                spread_k(t + 1, 1)

            newton_wide = trig[:, 0:2, :]
            nc.vector.memset(ones[:, :], 1.0).then_inc(ones_set, 1)
            link(nc.vector.memset(fp4_table[:, :], FP4_TABLE))
            dve.wait_ge(ld["x"], 32)
            layer_norm(0)
            dve.wait_ge(ld["rows"], 128)
            link(ts(gqk[:, 2:3], gqk[:, 0:1], gqk[:, 1:2], float(P) ** -0.5, ALU.mult, ALU.mult))
            ang, turns, args = trig[:, 0, :], trig[:, 1, :], trig[:, 2:4, :]
            for half, freq in enumerate((1.0, 0.01)):
                link(ts(ang.rearrange("p (b q e) -> p b q e", b=B, q=2)[:, :, :, half], fside[:, :, :], freq, None,
                        ALU.mult))
            magic = 1.5 * 2.0 ** 23
            link(ts(turns, ang, 1.0 / 6.283185307179586, magic, ALU.mult, ALU.add))
            link(ts(turns, turns, -magic, None, ALU.add))
            link(stt(ang, turns, -6.28125, ang, ALU.mult, ALU.add))
            link(stt(ang, turns, -(6.283185307179586 - 6.28125), ang, ALU.mult, ALU.add))
            link(ts(args[:, 1, :], ang, 1.5707963267948966, None, ALU.add))
            link(ts(turns, args[:, 1, :], 3.1415925, -6.283185307179586, ALU.is_gt, ALU.mult))
            link(tt(args[:, 1, :], args[:, 1, :], turns, ALU.add))
            link(ts(args[:, 1, :], args[:, 1, :], 3.1415925, -3.1415925, ALU.min, ALU.max))
            ts(args[:, 0, :], ang, 3.1415925, -3.1415925, ALU.min, ALU.max).then_inc(trig_arg, 1)
            dve.wait_ge(trig_sin, 1)
            sin = trig[:, 4, :].rearrange("p (b q) -> p b q", b=B)
            cos = trig[:, 5, :].rearrange("p (b q) -> p b q", b=B)
            link(nc.vector.tensor_copy(cosx[:, :, :, 0], cos))
            link(nc.vector.tensor_copy(cosx[:, :, :, 1], cos))
            link(ts(sinx[:, :, :, 0], sin, -1.0, None, ALU.mult))
            link(nc.vector.tensor_copy(sinx[:, :, :, 1], sin))
            dve.wait_ge(tg_ready, 1)
            link(nc.vector.reciprocal(scales8[:, 2:4], scales8[:, 0:2]))
            link(tt(scales8[:, 2:3], scales8[:, 2:3], scales8[:, 3:4], ALU.mult))
            link(tt(scales8[:, 2:3], scales8[:, 2:3], tg[:, 5:6], ALU.mult))
            layer_norm(1)

            FFN_STAGES_BEFORE = {}
            k = 0
            for n in range(STAGES):
                FFN_STAGES_BEFORE[n] = k
                if n // 2 in TILES:
                    k += 1

            for n in range(STAGES):
                kind = KIND[n // 2]
                if n == 4:
                    dve.wait_ge(ld["L1"], 80)
                if kind == WIDE:
                    wide(n)
                elif kind == FFN:
                    if n == 10:
                        cast_ff2()
                    ffn(n)
                elif kind == NARROW:
                    narrow(n)
                if kind == NARROW:
                    residual(n, 1)
                else:
                    residual(n, 0)
                    residual(n, 1)
                if n == 4:
                    flat = w8_raw.rearrange("p k n -> p (k n)")
                    link(quantise(flat, w8_tmp, S[:, 0:512], scales8[:, 1:2]))
                    nc.vector.tensor_copy(w8[:, :, :], w8_raw).then_inc(w8_ready, 1)
                if n + 2 < STAGES:
                    dve.wait_ge(resid_done, 2 * n + 2)
                    layer_norm(n + 2)


def constants(np):
    c = np.zeros((128, 552), np.float32)
    p = np.arange(128)
    c[:, 0:128] = np.eye(128)
    c[:, 128:144] = p[:, None] // 8 == np.arange(16)
    c[:, 144:152] = p[:, None] // 16 == np.arange(8)
    c[:, 152:280] = p[:, None] // 16 == p[None, :] // 16
    for off, size in ((280, 16), (536, 4)):
        e = np.arange(size)
        c[:, off:off + size * size] = (e[None, :] < e[:, None]).reshape(1, -1)
    return c


def kernel(**inputs):
    import numpy as np
    import concourse.bacc as _bacc
    from concourse import mybir as _mybir
    from concourse.bass_utils import run_bass_kernel_spmd as _run

    v = {k: np.asarray(a) for k, a in inputs.items()}

    def by_rows(w, p=128):
        return w.reshape(-1, p, w.shape[-1]).transpose(1, 0, 2).reshape(p, -1)

    def by_pairs(w):
        return np.concatenate([w[:, 0::2], w[:, 1::2]], 1)

    def pad_rows(w, rows):
        return np.concatenate([w, np.zeros((rows - w.shape[0],) + w.shape[1:], w.dtype)], 0)

    def by_heads(w, heads):
        return w.reshape(w.shape[0], heads, -1).transpose(2, 1, 0).reshape(w.shape[1] // heads, -1)

    i = "L0_ffn_"
    host = {
        "consts": constants(np), "x": v["x"], "ctx": v["ctx_1024"], "fside": v["fside_BxSx2_0"],
        "mask": v["mask_BxS2_bf1"].reshape(-1), "g_xattn": v["g_xattn"], "g_ffn": v["g_ffn"],
        "gq": v["L0_xattn_gq"].reshape(128, 1), "gk": v["L0_xattn_gk"].reshape(128, 1),
        "L0_wq": by_rows(v["L0_xattn_Wq"]), "L0_wk": v["L0_xattn_Wk"],
        "L0_wvT": by_heads(v["L0_xattn_Wv"], 16), "L0_wo": by_rows(v["L0_xattn_Wo"]),
        "ff0_gate": by_pairs(v[i + "gate_W_packed"].T), "ff0_gate_s": by_pairs(v[i + "gate_scales"].T),
        "ff0_up": by_pairs(v[i + "up_W_packed"].T), "ff0_up_s": by_pairs(v[i + "up_scales"].T),
        "ff0_down": by_rows(v[i + "down_W_packed"].T), "ff0_down_s": by_rows(v[i + "down_scales"].T, 8),
        "bq": v["L1_xattn_bq"], "bkv": np.concatenate([v["L1_xattn_bk"], v["L1_xattn_bv"]]),
        "bkv_dca": v["L1_xattn_bkv_dca"], "bo": v["L1_xattn_bo"],
        "L1_wq": by_rows(v["L1_xattn_Wq"]),
        "L1_wkv": np.concatenate([v["L1_xattn_Wk"], v["L1_xattn_Wv"]], 1),
        "L1_dca": v["L1_xattn_Wkv_dca"], "L1_wo": by_rows(v["L1_xattn_Wo"]),
        "w8": by_rows(v["L1_ffn_input2"]), "scale": v["L1_ffn_scale"].reshape(1), "scale1": v["L1_ffn_scale1"].reshape(1),
        "L2_wqT": by_heads(v["L2_xattn_Wq"], 16), "L2_wkT": by_heads(v["L2_xattn_Wk"], 8),
        "L2_wvT": by_heads(v["L2_xattn_Wv"], 8), "L2_wo": by_rows(v["L2_xattn_Wo"]),
        "ff2_gate": by_rows(v["L2_ffn_wq_gate"].T), "ff2_up": by_rows(v["L2_ffn_wq_up"].T),
        "ff2_down": by_rows(pad_rows(v["L2_ffn_wq_down"].T, 768)),
        "s_gate": pad_rows(v["L2_ffn_s_gate"], 768).reshape(6, 128).T,
        "s_up": pad_rows(v["L2_ffn_s_up"], 768).reshape(6, 128).T, "s_down": v["L2_ffn_s_down"],
        "L3_wq": by_rows(v["L3_xattn_Wq"]), "L3_wkv": v["L3_xattn_Wkv"], "L3_wo": by_rows(v["L3_xattn_Wout"]),
        "bout": v["L3_xattn_bout"],
        "moe_w1": by_rows(np.concatenate([v["L3_ffn_w1"], v["L3_ffn_sw1"]]).transpose(1, 0, 2).reshape(256, -1)),
        "moe_w2": by_rows(pad_rows(np.concatenate([v["L3_ffn_w2"], v["L3_ffn_sw2"]]).reshape(-1, 256), 3072)),
        "router": by_rows(v["L3_ffn_gate_w"].T),
    }
    for name in ("qn_w", "qn_b", "kn_w", "kn_b", "kn_dca_w", "kn_dca_b"):
        host[name] = v["L1_xattn_" + name]

    nc = _bacc.Bacc("TRN2", target_bir_lowering=False, num_devices=1)
    arrays, dram = {}, {}
    for name, a in host.items():
        a = np.ascontiguousarray(a)
        arrays["in_" + name] = a
        dram[name] = nc.dram_tensor("in_" + name, a.shape, _mybir.dt.from_np(a.dtype), kind="ExternalInput").ap()
    out = nc.dram_tensor("out_x", (8, 128, 256), _mybir.dt.float32, kind="ExternalOutput").ap()
    build(nc, dram, out)
    r = _run(nc, [arrays], core_ids=[0])
    return r.results[0]["out_x"]
```

```python
from contextlib import ExitStack

import concourse.bass as bass
from concourse import mybir

F32 = mybir.dt.float32
F32R = mybir.dt.float32r
BF16 = mybir.dt.bfloat16
I32 = mybir.dt.int32
U32 = mybir.dt.uint32
U8 = mybir.dt.uint8
ALU = mybir.AluOpType
ACT = mybir.ActivationFunctionType
AX = mybir.AxisListType.X

P = 128
B = 8
CB = 4
CT = CB * P
D = 256
STAGES = 16
WIDE, FFN, NARROW, FP8 = "wide", "ffn", "narrow", "fp8"
KIND = [WIDE, FFN, NARROW, FP8, WIDE, FFN, NARROW, FFN]
HEADS = 16
MOE_H = 176
EXPERTS = 16
MOE_ALL = (EXPERTS + 1) * MOE_H
HID2 = 704
NEG = 1e30
RSQRT_SEED = float(0x5F3759DF)


def tile_sizes(total):
    return [min(P, total - i) for i in range(0, total, P)]


TILES = {1: tile_sizes(2048), 5: tile_sizes(HID2), 7: tile_sizes(MOE_ALL)}
FFN_BASE = {n: sum(len(TILES[m // 2]) for m in range(n) if m // 2 in TILES) for n in range(STAGES)}
DOWN_BASE = {n: FFN_BASE[n] - sum(m // 2 in TILES for m in range(n)) for n in range(STAGES)}


TURN_LAG, OUT_LAG = 4, 5


class Narrow:

    def __init__(self, s):
        self.s = s
        self.hd = 16 if s == 2 else 8
        self.heads = P // self.hd
        self.keys = 112 if s == 2 else 128
        self.scale = float(self.hd) ** -0.5
        self.groups = self.heads // 4
        order = [(f, g) for f in range(2) for g in range(self.groups)]
        self.order = order + [("dca", 0)] * (s == 2)
        self.n = len(self.order)
        self.q_step = 3
        self.batch_base = 0 if s == 2 else B
        self.group_base = 0 if s == 2 else 5 * B
        mid, late = CB * self.n // 2, CB * self.n + 3 * self.n
        self.turn_steps = {mid: (1, 0), mid + 2: (1, 1), late: (2, 0), late + 2: (2, 1)}

    def turned_copy(self, gi):
        if gi < 5 * B:
            return "scalar", gi + 1
        gi -= 5 * B
        return ("scalar", 5 * B + gi // 2 + 1) if gi % 2 else ("vector", gi // 2 + 1)

    def spread(self, t, f):
        if self.s == 2:
            return "gpsimd", 2 * t + f + 1
        return ("gpsimd", 2 * B + t + 1) if f else ("vector", t + 1)

    def steps(self):
        for t in range(B):
            for k, (f, g) in enumerate(self.order):
                yield t, f, g, k, self.group_base + t * self.n + k


DOWN_LAG = 2
MOE_LEAD, MOE_DOWN_LAG = 8, 3
MOE_TILES = len(TILES[7])


def build(nc, dram, out):
    with ExitStack() as ctx:
        def sb(name, shape, dt=F32):
            return ctx.enter_context(nc.sbuf_tensor(name, shape, dt))

        sems = {}

        def sem(name):
            sems[name] = ctx.enter_context(nc.semaphore(name))
            return sems[name]

        bank = [ctx.enter_context(nc.psum_tensor(f"bank{i}", [P, 512], F32)) for i in range(8)]

        consts = sb("consts", [P, 552])
        ident = consts[:, 0:128]
        head_mask = {6: consts[:, 128:144], 2: consts[:, 144:152]}
        dca_mask = consts[:, 152:280]
        tie16 = consts[:, 280:536].rearrange("p (e j) -> p e j", e=16)
        tie4 = consts[:, 536:552].rearrange("p (e j) -> p e j", e=4)
        ones = sb("ones", [P, P])
        x_sb = sb("x_sb", [P, B, D])
        xn = sb("xn", [P, 2, CB, D])
        xT = sb("xT", [P, 2, 2, CT])
        xqT = sb("xqT", [P, 2, CT], BF16)
        w8 = sb("w8", [P, 2, D], BF16)
        ctx_tok = sb("ctx_tok", [P, B, P])
        ctxT = sb("ctxT", [P, B, P])
        mask8 = sb("mask8", [P, B * P], U8)
        gates = sb("gates", [P, 8])
        tg = sb("tg", [P, 8])
        scales8 = sb("scales8", [P, 4])
        gqk = sb("gqk", [P, 3])
        fside = sb("fside", [P, B, 2])
        trig = sb("trig", [P, 6, B * 4])
        cosx = sb("cosx", [P, B, 4, 2])
        sinx = sb("sinx", [P, B, 4, 2])
        ffn2_scale = sb("ffn2_scale", [P, 2, 6])
        stats = sb("stats", [P, CB, 6])
        mv = sb("mv", [P, CB, 2])
        x_rstd = sb("x_rstd", [P, CB])
        newton = sb("newton", [P, 3, 64])
        q_rstd = sb("q_rstd", [P, HEADS, CB])
        neg_max = sb("neg_max", [P, HEADS, CB])
        row_sum = sb("row_sum", [P, HEADS, CB])
        k_ss = sb("k_ss", [P, HEADS, CB])
        any_valid = sb("any_valid", [P, B])
        n_max = sb("n_max", [P, 6, 16])
        n_sum = sb("n_sum", [P, 6, 16])
        score = sb("score", [P, CB, 16])
        route = sb("route", [P, 8, CB * 16])

        sizes = {"A": 10240, "Bw": 12288, "H": 8192, "S": 5120, "R": 4608, "X": 1024}
        with ExitStack() as regions:
            A, Bw, H, S, R, X = (regions.enter_context(nc.sbuf_tensor(name, [P, cols], F32))
                                 for name, cols in sizes.items())
        A_r, Bw_r, H_r, S_r, _, X_r = (sb(name + "_r", [P, cols], F32R) for name, cols in sizes.items())

        def ring(region, off, n, cols=512):
            return [region[:, off + i * cols:off + (i + 1) * cols] for i in range(n)]

        def split(ap, pattern, **kw):
            return ap.rearrange(pattern, **kw)

        q_ring, q2_ring, p_ring, pt_ring = ring(S, 0, 2), ring(S, 1024, 2), ring(S, 2048, 4), ring(S, 4096, 2)
        heads = split(H[:, :], "p (h t) -> p h t", h=HEADS)
        L0_wq = split(A[:, 0:4096], "p (f n) -> p f n", f=2)
        L0_wk = A[:, 4096:6144]
        out_w = {0: split(A[:, 6144:10240], "p (h n) -> p h n", h=HEADS),
                 4: split(A[:, 4096:8192], "p (h n) -> p h n", h=HEADS)}
        L0_wvT = split(Bw[:, 6144:8192], "p (h n) -> p h n", h=HEADS)
        L0_wo = split(Bw[:, 8192:12288], "p (h n) -> p h n", h=HEADS)
        L2_m = split(A[:, 0:4096], "p (f h n) -> p f h n", f=2, h=HEADS)
        L2_wqT = split(Bw[:, 0:4096], "p (h n) -> p h n", h=HEADS)
        L2_wkT = split(Bw[:, 4096:5120], "p (h n) -> p h n", h=8)
        L2_wvT = split(Bw[:, 5120:6144], "p (h n) -> p h n", h=8)
        L2_wo = split(Bw[:, 6144:10240], "p (h n) -> p h n", h=HEADS)
        mask_bias = R[:, 0:1024]
        h_ring = ring(S, 1024, 3)
        act_ring = ring(S, 0, 2)
        ff0 = [split(Bw[:, 4096 * i:4096 * (i + 1)], "p (k n) -> p k n", k=2) for i in range(3)]
        ff_gate = {1: ff0[0], 5: split(Bw[:, 0:1408], "p (k n) -> p k n", k=2)}
        ff_up = {1: ff0[1], 5: split(Bw[:, 1408:2816], "p (k n) -> p k n", k=2)}
        ff_down = {1: split(Bw[:, 8192:12288], "p (m n) -> p m n", n=D),
                   5: split(Bw[:, 2816:4352], "p (m n) -> p m n", n=D)}
        down_scale = R[:, 1024:1280]
        fp4_slot = [(R[:, 1024 * i:1024 * i + 512].bitcast(U32), R[:, 1024 * i + 512:1024 * i + 1024]) for i in range(3)]
        fp4_tmp = ring(R, 3072, 2)
        nq = {2: split(A[:, 0:512], "p (k n) -> p k n", k=2), 6: split(Bw[:, 4352:4864], "p (k n) -> p k n", k=2)}
        nkv = {2: A[:, 512:1024], 6: Bw[:, 4864:5376]}
        nout = {2: split(A[:, 1536:2048], "p (k n) -> p k n", k=2), 6: split(Bw[:, 5376:5888], "p (k n) -> p k n", k=2)}
        dca_w = A[:, 1024:1536]
        kdca = split(A[:, 2048:4096], "p (f b h k) -> p f b h k", f=2, b=B, h=8)
        vdca = split(A[:, 4096:6144], "p (b n) -> p b n", b=B)
        kT_all = split(A[:, 6144:8192], "p (b f k) -> p b f k", b=B, f=2)
        v_all = split(A[:, 8192:10240], "p (b n) -> p b n", b=B)
        w8_raw = split(H[:, 0:512], "p (k n) -> p k n", k=2)
        w8_tmp, q8_tmp = ring(H, 512, 2), ring(Bw, 10240, 2, 1024)
        dca_tok, dca_tmp = H[:, 1536:1792], H[:, 1792:2048]
        dca_ctx = H[:, 2048:2176]
        dca_ctx8 = split(H[:, 2176:3200], "p (b k) -> p b k", b=B)
        k_tok, k_tmp = H[:, 3200:3456], H[:, 3456:3712]
        q_bias, kv_bias = R[:, 0:256], R[:, 256:768]
        dca_bias = R[:, 768:1280]
        ln_w, ln_b = R[:, 1280:1312], R[:, 1312:1344]
        dca_lnw, dca_lnb = R[:, 1344:1360], R[:, 1360:1376]
        out_bias = {2: R[:, 1376:1632], 6: R[:, 1280:1536]}
        q_tok, q_tmp, dca_diff = S[:, 0:256], S[:, 512:768], S[:, 1024:1280]
        np_ring, npt_ring = ring(S, 2048, 6), ring(R, 3072, 2)
        nqT = ring(X, 0, 2, 256)
        n_out = X[:, 512:768]
        kbd = [H[:, 2048 * f:2048 * (f + 1)] for f in range(2)]
        vpad = [H[:, 4096 + 2048 * f:4096 + 2048 * (f + 1)] for f in range(2)]
        w1_cols, w2_at = 2 * MOE_ALL, 2 * MOE_ALL + 32
        moe_w1, w1_lo, w1_hi = (split(t[:, 0:w1_cols], "p (k n) -> p k n", k=2) for t in (A, A_r, Bw_r))
        router_w = split(Bw[:, w1_cols:w2_at], "p (k n) -> p k n", k=2)
        moe_w2, w2_lo = (split(t[:, w2_at:w2_at + D * MOE_TILES], "p (m n) -> p m n", n=D) for t in (Bw, Bw_r))

        def w2_high(a, h, m):
            return a[:, w1_cols + D * m:w1_cols + D * (m + 1)] if m < 16 else h[:, D * (m + 4):D * (m + 5)]

        moe_act = ring(H, 0, 10)
        moe_h, h_lo_ring, h_hi_ring = ring(S, 1024, 4), ring(S_r, 1024, 4), ring(S_r, 3072, 4)
        x_hi, x_lo = (split(t[:, 0:1024], "p (f t) -> p f t", f=2) for t in (S_r, X_r))
        yT = ring(R, 0, 2)
        sel = R[:, 1536:1536 + MOE_ALL // 2].bitcast(BF16)
        comb_tok = split(R[:, 3072:3584], "p (b e) -> p b e", b=CB)
        combT = R[:, 3584:3840].bitcast(BF16)
        route_a = split(S[:, 3072:4096], "p (b e j) -> p b e j", b=CB, e=16)
        route_b = split(S[:, 4096:5120], "p (b e j) -> p b e j", b=CB, e=16)

        ld = {k: sem("ld_" + k) for k in (
            "const", "x", "x1", "ctx", "rows", "wq0", "wk0", "wvo0", "fp4_0", "fp4_1", "fp4_2", "L1", "L1rows",
            "L2", "late", "ff2", "moe1")}
        v_chain, tg_ready = sem("v_chain"), sem("tg_ready")
        ones_set, sel_chain, ctxT_mm, ctxT_cp, trig_arg, trig_sin = (
            sem("ones_set"), sem("sel_chain"), sem("ctxT_mm"), sem("ctxT_cp"), sem("trig_arg"), sem("trig_sin"))
        pre_mm, pre_cp = sem("pre_mm"), sem("pre_cp")
        fp4_done, ff2_cast, w8_ready = sem("fp4_done"), sem("ff2_cast"), sem("w8_ready")
        ln_done, xT_mm, xT_cp = sem("ln_done"), sem("xT_mm"), sem("xT_cp")
        y_ready, resid_done, stored = sem("y_ready"), sem("resid_done"), sem("stored")
        k_mm, k_sq, k_cp, k_red, k_rstd, k_scaled_v, k_scaled_g, kT_mm, kT_cp = (
            sem("k_mm"), sem("k_sq"), sem("k_cp"), sem("k_red"), sem("k_rstd"), sem("k_scaled_v"),
            sem("k_scaled_g"), sem("kT_mm"), sem("kT_cp"))
        q_mm, q_cp, q_sq, ss_mm, s_mm, nb, ex, rs, p_norm, pt_mm, pt_cp, ot_mm, ot_cp = (
            sem("q_mm"), sem("q_cp"), sem("q_sq"), sem("ss_mm"), sem("s_mm"), sem("nb"), sem("ex"), sem("rs"),
            sem("p_norm"), sem("pt_mm"), sem("pt_cp"), sem("ot_mm"), sem("ot_cp"))
        mask_set, gqk_set, ss_read = sem("mask_set"), sem("gqk_set"), sem("ss_read")
        g_mm, u_mm, g_act, h_done, d_mm = sem("g_mm"), sem("u_mm"), sem("g_act"), sem("h_done"), sem("d_mm")
        c_kv, c_tok, c_v, c_tr, c_kT = sem("c_kv"), sem("c_tok"), sem("c_v"), sem("c_tr"), sem("c_kT")
        (n_q, n_tok, n_tr, n_qT, n_kbd_v, n_kbd_g, n_vpad, n_s, n_nb, n_ex, n_rs, n_pn, n_ptm, n_ptc_v, n_ptc_a,
         n_otm, n_otc, vpad_zero) = (
            sem("n_q"), sem("n_tok"), sem("n_tr"), sem("n_qT"), sem("n_kbd_v"), sem("n_kbd_g"), sem("n_vpad"),
            sem("n_s"), sem("n_nb"), sem("n_ex"), sem("n_rs"), sem("n_pn"), sem("n_ptm"), sem("n_ptc_v"),
            sem("n_ptc_a"), sem("n_otm"), sem("n_otc"), sem("vpad_zero"))
        dca_copied = sem("dca_copied")
        dca_mm, dca_tr, dca_norm, dca_ready = sem("dca_mm"), sem("dca_tr"), sem("dca_norm"), sem("dca_ready")
        x_high, x_low, w_high, w_low, h_high, h_low, moe_d, yT_act, yT_dve = (
            sem("x_high"), sem("x_low"), sem("w_high"), sem("w_low"), sem("h_high"), sem("h_low"), sem("moe_d"),
            sem("yT_act"), sem("yT_dve"))
        r_mm, r_sig, r_comb, r_tr, r_combT = (
            sem("r_mm"), sem("r_sig"), sem("r_comb"), sem("r_tr"), sem("r_combT"))

        NAR = {s: Narrow(s) for s in (2, 6)}

        def turn_bank(n, f):
            if n == 0 or KIND[(n - 1) // 2] in (WIDE, FP8):
                return f
            if KIND[(n - 1) // 2] == NARROW:
                return 2
            return 4 + f
        DCA_V_STEPS = [3, 4, 6, 7, 9, 10, 12, 13]
        WIDE_INDEX = {0: 0, 1: 1, 8: 2, 9: 3}

        block = ctx.enter_context(nc.Block())

        @block.sync
        def _(sp):
            def load(dst, src, what):
                sp.dma_start(dst, src).then_inc(ld[what], 16)

            load(consts[:, :], dram["consts"], "const")
            load(ctx_tok[:, :, :], dram["ctx"].rearrange("b p d -> p b d"), "ctx")
            load(x_sb[:, 0:CB, :], dram["x"][0:CB].rearrange("b p d -> p b d"), "x")
            load(L0_wk, dram["L0_wk"], "wk0")
            load(A[:, 0:4096], dram["L0_wq"], "wq0")
            load(gates[:, 0:4], dram["g_xattn"].partition_broadcast(P), "rows")
            load(gates[:, 4:8], dram["g_ffn"].partition_broadcast(P), "rows")
            load(gqk[:, 0:1], dram["gq"], "rows")
            load(gqk[:, 1:2], dram["gk"], "rows")
            load(mask8[:, :], dram["mask"].partition_broadcast(P), "rows")
            load(fside[:, :, :], dram["fside"].rearrange("b p d -> p b d"), "rows")
            load(scales8[:, 0:1], dram["scale"].partition_broadcast(P), "rows")
            load(scales8[:, 1:2], dram["scale1"].partition_broadcast(P), "rows")
            load(Bw[:, 6144:8192], dram["L0_wvT"], "wvo0")
            load(Bw[:, 8192:12288], dram["L0_wo"], "wvo0")
            load(x_sb[:, CB:B, :], dram["x"][CB:B].rearrange("b p d -> p b d"), "x1")
            for p in range(12):
                if p >= 3:
                    sp.wait_ge(fp4_done, 2 * (p - 2))
                name, cols = ("gate", "up", "down")[p // 4], slice(512 * (p % 4), 512 * (p % 4) + 512)
                packed, scale = fp4_slot[p % 3]
                load(packed.bitcast(I32), dram[f"ff0_{name}"][:, cols], f"fp4_{p % 3}")
                load(scale,
                     dram[f"ff0_{name}_s"][:, cols].unsqueeze(1).broadcast_to([8, 16, 512]), f"fp4_{p % 3}")
            sp.wait_ge(fp4_done, 24)
            for dst, name in ((q_bias, "bq"), (kv_bias, "bkv"), (dca_bias, "bkv_dca"), (ln_w[:, 0:16], "qn_w"),
                              (ln_w[:, 16:32], "kn_w"), (ln_b[:, 0:16], "qn_b"), (ln_b[:, 16:32], "kn_b"),
                              (dca_lnw, "kn_dca_w"), (dca_lnb, "kn_dca_b"), (out_bias[2], "bo")):
                load(dst, dram[name].partition_broadcast(P), "L1rows")
            sp.wait_ge(y_ready, 4)
            load(A[:, 0:512], dram["L1_wq"], "L1")
            load(A[:, 512:1024], dram["L1_wkv"], "L1")
            load(A[:, 1024:1536], dram["L1_dca"], "L1")
            load(A[:, 1536:2048], dram["L1_wo"], "L1")
            load(H[:, 0:512], dram["w8"], "L1")
            sp.wait_ge(y_ready, 8)
            load(Bw[:, 0:4096], dram["L2_wqT"], "L2")
            load(Bw[:, 4096:5120], dram["L2_wkT"], "L2")
            load(Bw[:, 5120:6144], dram["L2_wvT"], "L2")
            load(Bw[:, 6144:10240], dram["L2_wo"], "L2")
            sp.wait_ge(resid_done, 12)
            load(down_scale, dram["s_down"].partition_broadcast(P), "late")
            load(out_bias[6], dram["bout"].partition_broadcast(P), "late")
            load(ffn2_scale[:, 0, :], dram["s_gate"], "late")
            load(ffn2_scale[:, 1, :], dram["s_up"], "late")
            sp.wait_ge(pre_mm, 24)
            sp.wait_ge(ln_done, 8)
            load(Bw[:, 0:1408].bitcast(I32), dram["ff2_gate"], "ff2")
            load(Bw[:, 1408:2816].bitcast(I32), dram["ff2_up"], "ff2")
            load(Bw[:, 2816:4352].bitcast(I32), dram["ff2_down"], "ff2")
            load(Bw[:, 4352:4864], dram["L3_wq"], "ff2")
            load(Bw[:, 4864:5376], dram["L3_wkv"], "ff2")
            load(Bw[:, 5376:5888], dram["L3_wo"], "ff2")
            load(Bw[:, w2_at:w2_at + D * MOE_TILES], dram["moe_w2"], "ff2")
            load(Bw[:, w1_cols:w2_at], dram["router"], "ff2")
            sp.wait_ge(y_ready, 20)
            load(A[:, 0:w1_cols], dram["moe_w1"], "moe1")
            for c in range(2):
                for j in range(2):
                    sp.wait_ge(resid_done, 2 * (14 + c) + j + 1)
                    b = CB * c + 2 * j
                    sp.dma_start(out[b:b + 2].rearrange("b p d -> p b d"), x_sb[:, b:b + 2, :]).then_inc(stored, 16)
            sp.wait_ge(stored, 64)

        @block.tensor
        def _(pe):
            def transpose_x(n, f):
                c = n % 2
                pe.wait_ge(ln_done, n + 1)
                for b in range(CB):
                    src = xn[:, c, b, f::2] if n // 2 == 1 else xn[:, c, b, f * P:(f + 1) * P]
                    mm = nc.tensor.transpose(bank[turn_bank(n, f)][:, b * P:(b + 1) * P], src, ident)
                mm.then_inc(xT_mm, 1)

            def keys0(a, b):
                for g in range(4):
                    u = 4 * b + g
                    if u >= 2:
                        pe.wait_ge(k_cp, 16 * a + u - 1)
                    nc.tensor.matmul(bank[2 + u % 2][:, :], ctxT[:, CB * a + b, :], L0_wk[:, 512 * g:512 * g + 512],
                                     start=True, stop=True).then_inc(k_mm, 1)

            def weight_products(which):
                units = [("n", i) for i in range(8)] if which == 0 else [("m", i) for i in range(8)] + [("n", i) for i in range(8)]
                base = 0 if which == 0 else 8
                for u, (kind, i) in enumerate(units):
                    if base + u >= 4:
                        pe.wait_ge(pre_cp, base + u - 3)
                    dst = bank[2 + (base + u) % 4]
                    for j in range(2):
                        h = 2 * i + j
                        if kind == "n":
                            wv = L0_wvT[:, h, :] if which == 0 else L2_wvT[:, h // 2, :]
                            wo = L0_wo[:, h, :] if which == 0 else L2_wo[:, h, :]
                            mm = nc.tensor.matmul(dst[:, j * 256:(j + 1) * 256], wv, wo, start=True, stop=True)
                        else:
                            for f in range(2):
                                mm = nc.tensor.matmul(dst[:, f * 256 + j * 128:f * 256 + (j + 1) * 128],
                                                      L2_wqT[:, h, f * P:(f + 1) * P], L2_wkT[:, h // 2, :],
                                                      start=True, stop=True)
                    mm.then_inc(pre_mm, 1)

            def wide(n):
                a, c, s = WIDE_INDEX[n], n % 2, n // 2
                base = HEADS * a
                if s == 0:
                    if a == 0:
                        pe.wait_ge(ld["wk0"], 16)
                        for b in range(CB):
                            keys0(0, b)
                        for f in range(2):
                            transpose_x(0, f)
                        pe.wait_ge(ld["wvo0"], 32)
                        pe.wait_ge(k_cp, 16)
                        weight_products(0)
                        pe.wait_ge(ones_set, 1)
                        pe.wait_ge(pre_cp, 8)
                        pe.wait_ge(ld["wq0"], 16)
                    pe.wait_ge(k_cp, 16 * a + 16)
                else:
                    pe.wait_ge(pre_cp, 24)
                pe.wait_ge(xT_cp, 2 * n + 2)

                def outputs(batches, some_heads):
                    for b in batches:
                        for h in some_heads:
                            mm = nc.tensor.matmul(bank[6 + b // 2][:, (b % 2) * D:(b % 2 + 1) * D],
                                                  heads[:, h, b * P:(b + 1) * P], out_w[s][:, h, :],
                                                  start=(h == 0 and b % 2 == 0), stop=(h == HEADS - 1),
                                                  skip_group_check=True)
                    return mm

                for i in range(HEADS + 4):
                    if i < HEADS:
                        if i:
                            pe.wait_ge(q_sq if s == 0 else q_cp, base + i)
                        for f in range(2):
                            w = L0_wq[:, f, i * P:(i + 1) * P] if s == 0 else L2_m[:, f, i, :]
                            mm = nc.tensor.matmul(bank[0][:, :], w, xT[:, c, f, :], start=(f == 0), stop=(f == 1))
                        mm.then_inc(q_mm, 1)
                        if s == 0:
                            pe.wait_ge(k_scaled_g if i % 2 else k_scaled_v, 8 * a + i // 2 + 1)
                            if i:
                                pe.wait_ge(kT_cp, base + i)
                            for b in range(CB):
                                mm = nc.tensor.transpose(bank[1][:, b * P:(b + 1) * P],
                                                         heads[:, i, b * P:(b + 1) * P], ident)
                            mm.then_inc(kT_mm, 1)
                    h = i - 1
                    if 0 <= h < HEADS:
                        qT = q_ring[h % 2]
                        if s == 0:
                            pe.wait_ge(q_sq, base + h + 1)
                            if h == 0:
                                pe.wait_ge(resid_done, 2 * n)
                            else:
                                pe.wait_ge(ss_read, base + h)
                            for b in range(CB):
                                mm = nc.tensor.matmul(bank[6][:, b * P:(b + 1) * P],
                                                      q2_ring[h % 2][:, b * P:(b + 1) * P], ones[:, :],
                                                      start=True, stop=True)
                            mm.then_inc(ss_mm, 1)
                            pe.wait_ge(kT_cp, base + h + 1)
                        else:
                            pe.wait_ge(q_cp, base + h + 1)
                        if h >= 2:
                            pe.wait_ge(ex, base + h - 1)
                        for b in range(CB):
                            keys = heads[:, h, b * P:(b + 1) * P] if s == 0 else ctxT[:, CB * c + b, :]
                            mm = nc.tensor.matmul(bank[2 + h % 2][:, b * P:(b + 1) * P], qT[:, b * P:(b + 1) * P],
                                                  keys, start=True, stop=True)
                        mm.then_inc(s_mm, 1)
                    if i > HEADS:
                        if i == HEADS + 1:
                            if s == 0:
                                pe.wait_ge(ss_read, base + HEADS)
                            pe.wait_ge(ot_cp, base + 12)
                        outputs(range(2), range(4 * (i - HEADS - 1), 4 * (i - HEADS)))
                    h = i - 3
                    if 0 <= h < HEADS:
                        pe.wait_ge(p_norm, base + h + 1)
                        if h:
                            pe.wait_ge(pt_cp, base + h)
                        for b in range(CB):
                            mm = nc.tensor.transpose(bank[4][:, b * P:(b + 1) * P],
                                                     p_ring[h % 4][:, b * P:(b + 1) * P], ident)
                        mm.then_inc(pt_mm, 1)
                    h = i - 4
                    if 0 <= h < HEADS:
                        pe.wait_ge(pt_cp, base + h + 1)
                        if h == 0:
                            pe.wait_ge(resid_done, 2 * n)
                        if h >= 2:
                            pe.wait_ge(ot_cp, base + h - 1)
                        for b in range(CB):
                            mm = nc.tensor.matmul(bank[5 + 2 * (h % 2)][:, b * P:(b + 1) * P],
                                                  ctx_tok[:, CB * c + b, :], pt_ring[h % 2][:, b * P:(b + 1) * P],
                                                  start=True, stop=True)
                        mm.then_inc(ot_mm, 1)
                for f in range(2):
                    transpose_x(n + 1, f)
                pe.wait_ge(ot_cp, base + HEADS)
                for b in range(CB):
                    mm = outputs([b], range(12 if b < 2 else 0, HEADS))
                    if b % 2:
                        mm.then_inc(y_ready, 1)
                    if n == 0:
                        keys0(1, b)

            def context(n, i):
                s, c = n // 2 + 1, n % 2
                na = NAR[s]
                first, every = (2, 3) if s == 2 else (0, 1)
                j = (i - first) // every
                if (i - first) % every or not 0 <= j <= CB:
                    return
                bt = na.batch_base + CB * c + j
                if j:
                    pe.wait_ge(c_tok, bt)
                    if bt >= 2:
                        pe.wait_ge(c_kT, bt - 1)
                    if s == 2:
                        pe.wait_ge(dca_ready, B + 2 if c else 2 * j)
                    for f in range(2):
                        mm = nc.tensor.transpose(bank[5][:, f * P:(f + 1) * P], k_tok[:, f * P:(f + 1) * P], ident)
                    mm.then_inc(c_tr, 1)
                if j < CB:
                    if bt == na.batch_base:
                        pe.wait_ge(ld["L1"] if s == 2 else ld["ff2"], 80 if s == 2 else 128)
                    if bt:
                        pe.wait_ge(c_v, bt)
                    if c and j == 0:
                        pe.wait_ge(xT_cp, 2 * n + 2)
                    nc.tensor.matmul(bank[4][:, :], ctxT[:, CB * c + j, :], nkv[s], start=True, stop=True)\
                        .then_inc(c_kv, 1)

            def dca(n, i):
                if n == 2 and i in DCA_V_STEPS:
                    b = DCA_V_STEPS.index(i)
                    if b == 0:
                        pe.wait_ge(ld["L1"], 80)
                        pe.wait_ge(dca_copied, 2)
                    else:
                        pe.wait_ge(dca_ready, b)
                    if b >= 2:
                        pe.wait_ge(c_kT, b // 2)
                    nc.tensor.matmul(bank[5][:, 0:256], dca_ctx8[:, b, :], dca_w[:, 256:512],
                                     start=True, stop=True).then_inc(dca_mm, 1)
                if n == 3 and i == 0:
                    pe.wait_ge(xT_cp, 8)
                    nc.tensor.matmul(bank[5][:, 0:256], dca_ctx, dca_w[:, 0:256], start=True, stop=True)\
                        .then_inc(dca_mm, 1)
                if n == 3 and i == 4:
                    pe.wait_ge(dca_norm, 1)
                    for f in range(2):
                        mm = nc.tensor.transpose(bank[5][:, f * P:(f + 1) * P], dca_tok[:, f * P:(f + 1) * P], ident)
                    mm.then_inc(dca_tr, 1)

            def project(n, t):
                bt = NAR[n // 2].batch_base + t
                if bt:
                    pe.wait_ge(n_tok, bt)
                if t % CB == 0:
                    pe.wait_ge(xT_cp, 2 * n + 2 + 2 * (t // CB))
                for f in range(2):
                    mm = nc.tensor.matmul(bank[1][:, 0:256], xT[:, t // CB, f, (t % CB) * P:(t % CB + 1) * P],
                                          nq[n // 2][:, f, :], start=(f == 0), stop=(f == 1))
                mm.then_inc(n_q, 1)

            def ffn(n):
                s, c = n // 2, n % 2
                base, tiles = FFN_BASE[n], TILES[s]
                if s == 1:
                    pe.wait_ge(fp4_done, 24)
                else:
                    pe.wait_ge(ff2_cast, 3)
                pe.wait_ge(xT_cp, 2 * n + 2)
                size = len(tiles)
                for i in range(size + DOWN_LAG):
                    if i < size:
                        w = tiles[i]
                        if i >= 2:
                            pe.wait_ge(g_act, base + i - 1)
                        for f in range(2):
                            mm = nc.tensor.matmul(bank[i % 2][0:w, :], ff_gate[s][:, f, i * P:i * P + w],
                                                  xT[:, c, f, :], start=(f == 0), stop=(f == 1))
                        mm.then_inc(g_mm, 1)
                        if i >= 2:
                            pe.wait_ge(h_done, base + i - 1)
                        for f in range(2):
                            mm = nc.tensor.matmul(bank[2 + i % 2][0:w, :], ff_up[s][:, f, i * P:i * P + w],
                                                  xT[:, c, f, :], start=(f == 0), stop=(f == 1))
                        mm.then_inc(u_mm, 1)
                    if s == 1:
                        dca(n, i)
                    context(n, i)
                    if i == size:
                        pe.wait_ge(c_v, NAR[s + 1].batch_base + CB * c + CB)
                        pe.wait_ge(c_kT, NAR[s + 1].batch_base + CB * c + CB)
                        for f in range(2):
                            transpose_x(n + 1, f)
                    m = i - DOWN_LAG
                    if m == size - 1 and c:
                        project(n + 1, 0)
                    if m >= 0:
                        w = tiles[m]
                        pe.wait_ge(h_done, base + m + 1)
                        if m == 0:
                            pe.wait_ge(resid_done, 2 * n)
                        for b in range(CB):
                            mm = nc.tensor.matmul(bank[6 + b // 2][:, (b % 2) * D:(b % 2 + 1) * D],
                                                  h_ring[m % 3][0:w, b * P:(b + 1) * P], ff_down[s][0:w, m, :],
                                                  start=(m == 0 and b % 2 == 0), stop=(m == size - 1),
                                                  skip_group_check=True)
                            if m == size - 1 and b % 2:
                                mm.then_inc(y_ready, 1)
                            elif m < size - 1 and b == CB - 1:
                                mm.then_inc(d_mm, 1)

            def moe(n):
                c, k, base, tiles = n % 2, n - 14, FFN_BASE[n], TILES[7]
                size = MOE_TILES
                pe.wait_ge(ld["ff2"], 128)
                pe.wait_ge(xT_cp, 2 * n + 2)
                for b in range(CB):
                    for f in range(2):
                        mm = nc.tensor.matmul(bank[2][:, b * 16:(b + 1) * 16], xT[:, c, f, b * P:(b + 1) * P],
                                              router_w[:, f, :], start=(f == 0), stop=(f == 1))
                mm.then_inc(r_mm, 1)
                for i in range(size + MOE_LEAD + MOE_DOWN_LAG):
                    if i < size:
                        w = tiles[i]
                        if i == 0:
                            pe.wait_ge(x_low, k + 1)
                        pe.wait_ge(w_low, i + 1)
                        if i >= 2:
                            pe.wait_ge(g_act, base + i - 1)
                        for f in range(2):
                            cols = slice(i * P, i * P + w)
                            for q, (weights, x) in enumerate(((w1_hi, x_hi), (w1_lo, x_hi), (w1_hi, x_lo))):
                                mm = nc.tensor.matmul(bank[i % 2][0:w, :], weights[:, f, cols], x[:, f, :],
                                                      start=(f == 0 and q == 0), stop=(f == 1 and q == 2))
                        mm.then_inc(g_mm, 1)
                    m = i - MOE_LEAD
                    if 0 <= m < size:
                        w = tiles[m]
                        if m == 0:
                            pe.wait_ge(r_comb, k + 1)
                            for b in range(CB):
                                mm = nc.tensor.transpose(bank[3][:, b * P:(b + 1) * P], comb_tok[:, b, :], ident)
                            mm.then_inc(r_tr, 1)
                            pe.wait_ge(r_combT, k + 1)
                        if m >= 2:
                            pe.wait_ge(h_done, base + m - 1)
                        nc.tensor.matmul(bank[2 + m % 2][0:w, :], sel[:, m * P:m * P + w], combT[:, :],
                                         start=True, stop=True).then_inc(u_mm, 1)
                    if m == size and n + 1 < STAGES:
                        for f in range(2):
                            transpose_x(n + 1, f)
                    m -= MOE_DOWN_LAG
                    if m >= 0:
                        w = tiles[m]
                        pe.wait_ge(h_low, size * k + m + 1)
                        if m == 0:
                            pe.wait_ge(resid_done, 2 * 14)
                            if k:
                                pe.wait_ge(yT_act, k)
                                pe.wait_ge(yT_dve, k)
                        for f in range(2):
                            cols = slice(f * P, (f + 1) * P)
                            high, low = w2_high(A_r, H_r, m)[0:w, cols], w2_lo[0:w, m, cols]
                            h_hi, h_lo = h_hi_ring[m % 4][0:w, :], h_lo_ring[m % 4][0:w, :]
                            for q, (weights, h) in enumerate(((high, h_hi), (low, h_hi), (high, h_lo))):
                                mm = nc.tensor.matmul(bank[6 + f][:, :], weights, h, start=(m == 0 and q == 0),
                                                      stop=(m == size - 1 and q == 2))
                        mm.then_inc(moe_d, 1)
                pe.wait_ge(yT_act, k + 1)
                pe.wait_ge(yT_dve, k + 1)
                pe.wait_ge(xT_cp, 2 * STAGES)
                pe.wait_ge(resid_done, 2 * n)
                for b in range(CB):
                    for f in range(2):
                        cols = slice((b % 2) * D + f * P, (b % 2) * D + (f + 1) * P)
                        mm = nc.tensor.transpose(bank[4 + b // 2][:, cols], yT[f][:, b * P:(b + 1) * P], ident)
                    if b % 2:
                        mm.then_inc(y_ready, 1)

            def fp8(n):
                pe.wait_ge(xT_cp, 2 * n + 2)
                pe.wait_ge(w8_ready, 1)
                pe.wait_ge(resid_done, 2 * n)
                for j in range(2):
                    for b in (2 * j, 2 * j + 1):
                        for f in range(2):
                            mm = nc.tensor.matmul(bank[6 + j][:, (b % 2) * D:(b % 2 + 1) * D],
                                                  xqT[:, f, b * P:(b + 1) * P], w8[:, f, :],
                                                  start=(f == 0), stop=(f == 1))
                    mm.then_inc(y_ready, 1)

            def narrow(n):
                s = n // 2
                na = NAR[s]

                def turn(t):
                    bt = na.batch_base + t
                    pe.wait_ge(n_tok, bt + 1)
                    if bt:
                        pe.wait_ge(n_qT, bt)
                    if t == CB // 2 + 1:
                        pe.wait_ge(xT_cp, 2 * n + 4)
                    for f in range(2):
                        mm = nc.tensor.transpose(bank[2][:, f * P:(f + 1) * P], q_tok[:, f * P:(f + 1) * P], ident)
                    mm.then_inc(n_tr, 1)

                def finish(t):
                    pe.wait_ge(n_otc, na.batch_base + t + 1)
                    for f in range(2):
                        if f == 0 and t % 2 == 0:
                            pe.wait_ge(resid_done, 2 * n + max(t // 2 - 1, 0))
                        mm = nc.tensor.matmul(bank[6 + t // 2 % 2][:, (t % 2) * D:(t % 2 + 1) * D],
                                              n_out[:, f * P:(f + 1) * P], nout[s][:, f, :],
                                              start=(f == 0), stop=(f == 1))
                    if t % 2:
                        mm.then_inc(y_ready, 1)

                steps = list(na.steps())
                turn(0)
                project(n, 1)
                for i in range(len(steps) + OUT_LAG + 1):
                    if i < len(steps):
                        t, f, g, k, gi = steps[i]
                        bt = na.batch_base + t
                        pe.wait_ge(n_qT, bt + 1)
                        if gi >= 2:
                            pe.wait_ge(n_ex, gi - 1)
                        dst = bank[3 + gi % 2]
                        if f == "dca":
                            for ff in range(2):
                                mm = nc.tensor.matmul(dst[:, ff * P:(ff + 1) * P], nqT[bt % 2][:, ff * P:(ff + 1) * P],
                                                      kdca[:, ff, t, :, :], start=True, stop=True)
                        else:
                            who, count = na.spread(t, f)
                            pe.wait_ge(n_kbd_g if who == "gpsimd" else n_kbd_v, count)
                            w = 4 * na.keys
                            mm = nc.tensor.matmul(dst[:, 0:w], nqT[bt % 2][:, f * P:(f + 1) * P],
                                                  kbd[f][:, g * w:(g + 1) * w], start=True, stop=True)
                        mm.then_inc(n_s, 1)
                    if i in na.turn_steps:
                        m, f = na.turn_steps[i]
                        if (m, f) != (1, 0):
                            pe.wait_ge(xT_cp, 2 * (n + m) + f)
                        transpose_x(n + m, f)
                    j = i - OUT_LAG - 1
                    if j >= 0 and steps[j][3] == na.n - 1:
                        finish(steps[j][0])
                    j = i - TURN_LAG
                    if 0 <= j < len(steps):
                        t, f, g, k, gi = steps[j]
                        pe.wait_ge(n_pn, gi + 1)
                        if gi:
                            who, count = na.turned_copy(gi - 1)
                            pe.wait_ge(n_ptc_a if who == "scalar" else n_ptc_v, count)
                        for u in range(2 if f == "dca" else 4):
                            w = P if f == "dca" else na.keys
                            mm = nc.tensor.transpose(bank[5][0:w, u * P:(u + 1) * P],
                                                     np_ring[gi % 6][:, u * w:(u + 1) * w], ident)
                        mm.then_inc(n_ptm, 1)
                    j = i - OUT_LAG
                    if 0 <= j < len(steps):
                        t, f, g, k, gi = steps[j]
                        bt = na.batch_base + t
                        dst = bank[0]
                        who, count = na.turned_copy(gi)
                        pe.wait_ge(n_ptc_a if who == "scalar" else n_ptc_v, count)
                        if k == 0:
                            if bt:
                                pe.wait_ge(n_otc, bt)
                        if f == "dca":
                            for ff in range(2):
                                mm = nc.tensor.matmul(dst[:, ff * P:(ff + 1) * P],
                                                      vdca[:, t, ff * P:(ff + 1) * P],
                                                      npt_ring[gi % 2][:, ff * P:(ff + 1) * P],
                                                      start=False, stop=True, skip_group_check=True)
                        else:
                            pe.wait_ge(n_vpad, 2 * bt + f + 1)
                            for u in range(4):
                                h = 4 * g + u
                                mm = nc.tensor.matmul(dst[:, f * P:(f + 1) * P],
                                                      vpad[f][0:na.keys, h * P:(h + 1) * P],
                                                      npt_ring[gi % 2][0:na.keys, u * P:(u + 1) * P],
                                                      start=(k == 0 and u == 0), stop=(h == na.heads - 1),
                                                      skip_group_check=True)
                        mm.then_inc(n_otm, 1)
                    if i < len(steps) and steps[i][3] == na.q_step and steps[i][0] + 1 < B:
                        turn(steps[i][0] + 1)
                        if steps[i][0] + 2 < B:
                            project(n, steps[i][0] + 2)

            pe.wait_ge(ld["const"], 16)
            pe.wait_ge(ld["ctx"], 16)
            for b in range(B):
                mm = nc.tensor.transpose(bank[4 + b // 4][:, (b % 4) * P:(b % 4 + 1) * P], ctx_tok[:, b, :], ident)
            mm.then_inc(ctxT_mm, 1)
            pe.wait_ge(ctxT_cp, 1)
            for n in range(STAGES):
                kind = KIND[n // 2]
                if n == 7:
                    pe.wait_ge(ld["L2"], 64)
                    weight_products(4)
                if kind == NARROW and n % 2:
                    continue
                if n in (7, 8):
                    for f in range(2):
                        transpose_x(n, f)
                {WIDE: wide, FFN: moe if n >= 14 else ffn, NARROW: narrow, FP8: fp8}[kind](n)

        @block.scalar
        def _(act):
            def copy_xT(n, f):
                act.wait_ge(xT_mm, 2 * n + f + 1)
                dst = xqT[:, f, :] if n // 2 == 3 else xT[:, n % 2, f, :]
                nc.scalar.activation(dst, bank[turn_bank(n, f)][:, :], ACT.Copy).then_inc(xT_cp, 1)

            def copy_products(which):
                base = 0 if which == 0 else 8
                for u in range(8 if which == 0 else 16):
                    act.wait_ge(pre_mm, base + u + 1)
                    src = bank[2 + (base + u) % 4]
                    if which == 4 and u < 8:
                        dst = L2_m[:, :, 2 * u:2 * u + 2, :]
                        src = src[:, :].rearrange("p (f h n) -> p f h n", f=2, h=2)
                    else:
                        dst = out_w[which][:, 2 * (u % 8):2 * (u % 8) + 2, :]
                        src = src[:, :].rearrange("p (h n) -> p h n", h=2)
                    nc.scalar.activation(dst, src, ACT.Copy).then_inc(pre_cp, 1)

            def keys0(a, b):
                for g in range(4):
                    u = 4 * b + g
                    act.wait_ge(k_mm, 16 * a + u + 1)
                    if u >= 2:
                        act.wait_ge(k_red, 16 * a + u - 1)
                    src = bank[2 + u % 2][:, :]
                    nc.scalar.activation(q2_ring[u % 2], src, ACT.Square).then_inc(k_sq, 1)
                    nc.scalar.activation(heads[:, 4 * g:4 * g + 4, b * P:(b + 1) * P],
                                         src.rearrange("p (h d) -> p h d", h=4), ACT.Copy).then_inc(k_cp, 1)

            def wide(n):
                a, c, s = WIDE_INDEX[n], n % 2, n // 2
                base = HEADS * a
                if n == 0:
                    for b in range(CB):
                        keys0(0, b)
                    for f in range(2):
                        copy_xT(0, f)
                    copy_products(0)
                    act.wait_ge(ld["rows"], 128)
                    nc.scalar.activation(tg[:, :], gates[:, :], ACT.Tanh).then_inc(tg_ready, 1)
                    act.wait_ge(trig_arg, 1)
                    nc.scalar.activation(trig[:, 4:6, :], trig[:, 2:4, :], ACT.Sin).then_inc(trig_sin, 1)
                if s == 0:
                    act.wait_ge(gqk_set, 1)
                    act.wait_ge(k_red, 16 * a + 16)
                for i in range(HEADS + 3):
                    if i < HEADS:
                        act.wait_ge(q_mm, base + i + 1)
                        if i >= 2:
                            act.wait_ge(s_mm, base + i - 1)
                        nc.scalar.activation(q_ring[i % 2], bank[0][:, :], ACT.Copy).then_inc(q_cp, 1)
                        if s == 0:
                            nc.scalar.activation(q2_ring[i % 2], bank[0][:, :], ACT.Square).then_inc(q_sq, 1)
                            act.wait_ge(kT_mm, base + i + 1)
                            nc.scalar.activation(heads[:, i, :], bank[1][:, :], ACT.Copy, scale=gqk[:, 2:3])\
                                .then_inc(kT_cp, 1)
                    h = i - 3
                    if 0 <= h < HEADS:
                        act.wait_ge(pt_mm, base + h + 1)
                        if h >= 2:
                            act.wait_ge(ot_mm, base + h - 1)
                        nc.scalar.activation(pt_ring[h % 2], bank[4][:, :], ACT.Copy).then_inc(pt_cp, 1)
                    h = i - 1
                    if 0 <= h < HEADS:
                        act.wait_ge(nb, base + h + 1)
                        if h >= 4:
                            act.wait_ge(pt_mm, base + h - 3)
                        for b in range(CB):
                            cols = slice(b * P, (b + 1) * P)
                            e = nc.scalar.activation(
                                p_ring[h % 4][:, cols], bank[2 + h % 2][:, cols], ACT.Exp,
                                bias=neg_max[:, h, b:b + 1],
                                scale=q_rstd[:, h, b:b + 1] if s == 0 else float(P) ** -0.5,
                                accum_out=row_sum[:, h, b:b + 1])
                        e.then_inc(ex, 1)
                for f in range(2):
                    copy_xT(n + 1, f)
                if n == 0:
                    for b in range(CB):
                        keys0(1, b)

            def ffn(n):
                s, c = n // 2, n % 2
                base, tiles = FFN_BASE[n], TILES[s]
                if s == 5:
                    act.wait_ge(ld["late"], 64)
                for i in range(len(tiles) + 1):
                    first, every = (2, 3) if s == 1 else (0, 1)
                    j = (i - first) // every
                    if (i - first) % every == 0 and 1 <= j <= CB:
                        bt = NAR[s + 1].batch_base + CB * c + j
                        act.wait_ge(c_tr, bt)
                        nc.scalar.activation(kT_all[:, CB * c + j - 1, :, :],
                                             bank[5][:, 0:256].rearrange("p (f k) -> p f k", f=2), ACT.Copy)\
                            .then_inc(c_kT, 1)
                    if i == len(tiles):
                        break
                    w = tiles[i]
                    act.wait_ge(g_mm, base + i + 1)
                    if i >= 2:
                        act.wait_ge(h_done, base + i - 1)
                    dst = act_ring[i % 2][0:w, :]
                    if s == 1:
                        g = nc.scalar.activation(dst, bank[i % 2][0:w, :], ACT.Gelu_apprx_tanh)
                    else:
                        g = nc.scalar.activation(dst, bank[i % 2][0:w, :], ACT.Silu,
                                                 scale=ffn2_scale[0:w, 0, i:i + 1])
                    g.then_inc(g_act, 1)
                for f in range(2):
                    copy_xT(n + 1, f)

            def moe(n):
                c, k, base, tiles = n % 2, n - 14, FFN_BASE[n], TILES[7]
                size = MOE_TILES

                def high_weights(i):
                    w = tiles[i]
                    nc.scalar.activation(w1_hi[:, :, i * P:i * P + w], moe_w1[:, :, i * P:i * P + w], ACT.Copy)
                    nc.scalar.activation(w2_high(A_r, H_r, i), moe_w2[:, i, :], ACT.Copy).then_inc(w_high, 1)

                if k == 0:
                    act.wait_ge(y_ready, 28)
                    act.wait_ge(ld["moe1"], 16)
                    act.wait_ge(ld["ff2"], 128)
                else:
                    act.wait_ge(g_mm, base)
                act.wait_ge(xT_cp, 2 * n + 2)
                nc.scalar.activation(x_hi, xT[:, c, :, :], ACT.Copy).then_inc(x_high, 1)
                if k == 0:
                    high_weights(0)
                    high_weights(1)
                act.wait_ge(r_mm, k + 1)
                nc.scalar.activation(score[:, :, :], bank[2][:, 0:64].rearrange("p (b e) -> p b e", b=CB),
                                     ACT.Sigmoid).then_inc(r_sig, 1)
                for i in range(size + MOE_LEAD):
                    if k == 0 and i + 2 < size:
                        high_weights(i + 2)
                    if i < size:
                        w = tiles[i]
                        act.wait_ge(g_mm, base + i + 1)
                        if i >= 10:
                            act.wait_ge(h_done, base + i - 9)
                        nc.scalar.activation(moe_act[i % 10][0:w, :], bank[i % 2][0:w, :], ACT.Silu)\
                            .then_inc(g_act, 1)
                    m = i - MOE_LEAD
                    if m >= 0:
                        w = tiles[m]
                        act.wait_ge(h_done, base + m + 1)
                        if size * k + m >= 4:
                            act.wait_ge(moe_d, size * k + m - 3)
                        nc.scalar.activation(h_hi_ring[m % 4][0:w, :], moe_h[m % 4][0:w, :], ACT.Copy)\
                            .then_inc(h_high, 1)
                if n + 1 < STAGES:
                    for f in range(2):
                        copy_xT(n + 1, f)
                act.wait_ge(moe_d, size * (k + 1))
                if k:
                    act.wait_ge(y_ready, 2 * n)
                nc.scalar.activation(yT[0], bank[6][:, :], ACT.Copy).then_inc(yT_act, 1)

            def narrow(n):
                s = n // 2
                na = NAR[s]

                def copy_qT(t):
                    bt = na.batch_base + t
                    act.wait_ge(n_tr, bt + 1)
                    nc.scalar.activation(nqT[bt % 2], bank[2][:, 0:256], ACT.Copy).then_inc(n_qT, 1)

                steps = list(na.steps())
                copy_qT(0)
                for i in range(len(steps) + OUT_LAG):
                    j = i - TURN_LAG
                    if 0 <= j < len(steps) and na.turned_copy(steps[j][4])[0] == "scalar":
                        t, f, g, k, gi = steps[j]
                        act.wait_ge(n_ptm, gi + 1)
                        if gi >= 2:
                            act.wait_ge(n_otm, gi - 1)
                        w, m = (P, 256) if f == "dca" else (na.keys, 512)
                        nc.scalar.activation(npt_ring[gi % 2][0:w, 0:m], bank[5][0:w, 0:m], ACT.Copy)\
                            .then_inc(n_ptc_a, 1)
                    if i < len(steps):
                        t, f, g, k, gi = steps[i]
                        act.wait_ge(n_nb, gi + 1)
                        if gi >= 6:
                            act.wait_ge(n_ptm, gi - 5)
                        if f == "dca":
                            nc.scalar.activation(np_ring[gi % 6][:, 0:256], dca_diff, ACT.Exp,
                                                 scale=na.scale).then_inc(n_ex, 1)
                        else:
                            for u in range(4):
                                cols = slice(u * na.keys, (u + 1) * na.keys)
                                e = nc.scalar.activation(np_ring[gi % 6][:, cols], bank[3 + gi % 2][:, cols], ACT.Exp,
                                                         bias=n_max[:, gi % 6, u:u + 1], scale=na.scale,
                                                         accum_out=n_sum[:, gi % 6, u:u + 1])
                            e.then_inc(n_ex, 1)
                    if i in na.turn_steps:
                        m, f = na.turn_steps[i]
                        copy_xT(n + m, f)
                    j = i - OUT_LAG
                    if 0 <= j < len(steps) and steps[j][3] == na.n - 1:
                        t, f, g, k, gi = steps[j]
                        act.wait_ge(n_otm, gi + 1)
                        nc.scalar.activation(n_out, bank[0][:, 0:256], ACT.Copy).then_inc(n_otc, 1)
                    if i < len(steps) and steps[i][3] == na.q_step and steps[i][0] + 1 < B:
                        copy_qT(steps[i][0] + 1)

            act.wait_ge(ctxT_mm, 1)
            for i in range(2):
                m = nc.scalar.activation(ctxT[:, 4 * i:4 * i + 4, :].rearrange("p b k -> p (b k)"), bank[4 + i][:, :],
                                         ACT.Copy)
            m.then_inc(ctxT_cp, 1)
            for n in range(STAGES):
                kind = KIND[n // 2]
                if n == 7:
                    copy_products(4)
                if n in (7, 8):
                    for f in range(2):
                        copy_xT(n, f)
                if kind == NARROW and n % 2 == 0:
                    narrow(n)
                elif kind in (WIDE, FFN):
                    {WIDE: wide, FFN: moe if n >= 14 else ffn}[kind](n)

        @block.gpsimd
        def _(pool):
            def broadcast(ap, shape):
                return ap.unsqueeze(2).broadcast_to(shape)

            def selection():
                rows = sel.rearrange("p (e j) -> p e j", e=EXPERTS + 1)
                nc.gpsimd.memset(sel, 0.0).then_inc(sel_chain, 1)
                for k in range(3):
                    pool.wait_ge(sel_chain, k + 1)
                    nc.gpsimd.affine_select(out=rows, in_=rows, compare_op=ALU.not_equal, fill=1.0,
                                            base=-(EXPERTS + 1) * k, pattern=[[-1, EXPERTS + 1], [0, MOE_H]],
                                            channel_multiplier=1).then_inc(sel_chain, 1)

            def wide(n):
                a, s = WIDE_INDEX[n], n // 2
                base = HEADS * a
                if s == 0:
                    pool.wait_ge(k_rstd, a + 1)
                    pool.wait_ge(k_cp, 16 * a + 16)
                    for h in range(1, HEADS, 2):
                        v = heads[:, h, :].rearrange("p (b d) -> p b d", b=CB)
                        nc.gpsimd.tensor_tensor(v, v, broadcast(k_ss[:, h, :], [P, CB, P]), ALU.mult)\
                            .then_inc(k_scaled_g, 1)
                for h in range(HEADS):
                    pool.wait_ge(rs, base + h + 1)
                    v = p_ring[h % 4].rearrange("p (b k) -> p b k", b=CB)
                    nc.gpsimd.tensor_tensor(v, v, broadcast(row_sum[:, h, :], [P, CB, P]), ALU.mult)\
                        .then_inc(p_norm, 1)

            def narrow(n):
                s = n // 2
                na = NAR[s]

                def pad_v(t, f):
                    bt = na.batch_base + t
                    if t == 0:
                        pool.wait_ge(c_v, na.batch_base + B)
                    else:
                        pool.wait_ge(n_otm, na.group_base + (t - 1) * na.n + (f + 1) * na.groups)
                    dst = bass.AP(vpad[f].tensor, vpad[f].offset,
                                  [list(vpad[f].ap[0]), [P + na.hd, na.heads], [1, na.hd]])
                    nc.gpsimd.tensor_copy(
                        dst, v_all[:, t, f * P:(f + 1) * P].rearrange("p (h d) -> p h d", d=na.hd))\
                        .then_inc(n_vpad, 1)

                def spread_k(t, f):
                    if t == 0:
                        pool.wait_ge(c_kT, na.batch_base + B)
                    else:
                        pool.wait_ge(n_s, na.group_base + (t - 1) * na.n + (f + 1) * na.groups)
                    shape = [P, na.heads, na.keys]
                    nc.gpsimd.tensor_tensor(
                        kbd[f][:, 0:na.heads * na.keys].rearrange("p (h k) -> p h k", h=na.heads),
                        kT_all[:, t, f, 0:na.keys].unsqueeze(1).broadcast_to(shape),
                        head_mask[s].unsqueeze(2).broadcast_to(shape), ALU.mult).then_inc(n_kbd_g, 1)

                steps = list(na.steps())
                pool.wait_ge(vpad_zero, 1 if s == 2 else 2)
                if s == 2:
                    pool.wait_ge(w8_ready, 1)
                own = [f for f in range(2) if na.spread(0, f)[0] == "gpsimd"]
                for f in own:
                    spread_k(0, f)
                pad_v(0, 0)
                pad_v(0, 1)
                for i, (t, f, g, k, gi) in enumerate(steps):
                    pool.wait_ge(n_rs, gi + 1)
                    m, w = (16, 16) if f == "dca" else (4, na.keys)
                    v = np_ring[gi % 6][:, 0:m * w].rearrange("p (h k) -> p h k", h=m)
                    nc.gpsimd.tensor_tensor(v, v, broadcast(n_sum[:, gi % 6, 0:m], [P, m, w]), ALU.mult)\
                        .then_inc(n_pn, 1)
                    for f in range(2):
                        if t and k == (f + 1) * na.groups + OUT_LAG - 1 - na.n:
                            pad_v(t, f)
                    for f in own:
                        if k == min((f + 1) * na.groups, na.n - 1) and t + 1 < B:
                            spread_k(t + 1, f)

            for n in range(STAGES):
                if n in (2, 10):
                    pool.wait_ge(y_ready, 2 * n)
                    if n == 2:
                        dca_keys = ctxT[:, :, 112:128]
                        nc.gpsimd.tensor_copy(dca_ctx.rearrange("p (b k) -> p b k", b=B), dca_keys)\
                            .then_inc(dca_copied, 1)
                        nc.gpsimd.tensor_copy(dca_ctx8.rearrange("p b (r k) -> p b r k", r=8),
                                              dca_keys.unsqueeze(2).broadcast_to([P, B, 8, 16])).then_inc(dca_copied, 1)
                    nc.gpsimd.memset(H[:, 4096:8192], 0.0).then_inc(vpad_zero, 1)
                if n == 10:
                    pool.wait_ge(resid_done, 12)
                    selection()
                if KIND[n // 2] == WIDE:
                    wide(n)
                elif KIND[n // 2] == NARROW and n % 2 == 0:
                    narrow(n)
                elif n == 14:
                    for i, w in enumerate(TILES[7]):
                        pool.wait_ge(w_high, i + 1)
                        cols = slice(i * P, i * P + w)
                        nc.gpsimd.tensor_tensor(w1_lo[:, :, cols], moe_w1[:, :, cols], w1_hi[:, :, cols].bitcast(F32),
                                                ALU.subtract)
                        nc.gpsimd.tensor_tensor(w2_lo[:, i, :], moe_w2[:, i, :], w2_high(A_r, H_r, i).bitcast(F32), ALU.subtract)\
                            .then_inc(w_low, 1)

        @block.vector
        def _(dve):
            count = [0]

            def link(ins):
                count[0] += 1
                ins.then_inc(v_chain, 1)
                dve.wait_ge(v_chain, count[0])

            def mark(ins):
                count[0] += 1
                ins.then_inc(v_chain, 1)
                return count[0]

            def tt(o, a, b, op):
                return nc.vector.tensor_tensor(o, a, b, op)

            def ts(o, a, s1, s2, op0, op1=ALU.bypass):
                return nc.vector.tensor_scalar(o, a, s1, s2, op0, op1) if s2 is not None else \
                    nc.vector.tensor_scalar(o, a, s1, None, op0)

            def stt(o, a, s, b, op0, op1):
                return nc.vector.scalar_tensor_tensor(o, a, s, b, op0, op1)

            def rsqrt(dst, v, scale, eps, width, ss_index=0):
                x, y, t = (newton[:, k, 0:width] for k in range(3))
                if ss_index:
                    ts(x, v, scale, eps, ALU.mult, ALU.add).then_inc(ss_read, 1)
                    dve.wait_ge(ss_read, ss_index)
                else:
                    link(ts(x, v, scale, eps, ALU.mult, ALU.add))
                link(ts(t.bitcast(I32), x.bitcast(I32), 1, None, ALU.logical_shift_right))
                link(ts(y.bitcast(I32), t.bitcast(I32), -1.0, RSQRT_SEED, ALU.mult, ALU.add))
                for k in range(3):
                    link(tt(t, y, y, ALU.mult))
                    link(stt(t, t, -0.5, x, ALU.mult, ALU.mult))
                    if k < 2:
                        link(stt(y, t, 1.5, y, ALU.add, ALU.mult))
                return stt(dst, t, 1.5, y, ALU.add, ALU.mult)

            def quantise(v, t, u, scale):
                link(ts(v, v, scale, None, ALU.mult))
                link(ts(t.bitcast(U32), v.bitcast(U32), 0x7F800000, None, ALU.bitwise_and))
                link(ts(t, t, 2.0 ** -6, 1.5 * 2.0 ** 20, ALU.max, ALU.mult))
                link(tt(u, v, t, ALU.add))
                link(tt(v, u, t, ALU.subtract))
                link(ts(t, v, 1.1 * 2.0 ** 119, None, ALU.mult))
                return stt(v, t, 0.0, v, ALU.mult, ALU.add)

            def moments(n, batches=range(CB)):
                lo, hi = batches[0], batches[-1] + 1
                for b in batches:
                    m = mark(nc.vector.bn_stats(stats[:, b, :], x_sb[:, CB * (n % 2) + b, :]))
                dve.wait_ge(v_chain, m)
                for b in batches:
                    m = mark(nc.vector.bn_aggr(mv[:, b, :], stats[:, b, :]))
                dve.wait_ge(v_chain, m)
                link(rsqrt(x_rstd[:, lo:hi], mv[:, lo:hi, 1], 1.0, 1e-5, hi - lo))

            def centre_rows(n, batches=range(CB)):
                c = n % 2
                if n >= 2:
                    dve.wait_ge(xT_mm, 2 * n - 2)
                for b in batches:
                    m = mark(ts(xn[:, c, b, :], x_sb[:, CB * c + b, :], mv[:, b, 0:1], x_rstd[:, b:b + 1],
                                ALU.subtract, ALU.mult))
                dve.wait_ge(v_chain, m)

            def normalise(n):
                centre_rows(n)
                nc.vector.nop().then_inc(ln_done, 1)

            def quantise_rows(n, batches):
                rows = xn[:, n % 2, batches[0]:batches[-1] + 1, :].rearrange("p b d -> p (b d)")
                w = rows.shape[-1]
                link(quantise(rows, q8_tmp[0][:, 0:w], q8_tmp[1][:, 0:w], scales8[:, 0:1]))
                if batches[-1] == CB - 1:
                    nc.vector.nop().then_inc(ln_done, 1)

            def layer_norm(n):
                moments(n)
                normalise(n)

            def residual(n, j):
                s, c = n // 2, n % 2
                dve.wait_ge(y_ready, 2 * n + j + 1)
                x = x_sb[:, CB * c + 2 * j:CB * c + 2 * j + 2, :]
                y = bank[(4 if s == 7 else 6) + j][:, :].rearrange("p (b d) -> p b d", b=2)
                gate = tg[:, s // 2 + 4 * (s % 2):s // 2 + 4 * (s % 2) + 1]
                if s == 3:
                    gate = scales8[:, 2:3]
                if s == 5:
                    if j:
                        dve.wait_ge(resid_done, 2 * n + 1)
                    t = R[:, 4096:4608].rearrange("p (b d) -> p b d", b=2)
                    link(tt(t, y, down_scale.unsqueeze(1).broadcast_to([P, 2, D]), ALU.mult))
                    i = stt(x, t, gate, x, ALU.mult, ALU.add)
                elif s in (2, 6):
                    t = X[:, 768:1024]
                    link(ts(t, out_bias[s], gate, None, ALU.mult))
                    link(tt(x, x, t.unsqueeze(1).broadcast_to([P, 2, D]), ALU.add))
                    i = stt(x, y, gate, x, ALU.mult, ALU.add)
                else:
                    i = stt(x, y, gate, x, ALU.mult, ALU.add)
                i.then_inc(resid_done, 1)

            def rsqrt_and_unpack(dst, v, scale, eps, width, ss_index, p, high):
                x, y, t = (newton[:, k, 0:width] for k in range(3))
                packed, block_scale = fp4_slot[p % 3]
                bits, biased = fp4_tmp[0], fp4_tmp[1]
                after = dve.wait_ge
                if not high:
                    after(ld[f"fp4_{p % 3}"], 32 * (p // 3 + 1))
                ts(x, v, scale, eps, ALU.mult, ALU.add).then_inc(ss_read, 1)
                u0 = mark(ts(bits.bitcast(I32), packed.bitcast(I32), 24 if high else 28, 6,
                             ALU.logical_shift_left, ALU.arith_shift_right))
                after(ss_read, ss_index)
                r1 = mark(ts(t.bitcast(I32), x.bitcast(I32), 1, None, ALU.logical_shift_right))
                after(v_chain, u0)
                u1 = mark(ts(bits.bitcast(U32), bits.bitcast(U32), 0x81C00000, None, ALU.bitwise_and))
                after(v_chain, r1)
                r2 = mark(ts(y.bitcast(I32), t.bitcast(I32), -1.0, RSQRT_SEED, ALU.mult, ALU.add))
                after(v_chain, u1)
                u2 = mark(ts(biased, bits, 2.0 ** -120, 2.0 ** 126, ALU.add, ALU.mult))
                after(v_chain, r2)
                r3 = mark(tt(t, y, y, ALU.mult))
                after(v_chain, u2)
                stt(ff0[p // 4][:, high, 512 * (p % 4):512 * (p % 4) + 512], biased, -64.0, block_scale,
                    ALU.add, ALU.mult).then_inc(fp4_done, 1)
                after(v_chain, r3)
                link(stt(t, t, -0.5, x, ALU.mult, ALU.mult))
                link(stt(y, t, 1.5, y, ALU.add, ALU.mult))
                link(tt(t, y, y, ALU.mult))
                link(stt(t, t, -0.5, x, ALU.mult, ALU.mult))
                link(stt(y, t, 1.5, y, ALU.add, ALU.mult))
                link(tt(t, y, y, ALU.mult))
                link(stt(t, t, -0.5, x, ALU.mult, ALU.mult))
                link(stt(dst, t, 1.5, y, ALU.add, ALU.mult))
                after(fp4_done, 2 * p + high + 1)

            def keys0(a, b):
                for g in range(4):
                    u = 4 * b + g
                    dve.wait_ge(k_sq, 16 * a + u + 1)
                    nc.vector.tensor_reduce(k_ss[:, 4 * g:4 * g + 4, b],
                                            q2_ring[u % 2].rearrange("p (h d) -> p h d", h=4), AX, ALU.add)\
                        .then_inc(k_red, 1)

            def scale_keys0(a):
                dve.wait_ge(k_red, 16 * a + 16)
                flat = k_ss[:, :, :].rearrange("p h b -> p (h b)")
                rsqrt(flat, flat, 1.0 / P, 1e-5, 64).then_inc(k_rstd, 1)
                dve.wait_ge(k_rstd, a + 1)
                dve.wait_ge(k_cp, 16 * a + 16)
                for h in range(0, HEADS, 2):
                    v = heads[:, h, :].rearrange("p (b d) -> p b d", b=CB)
                    tt(v, v, k_ss[:, h, :].unsqueeze(2).broadcast_to([P, CB, P]), ALU.mult)\
                        .then_inc(k_scaled_v, 1)

            def wide(n):
                a, c, s = WIDE_INDEX[n], n % 2, n // 2
                base = HEADS * a
                if n == 0:
                    for b in range(CB):
                        keys0(0, b)
                    scale_keys0(0)
                    angles()
                elif n == 8:
                    ts(mask_bias, mask8[:, :], 1.0, NEG, ALU.subtract, ALU.mult).then_inc(mask_set, 1)
                    nc.vector.tensor_reduce(any_valid[:, :], mask8[:, :].rearrange("p (b k) -> p b k", b=B), AX,
                                            ALU.max).then_inc(mask_set, 1)
                    dve.wait_ge(mask_set, 2)
                for i in range(HEADS + 4):
                    h = i - 1
                    if 0 <= h < HEADS:
                        if s == 0:
                            dve.wait_ge(ss_mm, base + h + 1)
                            ss = bank[6][:, :].rearrange("p (b k) -> p b k", b=CB)[:, :, 0]
                            k = HEADS * c + h
                            if k < 24:
                                rsqrt_and_unpack(q_rstd[:, h, :], ss, 1.0 / P, 1e-5, CB, base + h + 1, k // 2, k % 2)
                            else:
                                link(rsqrt(q_rstd[:, h, :], ss, 1.0 / P, 1e-5, CB, base + h + 1))
                    h = i - 2
                    if 0 <= h < HEADS:
                        dve.wait_ge(ex, base + h + 1)
                        if s == 0:
                            nc.vector.reciprocal(row_sum[:, h, :], row_sum[:, h, :]).then_inc(rs, 1)
                        else:
                            link(nc.vector.reciprocal(row_sum[:, h, :], row_sum[:, h, :]))
                            tt(row_sum[:, h, :], row_sum[:, h, :], any_valid[:, CB * c:CB * c + CB], ALU.mult)\
                                .then_inc(rs, 1)
                    h = i - 1
                    if 0 <= h < HEADS:
                        dve.wait_ge(s_mm, base + h + 1)
                        sc = bank[2 + h % 2][:, :]
                        if s != 0:
                            link(tt(sc, sc, mask_bias[:, CT * c:CT * (c + 1)], ALU.add))
                        link(nc.vector.tensor_reduce(neg_max[:, h, :], sc.rearrange("p (b k) -> p b k", b=CB), AX,
                                                     ALU.max))
                        if s == 0:
                            stt(neg_max[:, h, :], neg_max[:, h, :], -1.0, q_rstd[:, h, :], ALU.mult, ALU.mult)\
                                .then_inc(nb, 1)
                        else:
                            ts(neg_max[:, h, :], neg_max[:, h, :], -float(P) ** -0.5, None, ALU.mult)\
                                .then_inc(nb, 1)
                    h = i - 4
                    if 0 <= h < HEADS:
                        dve.wait_ge(ot_mm, base + h + 1)
                        nc.vector.tensor_copy(heads[:, h, :], bank[5 + 2 * (h % 2)][:, :]).then_inc(ot_cp, 1)
                    if i == 4:
                        if n == 0:
                            dve.wait_ge(ld["x1"], 16)
                        moments(n + 1)
                    if i == 8:
                        normalise(n + 1)
                    if n == 0 and i == HEADS:
                        rotations()
                    if n == 9 and i == 10:
                        cast_ff2()

            def cast_ff2():
                dve.wait_ge(ld["ff2"], 128)
                for k, (lo, hi) in enumerate(((0, 1408), (1408, 2816), (2816, 4352))):
                    v = Bw[:, lo:hi]
                    ts(v, v.bitcast(I32), -128.0, None, ALU.add).then_inc(ff2_cast, 1)

            def route_dve(n):
                k = n - 13
                dve.wait_ge(r_sig, k)
                sg = score[:, :, :].rearrange("p b (g j) -> p (b g) j", j=4)
                m, top2, pair = route[:, 0, :], route[:, 1, 0:16], route[:, 1, 16:32]
                first = True
                for u in range(4):
                    for v in range(u + 1, 4):
                        if first:
                            link(tt(top2, sg[:, :, u], sg[:, :, v], ALU.add))
                        else:
                            link(tt(pair, sg[:, :, u], sg[:, :, v], ALU.add))
                            link(tt(top2, top2, pair, ALU.max))
                        first = False

                def in_top2(dst, v, tie, size, ra, rb):
                    shape = [P, CB, size, size]
                    other, own = v.unsqueeze(2).broadcast_to(shape), v.unsqueeze(3).broadcast_to(shape)
                    link(tt(ra, other, own, ALU.is_equal))
                    link(tt(ra, ra, tie.unsqueeze(1).broadcast_to(shape), ALU.mult))
                    link(tt(rb, other, own, ALU.is_gt))
                    link(tt(ra, ra, rb, ALU.add))
                    link(nc.vector.tensor_reduce(dst, ra, AX, ALU.add))
                    link(ts(dst, dst, 2.0, None, ALU.is_lt))

                gsel = route[:, 2, 0:16].rearrange("p (b g) -> p b g", b=CB)
                in_top2(gsel, top2.rearrange("p (b g) -> p b g", b=CB), tie4, 4,
                        route_a[:, :, 0:4, 0:4], route_b[:, :, 0:4, 0:4])
                masked = m.rearrange("p (b e) -> p b e", b=CB)
                link(tt(m.rearrange("p (g j) -> p g j", j=4), sg,
                        route[:, 2, 0:16].unsqueeze(2).broadcast_to([P, 16, 4]), ALU.mult))
                chosen = route[:, 3, :].rearrange("p (b e) -> p b e", b=CB)
                in_top2(chosen, masked, tie16, 16, route_a, route_b)
                link(tt(chosen, chosen, masked, ALU.mult))
                total = route[:, 4, 0:CB]
                link(nc.vector.tensor_reduce(total, chosen, AX, ALU.add))
                link(ts(total, total, 1e-20, None, ALU.add))
                link(nc.vector.reciprocal(total, total))
                if n == 14:
                    link(nc.vector.memset(comb_tok, 0.0))
                    link(nc.vector.memset(comb_tok[:, :, 16:17], 1.0))
                else:
                    dve.wait_ge(r_tr, 1)
                link(tt(chosen, chosen, total.unsqueeze(2).broadcast_to([P, CB, 16]), ALU.mult))
                part = route[:, 5, 0:32].bitcast(BF16).rearrange("p (b e) -> p b e", b=CB)
                for q in range(3):
                    link(nc.vector.tensor_copy(part, chosen))
                    dst = comb_tok[:, :, 17 * q:17 * q + 16]
                    if q < 2:
                        link(nc.vector.tensor_copy(dst, part))
                        link(tt(chosen, chosen, dst, ALU.subtract))
                    else:
                        nc.vector.tensor_copy(dst, part).then_inc(r_comb, 1)
                dve.wait_ge(r_tr, k)
                nc.vector.tensor_copy(combT, bank[3][:, :]).then_inc(r_combT, 1)

            def ffn(n):
                s, c = n // 2, n % 2
                base, tiles = FFN_BASE[n], TILES[s]
                if s == 5:
                    dve.wait_ge(ld["late"], 64)
                for i, w in enumerate(tiles):
                    dve.wait_ge(g_act, base + i + 1)
                    dve.wait_ge(u_mm, base + i + 1)
                    if i >= 3:
                        dve.wait_ge(d_mm, DOWN_BASE[n] + i - 2)
                    up, ga, dst = bank[2 + i % 2][0:w, :], act_ring[i % 2][0:w, :], h_ring[i % 3][0:w, :]
                    if s == 5:
                        o = stt(dst, up, ffn2_scale[0:w, 1, i:i + 1], ga, ALU.mult, ALU.mult)
                    else:
                        o = tt(dst, up, ga, ALU.mult)
                    o.then_inc(h_done, 1)
                    if s == 1:
                        j, part = divmod(i - 2, 3)
                        if n == 3 and i == 0:
                            dca_k_norm()
                        if n == 3 and i == 4:
                            dca_k_spread()
                        if 0 <= j < CB and part < 2:
                            norm_k(c, j, part)
                        if n == 2 and i in DCA_V_STEPS:
                            dca_v(DCA_V_STEPS.index(i))
                        if n == 3 and i == 15:
                            quantise_w8()
                    if s == 5 and i < CB:
                        rope_k(c, i)
                    if i == len(tiles) - 3:
                        layer_norm(n + 1)

            def moe(n):
                c, k, base, tiles = n % 2, n - 14, FFN_BASE[n], TILES[7]
                size = MOE_TILES
                dve.wait_ge(x_high, k + 1)
                tt(x_lo, xT[:, c, :, :], x_hi.bitcast(F32), ALU.subtract).then_inc(x_low, 1)
                route_dve(n)
                for i in range(size + 1):
                    if i < size:
                        w = tiles[i]
                        dve.wait_ge(g_act, base + i + 1)
                        dve.wait_ge(u_mm, base + i + 1)
                        if size * k + i >= 4:
                            dve.wait_ge(moe_d, size * k + i - 3)
                        tt(moe_h[i % 4][0:w, :], bank[2 + i % 2][0:w, :], moe_act[i % 10][0:w, :], ALU.mult)\
                            .then_inc(h_done, 1)
                    m = i - 1
                    if m >= 0:
                        w = tiles[m]
                        dve.wait_ge(h_high, size * k + m + 1)
                        tt(h_lo_ring[m % 4][0:w, :], moe_h[m % 4][0:w, :], h_hi_ring[m % 4][0:w, :].bitcast(F32),
                           ALU.subtract).then_inc(h_low, 1)
                dve.wait_ge(moe_d, size * (k + 1))
                if k:
                    dve.wait_ge(y_ready, 2 * n)
                nc.vector.tensor_copy(yT[1], bank[7][:, :]).then_inc(yT_dve, 1)

            def quantise_w8():
                flat = w8_raw.rearrange("p k n -> p (k n)")
                dve.wait_ge(ld["L1"], 80)
                link(quantise(flat, w8_tmp[0], w8_tmp[1], scales8[:, 1:2]))
                nc.vector.tensor_copy(w8[:, :, :], w8_raw).then_inc(w8_ready, 1)

            def norm_k(c, j, part):
                t = CB * c + j
                v = k_tok.rearrange("p (h d) -> p h d", d=16)
                if part == 0:
                    dve.wait_ge(c_kv, t + 1)
                    if t == 0:
                        dve.wait_ge(ld["L1rows"], 160)
                    else:
                        dve.wait_ge(c_tr, t)
                    kv = bank[4][:, :].rearrange("p (h z d) -> p h z d", z=2, d=16)
                    bias = kv_bias.rearrange("p (h z d) -> p h z d", z=2, d=16)
                    link(tt(v, kv[:, :, 0, :], bias[:, :, 0, :], ALU.add))
                    tt(v_all[:, t, :].rearrange("p (h d) -> p h d", d=16), kv[:, :, 1, :], bias[:, :, 1, :],
                       ALU.add).then_inc(c_v, 1)
                    centre(v, k_tmp.rearrange("p (h d) -> p h d", d=16), 16)
                else:
                    rescale(v, 16, 1e-6, ln_w[:, 16:32].unsqueeze(1), ln_b[:, 16:32].unsqueeze(1), [P, 16, 16])\
                        .then_inc(c_tok, 1)
                    dve.wait_ge(c_tok, t + 1)

            def rope(dst, tmp, src, b):
                pairs = src.rearrange("p (h q e) -> p h q e", q=4, e=2)
                out_ = tmp.rearrange("p (h q e) -> p h q e", q=4, e=2)
                link(tt(dst.rearrange("p (h q) -> p h q", q=8), src.rearrange("p (h q) -> p h q", q=8),
                        cosx[:, b, :, :].rearrange("p q e -> p (q e)").unsqueeze(1).broadcast_to([P, 32, 8]),
                        ALU.mult))
                for e in range(2):
                    link(tt(out_[:, :, :, e], pairs[:, :, :, 1 - e],
                            sinx[:, b, :, e].unsqueeze(1).broadcast_to([P, 32, 4]), ALU.mult))
                return tt(dst, dst, tmp, ALU.add)

            def rope_k(c, j):
                t = CB * c + j
                dve.wait_ge(c_kv, B + t + 1)
                dve.wait_ge(c_tr, B + t)
                i = rope(k_tok, k_tmp, bank[4][:, 0:256], t)
                i.then_inc(c_tok, 1)
                nc.vector.tensor_copy(v_all[:, t, :], bank[4][:, 256:512]).then_inc(c_v, 1)
                dve.wait_ge(c_tok, B + t + 1)

            def subtract_mean(v, mean, m):
                width = v.shape[-1]
                link(nc.vector.tensor_reduce(mean, v, AX, ALU.add))
                link(ts(mean, mean, -1.0 / width, None, ALU.mult))
                link(tt(v, v, mean.unsqueeze(2).broadcast_to([P, m, width]), ALU.add))

            def square_sum(v, t, total):
                link(tt(t, v, v, ALU.mult))
                link(nc.vector.tensor_reduce(total, t, AX, ALU.add))

            def weigh(v, rstd, w, b, shape):
                link(tt(v, v, rstd.unsqueeze(2).broadcast_to(shape), ALU.mult))
                link(tt(v, v, w.broadcast_to(shape), ALU.mult))
                return tt(v, v, b.broadcast_to(shape), ALU.add)

            def centre(v, t, m):
                mean = newton_wide[:, 0, 0:m]
                subtract_mean(v, mean, m)
                square_sum(v, t, mean)

            def rescale(v, m, eps, w, b, shape):
                mean, rstd = newton_wide[:, 0, 0:m], newton_wide[:, 1, 0:m]
                link(rsqrt(rstd, mean, 1.0 / v.shape[-1], eps, m))
                return weigh(v, rstd, w, b, shape)

            def dca_k_norm():
                dve.wait_ge(dca_mm, B + 1)
                link(tt(dca_tok, bank[5][:, 0:256], dca_bias[:, 0:256], ALU.add))
                v = dca_tok.rearrange("p (h d) -> p h d", d=16)
                centre(v, dca_tmp.rearrange("p (h d) -> p h d", d=16), 16)
                link(rescale(v, 16, 1e-6, dca_lnw.unsqueeze(1), dca_lnb.unsqueeze(1), [P, 16, 16]))
                nc.vector.nop().then_inc(dca_norm, 1)

            def dca_k_spread():
                dve.wait_ge(dca_tr, 1)
                for f in range(2):
                    src = bank[5][:, f * P:(f + 1) * P].rearrange("p (b k) -> p b k", b=B)
                    shape = [P, B, 8, 16]
                    tt(kdca[:, f, :, :, :], src.unsqueeze(2).broadcast_to(shape),
                       head_mask[2].unsqueeze(1).unsqueeze(3).broadcast_to(shape), ALU.mult).then_inc(dca_ready, 1)

            def dca_v(b):
                dve.wait_ge(dca_mm, b + 1)
                link(tt(vdca[:, b, :], bank[5][:, 0:256], dca_bias[:, 256:512], ALU.add))
                v = vdca[:, b, :].rearrange("p (f k) -> p f k", f=2)
                tt(v, v, dca_mask.unsqueeze(1).broadcast_to([P, 2, P]), ALU.mult).then_inc(dca_ready, 1)

            def tokens(s, t, part):
                bt = NAR[s].batch_base + t
                if part == 0:
                    dve.wait_ge(n_q, bt + 1)
                    if bt:
                        dve.wait_ge(n_tr, bt)
                v = q_tok.rearrange("p (h d) -> p h d", d=16)
                mean, rstd = newton_wide[:, 0, 0:16], newton_wide[:, 1, 0:16]
                if s == 2 and part == 0:
                    link(tt(q_tok, bank[1][:, 0:256], q_bias, ALU.add))
                    subtract_mean(v, mean, 16)
                elif s == 2 and part == 1:
                    square_sum(v, q_tmp.rearrange("p (h d) -> p h d", d=16), mean)
                elif s == 2 and part == 2:
                    link(rsqrt(rstd, mean, 1.0 / 16, 1e-6, 16))
                elif s == 2:
                    weigh(v, rstd, ln_w[:, 0:16].unsqueeze(1), ln_b[:, 0:16].unsqueeze(1),
                          [P, 16, 16]).then_inc(n_tok, 1)
                    dve.wait_ge(n_tok, bt + 1)
                elif part == 0:
                    rope(q_tok, q_tmp, bank[1][:, 0:256], t).then_inc(n_tok, 1)
                    dve.wait_ge(n_tok, bt + 1)

            def narrow(n):
                s = n // 2
                na = NAR[s]

                def spread_k(t, f):
                    if t == 0:
                        dve.wait_ge(c_kT, na.batch_base + B)
                    else:
                        dve.wait_ge(n_s, na.group_base + (t - 1) * na.n + (f + 1) * na.groups)
                    shape = [P, na.heads, na.keys]
                    tt(kbd[f][:, 0:na.heads * na.keys].rearrange("p (h k) -> p h k", h=na.heads),
                       kT_all[:, t, f, 0:na.keys].unsqueeze(1).broadcast_to(shape),
                       head_mask[s].unsqueeze(2).broadcast_to(shape), ALU.mult).then_inc(n_kbd_v, 1)

                steps = list(na.steps())
                if s == 2:
                    dve.wait_ge(w8_ready, 1)
                own = [f for f in range(2) if na.spread(0, f)[0] == "vector"]
                for f in own:
                    spread_k(0, f)
                tokens(s, 1, 0)
                for i in range(len(steps) + OUT_LAG + 9):
                    if i < len(steps):
                        t, f, g, k, gi = steps[i]
                        dve.wait_ge(n_s, gi + 1)
                        m, w = (16, 16) if f == "dca" else (4, na.keys)
                        sc = bank[3 + gi % 2][:, 0:m * w].rearrange("p (h k) -> p h k", h=m)
                        top = n_max[:, gi % 6, 0:m]
                        link(nc.vector.tensor_reduce(top, sc, AX, ALU.max))
                        if f == "dca":
                            tt(dca_diff.rearrange("p (h k) -> p h k", h=16), sc,
                               top.unsqueeze(2).broadcast_to([P, 16, 16]), ALU.subtract).then_inc(n_nb, 1)
                        else:
                            ts(top, top, -na.scale, None, ALU.mult).then_inc(n_nb, 1)
                    j = i - 1
                    if 0 <= j < len(steps):
                        t, f, g, k, gi = steps[j]
                        dve.wait_ge(n_ex, gi + 1)
                        m = 16 if f == "dca" else 4
                        total = n_sum[:, gi % 6, 0:m]
                        if f == "dca":
                            link(nc.vector.tensor_reduce(
                                total, np_ring[gi % 6][:, 0:256].rearrange("p (h k) -> p h k", h=16), AX, ALU.add))
                        nc.vector.reciprocal(total, total).then_inc(n_rs, 1)
                    for part, later in enumerate((0, 3, 4, 5, 8)):
                        j = i - OUT_LAG - 1 - later
                        if not 0 <= j < len(steps) or steps[j][3] != na.n - 1 or steps[j][0] % 2 == 0:
                            continue
                        t = steps[j][0]
                        m, pair = n + 2 + t // CB, (t % CB - 1, t % CB)
                        if part == 0:
                            residual(n + t // CB, t // 2 % 2)
                        elif part == 1:
                            dve.wait_ge(resid_done, 2 * n + 1 + t // 2)
                            moments(m, pair)
                        elif part == 2:
                            centre_rows(m, pair)
                            if s == 6 and pair[1] == CB - 1:
                                nc.vector.nop().then_inc(ln_done, 1)
                        elif s == 2:
                            quantise_rows(m, pair[part - 3:part - 2])
                    if i == 2:
                        moments(n + 1)
                    if i == 4:
                        normalise(n + 1)
                    j = i - TURN_LAG
                    if 0 <= j < len(steps) and na.turned_copy(steps[j][4])[0] == "vector":
                        t, f, g, k, gi = steps[j]
                        dve.wait_ge(n_ptm, gi + 1)
                        if gi >= 2:
                            dve.wait_ge(n_otm, gi - 1)
                        w, m = (P, 256) if f == "dca" else (na.keys, 512)
                        nc.vector.tensor_copy(npt_ring[gi % 2][0:w, 0:m], bank[5][0:w, 0:m]).then_inc(n_ptc_v, 1)
                    if i < len(steps):
                        t, f, g, k, gi = steps[i]
                        later, part = divmod(i + 1, na.n)
                        if later + 1 < B and part <= 3:
                            tokens(s, later + 1, part)
                        if t + 1 < B:
                            for f in own:
                                if k == min((f + 1) * na.groups, na.n - 1):
                                    spread_k(t + 1, f)

            def angles():
                dve.wait_ge(ld["rows"], 128)
                ts(gqk[:, 2:3], gqk[:, 0:1], gqk[:, 1:2], float(P) ** -0.5, ALU.mult, ALU.mult).then_inc(gqk_set, 1)
                ang, turns, args = trig[:, 0, :], trig[:, 1, :], trig[:, 2:4, :]
                for half, freq in enumerate((1.0, 0.01)):
                    link(ts(ang.rearrange("p (b q e) -> p b q e", b=B, q=2)[:, :, :, half], fside[:, :, :], freq, None,
                            ALU.mult))
                magic = 1.5 * 2.0 ** 23
                link(ts(turns, ang, 1.0 / 6.283185307179586, magic, ALU.mult, ALU.add))
                link(ts(turns, turns, -magic, None, ALU.add))
                link(stt(ang, turns, -6.28125, ang, ALU.mult, ALU.add))
                link(stt(ang, turns, -(6.283185307179586 - 6.28125), ang, ALU.mult, ALU.add))
                link(ts(args[:, 1, :], ang, 1.5707963267948966, None, ALU.add))
                link(ts(turns, args[:, 1, :], 3.1415925, -6.283185307179586, ALU.is_gt, ALU.mult))
                link(tt(args[:, 1, :], args[:, 1, :], turns, ALU.add))
                link(ts(args[:, 1, :], args[:, 1, :], 3.1415925, -3.1415925, ALU.min, ALU.max))
                ts(args[:, 0, :], ang, 3.1415925, -3.1415925, ALU.min, ALU.max).then_inc(trig_arg, 1)

            def rotations():
                dve.wait_ge(trig_sin, 1)
                sin = trig[:, 4, :].rearrange("p (b q) -> p b q", b=B)
                cos = trig[:, 5, :].rearrange("p (b q) -> p b q", b=B)
                link(nc.vector.tensor_copy(cosx[:, :, :, 0], cos))
                link(nc.vector.tensor_copy(cosx[:, :, :, 1], cos))
                link(ts(sinx[:, :, :, 0], sin, -1.0, None, ALU.mult))
                link(nc.vector.tensor_copy(sinx[:, :, :, 1], sin))
                dve.wait_ge(tg_ready, 1)
                link(nc.vector.reciprocal(scales8[:, 2:4], scales8[:, 0:2]))
                link(tt(scales8[:, 2:3], scales8[:, 2:3], scales8[:, 3:4], ALU.mult))
                link(tt(scales8[:, 2:3], scales8[:, 2:3], tg[:, 5:6], ALU.mult))

            newton_wide = trig[:, 0:2, :]
            nc.vector.memset(ones[:, :], 1.0).then_inc(ones_set, 1)
            dve.wait_ge(ld["x"], 16)
            layer_norm(0)
            for n in range(STAGES):
                kind = KIND[n // 2]
                if n == 2:
                    dve.wait_ge(ld["L1rows"], 160)
                if kind == NARROW:
                    if n % 2 == 0:
                        narrow(n)
                    continue
                if kind == WIDE:
                    wide(n)
                elif n >= 14:
                    moe(n)
                elif kind == FFN:
                    ffn(n)
                if n == 0:
                    keys0(1, 0)
                    keys0(1, 1)
                    residual(0, 0)
                    keys0(1, 2)
                    keys0(1, 3)
                    scale_keys0(1)
                    residual(0, 1)
                else:
                    if n in (3, 11):
                        for part in range(4):
                            tokens((n + 1) // 2, 0, part)
                    residual(n, 0)
                    residual(n, 1)
                if n == 6:
                    dve.wait_ge(resid_done, 2 * n + 2)
                    layer_norm(8)


def constants(np):
    c = np.zeros((128, 552), np.float32)
    p = np.arange(128)
    c[:, 0:128] = np.eye(128)
    c[:, 128:144] = p[:, None] // 8 == np.arange(16)
    c[:, 144:152] = p[:, None] // 16 == np.arange(8)
    c[:, 152:280] = p[:, None] // 16 == p[None, :] // 16
    for off, size in ((280, 16), (536, 4)):
        e = np.arange(size)
        c[:, off:off + size * size] = (e[None, :] < e[:, None]).reshape(1, -1)
    return c


def kernel(**inputs):
    import numpy as np
    import concourse.bacc as _bacc
    from concourse import mybir as _mybir
    from concourse.bass_utils import run_bass_kernel_spmd as _run

    v = {k: np.asarray(a) for k, a in inputs.items()}

    def by_rows(w, p=128):
        return w.reshape(-1, p, w.shape[-1]).transpose(1, 0, 2).reshape(p, -1)

    def by_pairs(w):
        return np.concatenate([w[:, 0::2], w[:, 1::2]], 1)

    def pad_rows(w, rows):
        return np.concatenate([w, np.zeros((rows - w.shape[0],) + w.shape[1:], w.dtype)], 0)

    def by_heads(w, heads):
        return w.reshape(w.shape[0], heads, -1).transpose(2, 1, 0).reshape(w.shape[1] // heads, -1)

    i = "L0_ffn_"
    host = {
        "consts": constants(np), "x": v["x"], "ctx": v["ctx_1024"], "fside": v["fside_BxSx2_0"],
        "mask": v["mask_BxS2_bf1"].reshape(-1), "g_xattn": v["g_xattn"], "g_ffn": v["g_ffn"],
        "gq": v["L0_xattn_gq"].reshape(128, 1), "gk": v["L0_xattn_gk"].reshape(128, 1),
        "L0_wq": by_rows(v["L0_xattn_Wq"]), "L0_wk": v["L0_xattn_Wk"],
        "L0_wvT": by_heads(v["L0_xattn_Wv"], 16), "L0_wo": by_rows(v["L0_xattn_Wo"]),
        "ff0_gate": by_pairs(v[i + "gate_W_packed"].T), "ff0_gate_s": by_pairs(v[i + "gate_scales"].T),
        "ff0_up": by_pairs(v[i + "up_W_packed"].T), "ff0_up_s": by_pairs(v[i + "up_scales"].T),
        "ff0_down": by_rows(v[i + "down_W_packed"].T), "ff0_down_s": by_rows(v[i + "down_scales"].T, 8),
        "bq": v["L1_xattn_bq"], "bkv": np.concatenate([v["L1_xattn_bk"], v["L1_xattn_bv"]]),
        "bkv_dca": v["L1_xattn_bkv_dca"], "bo": v["L1_xattn_bo"],
        "L1_wq": by_rows(v["L1_xattn_Wq"]),
        "L1_wkv": np.concatenate([v["L1_xattn_Wk"], v["L1_xattn_Wv"]], 1),
        "L1_dca": v["L1_xattn_Wkv_dca"], "L1_wo": by_rows(v["L1_xattn_Wo"]),
        "w8": by_rows(v["L1_ffn_input2"]), "scale": v["L1_ffn_scale"].reshape(1), "scale1": v["L1_ffn_scale1"].reshape(1),
        "L2_wqT": by_heads(v["L2_xattn_Wq"], 16), "L2_wkT": by_heads(v["L2_xattn_Wk"], 8),
        "L2_wvT": by_heads(v["L2_xattn_Wv"], 8), "L2_wo": by_rows(v["L2_xattn_Wo"]),
        "ff2_gate": by_rows(v["L2_ffn_wq_gate"].T), "ff2_up": by_rows(v["L2_ffn_wq_up"].T),
        "ff2_down": by_rows(pad_rows(v["L2_ffn_wq_down"].T, 768)),
        "s_gate": pad_rows(v["L2_ffn_s_gate"], 768).reshape(6, 128).T,
        "s_up": pad_rows(v["L2_ffn_s_up"], 768).reshape(6, 128).T, "s_down": v["L2_ffn_s_down"],
        "L3_wq": by_rows(v["L3_xattn_Wq"]), "L3_wkv": v["L3_xattn_Wkv"], "L3_wo": by_rows(v["L3_xattn_Wout"]),
        "bout": v["L3_xattn_bout"],
        "moe_w1": by_rows(np.concatenate([v["L3_ffn_w1"], v["L3_ffn_sw1"]]).transpose(1, 0, 2).reshape(256, -1)),
        "moe_w2": by_rows(pad_rows(np.concatenate([v["L3_ffn_w2"], v["L3_ffn_sw2"]]).reshape(-1, 256), 3072)),
        "router": by_rows(v["L3_ffn_gate_w"].T),
    }
    for name in ("qn_w", "qn_b", "kn_w", "kn_b", "kn_dca_w", "kn_dca_b"):
        host[name] = v["L1_xattn_" + name]

    nc = _bacc.Bacc("TRN2", target_bir_lowering=False, num_devices=1)
    arrays, dram = {}, {}
    for name, a in host.items():
        a = np.ascontiguousarray(a)
        arrays["in_" + name] = a
        dram[name] = nc.dram_tensor("in_" + name, a.shape, _mybir.dt.from_np(a.dtype), kind="ExternalInput").ap()
    out = nc.dram_tensor("out_x", (8, 128, 256), _mybir.dt.float32, kind="ExternalOutput").ap()
    build(nc, dram, out)
    r = _run(nc, [arrays], core_ids=[0])
    return r.results[0]["out_x"]
```

```python
from contextlib import ExitStack

import concourse.bass as bass
from concourse import mybir

F32 = mybir.dt.float32
F32R = mybir.dt.float32r
BF16 = mybir.dt.bfloat16
I32 = mybir.dt.int32
U32 = mybir.dt.uint32
U8 = mybir.dt.uint8
ALU = mybir.AluOpType
ACT = mybir.ActivationFunctionType
AX = mybir.AxisListType.X

P = 128
B = 8
CB = 4
CT = CB * P
D = 256
STAGES = 16
WIDE, FFN, NARROW, FP8 = "wide", "ffn", "narrow", "fp8"
KIND = [WIDE, FFN, NARROW, FP8, WIDE, FFN, NARROW, FFN]
HEADS = 16
MOE_H = 176
EXPERTS = 16
MOE_ALL = (EXPERTS + 1) * MOE_H
HID2 = 704
NEG = 1e30
RSQRT_SEED = float(0x5F3759DF)


def tile_sizes(total):
    return [min(P, total - i) for i in range(0, total, P)]


TILES = {1: tile_sizes(2048), 5: tile_sizes(HID2), 7: tile_sizes(MOE_ALL)}
FFN_BASE = {n: sum(len(TILES[m // 2]) for m in range(n) if m // 2 in TILES) for n in range(STAGES)}
DOWN_BASE = {n: FFN_BASE[n] - sum(m // 2 in TILES for m in range(n)) for n in range(STAGES)}


TURN_LAG, OUT_LAG = 4, 5


class Narrow:

    def __init__(self, s):
        self.s = s
        self.hd = 16 if s == 2 else 8
        self.heads = P // self.hd
        self.keys = 112 if s == 2 else 128
        self.scale = float(self.hd) ** -0.5
        self.groups = self.heads // 4
        order = [(f, g) for f in range(2) for g in range(self.groups)]
        self.order = order + [("dca", 0)] * (s == 2)
        self.n = len(self.order)
        self.q_step = 3
        self.batch_base = 0 if s == 2 else B
        self.group_base = 0 if s == 2 else 5 * B
        mid, late = CB * self.n // 2, CB * self.n + 3 * self.n
        self.turn_steps = {mid: (1, 0), mid + 2: (1, 1), late: (2, 0), late + 2: (2, 1)}

    def turned_copy(self, gi):
        if gi < 5 * B:
            return "scalar", gi + 1
        gi -= 5 * B
        return ("scalar", 5 * B + gi // 2 + 1) if gi % 2 else ("vector", gi // 2 + 1)

    def spread(self, t, f):
        if self.s == 2:
            return "gpsimd", 2 * t + f + 1
        return ("gpsimd", 2 * B + t + 1) if f else ("vector", t + 1)

    def steps(self):
        for t in range(B):
            for k, (f, g) in enumerate(self.order):
                yield t, f, g, k, self.group_base + t * self.n + k


DOWN_LAG, FF2_DOWN_LAG = 2, 3
X_SPLIT = {2: 0, 3: 1, 8: 2, 9: 3, 10: 4, 11: 5, 14: 6, 15: 7}
SPLIT = {10: 0, 11: 1, 14: 2, 15: 3}
SPLIT_BASE = {n: sum(len(TILES[m // 2]) for m in SPLIT if m < n) for n in SPLIT}
Y_BANKS = {10: (1, 3), 11: (0, 5), 14: (4, 5), 15: (4, 5)}
MOE_LEAD, MOE_DOWN_LAG = 10, 3
MOE_TILES = len(TILES[7])


def build(nc, dram, out):
    with ExitStack() as ctx:
        def sb(name, shape, dt=F32):
            return ctx.enter_context(nc.sbuf_tensor(name, shape, dt))

        sems = {}

        def sem(name):
            sems[name] = ctx.enter_context(nc.semaphore(name))
            return sems[name]

        bank = [ctx.enter_context(nc.psum_tensor(f"bank{i}", [P, 512], F32)) for i in range(8)]

        consts = sb("consts", [P, 552])
        ident = consts[:, 0:128]
        head_mask = {6: consts[:, 128:144], 2: consts[:, 144:152]}
        dca_mask = consts[:, 152:280]
        tie16 = consts[:, 280:536].rearrange("p (e j) -> p e j", e=16)
        tie4 = consts[:, 536:552].rearrange("p (e j) -> p e j", e=4)
        ones = sb("ones", [P, P])
        x_sb = sb("x_sb", [P, B, D])
        xn = sb("xn", [P, 2, CB, D])
        xT = sb("xT", [P, 2, 2, CT])
        xqT = sb("xqT", [P, 2, CT], BF16)
        w8 = sb("w8", [P, 2, D], BF16)
        ctx_tok = sb("ctx_tok", [P, B, P])
        ctxT = sb("ctxT", [P, B, P])
        mask8 = sb("mask8", [P, B * P], U8)
        gates = sb("gates", [P, 8])
        tg = sb("tg", [P, 8])
        scales8 = sb("scales8", [P, 4])
        gqk = sb("gqk", [P, 3])
        qn_col = sb("qn_col", [P, 2])
        fside = sb("fside", [P, B, 2])
        trig = sb("trig", [P, 6, B * 4])
        cosx = sb("cosx", [P, B, 4, 2])
        sinx = sb("sinx", [P, B, 4, 2])
        ffn2_scale = sb("ffn2_scale", [P, 2, 6])
        stats = sb("stats", [P, CB, 6])
        mv = sb("mv", [P, CB, 2])
        x_rstd = sb("x_rstd", [P, CB])
        newton = sb("newton", [P, 3, 64])
        q_rstd = sb("q_rstd", [P, HEADS, CB])
        neg_max = sb("neg_max", [P, HEADS, CB])
        row_sum = sb("row_sum", [P, HEADS, CB])
        k_ss = sb("k_ss", [P, HEADS, CB])
        any_valid = sb("any_valid", [P, B])
        n_max = sb("n_max", [P, 6, 16])
        n_sum = sb("n_sum", [P, 6, 16])
        score = sb("score", [P, CB, 16])
        route = sb("route", [P, 8, CB * 16])

        sizes = {"A": 10240, "Bw": 12288, "H": 8192, "S": 5120, "R": 4608, "X": 1024}
        with ExitStack() as regions:
            A, Bw, H, S, R, X = (regions.enter_context(nc.sbuf_tensor(name, [P, cols], F32))
                                 for name, cols in sizes.items())
        A_r, Bw_r, H_r, S_r, R_r, X_r = (sb(name + "_r", [P, cols], F32R) for name, cols in sizes.items())

        def ring(region, off, n, cols=512):
            return [region[:, off + i * cols:off + (i + 1) * cols] for i in range(n)]

        def split(ap, pattern, **kw):
            return ap.rearrange(pattern, **kw)

        q_ring, q2_ring, p_ring, pt_ring = ring(S, 0, 2), ring(S, 1024, 2), ring(S, 2048, 4), ring(S, 4096, 2)
        heads = split(H[:, :], "p (h t) -> p h t", h=HEADS)
        L0_wq = split(A[:, 0:4096], "p (f n) -> p f n", f=2)
        L0_wk = A[:, 4096:6144]
        out_w = {0: split(A[:, 6144:10240], "p (h n) -> p h n", h=HEADS),
                 4: split(A[:, 4096:8192], "p (h n) -> p h n", h=HEADS)}
        L0_wvT = split(Bw[:, 6144:8192], "p (h n) -> p h n", h=HEADS)
        L0_wo = split(Bw[:, 8192:12288], "p (h n) -> p h n", h=HEADS)
        L2_m = split(A[:, 0:4096], "p (f h n) -> p f h n", f=2, h=HEADS)
        L2_wqT = split(Bw[:, 0:4096], "p (h n) -> p h n", h=HEADS)
        L2_wkT = split(Bw[:, 4096:5120], "p (h n) -> p h n", h=8)
        L2_wvT = split(Bw[:, 5120:6144], "p (h n) -> p h n", h=8)
        L2_wo = split(Bw[:, 6144:10240], "p (h n) -> p h n", h=HEADS)
        mask_bias = R[:, 0:1024]
        h_ring = ring(S, 1024, 3)
        act_ring = ring(S, 0, 2)
        ff0 = [split(Bw[:, 4096 * i:4096 * (i + 1)], "p (k n) -> p k n", k=2) for i in range(3)]
        ff0_down = split(Bw[:, 8192:12288], "p (m n) -> p m n", n=D)
        down_scale = R[:, 1024:1280]
        fp4_slot = [(R[:, 1024 * i:1024 * i + 512].bitcast(U32), R[:, 1024 * i + 512:1024 * i + 1024]) for i in range(3)]
        fp4_tmp = ring(R, 3072, 2)
        nq = {2: split(A[:, 0:512], "p (k n) -> p k n", k=2), 6: split(Bw[:, 4352:4864], "p (k n) -> p k n", k=2)}
        nkv = {2: A[:, 512:1024], 6: Bw[:, 4864:5376]}
        nout = {2: split(A[:, 1536:2048], "p (k n) -> p k n", k=2), 6: split(Bw[:, 5376:5888], "p (k n) -> p k n", k=2)}
        dca_w = A[:, 1024:1536]
        kdca = split(A[:, 2048:4096], "p (f b h k) -> p f b h k", f=2, b=B, h=8)
        vdca = split(A[:, 4096:6144], "p (b n) -> p b n", b=B)
        kT_all = split(A[:, 6144:8192], "p (b f k) -> p b f k", b=B, f=2)
        v_all = split(A[:, 8192:10240], "p (b n) -> p b n", b=B)
        w8_raw = split(H[:, 0:512], "p (k n) -> p k n", k=2)
        w8_tmp, q8_tmp = ring(H, 512, 2), ring(Bw, 10240, 2, 1024)
        dca_tok, dca_tmp = H[:, 1536:1792], H[:, 1792:2048]
        dca_ctx = H[:, 2048:2176]
        dca_ctx8 = split(H[:, 2176:3200], "p (b k) -> p b k", b=B)
        k_tok, k_tmp = H[:, 3200:3456], H[:, 3456:3712]
        q_bias, kv_bias = R[:, 0:256], R[:, 256:768]
        dca_bias = R[:, 768:1280]
        kn_w, kn_b = R[:, 1280:1296], R[:, 1296:1312]
        dca_lnw, dca_lnb = R[:, 1344:1360], R[:, 1360:1376]
        out_bias = {2: R[:, 1376:1632], 6: R[:, 1280:1536]}
        q_tok, q_tmp, dca_diff = S[:, 0:256], S[:, 512:768], S[:, 1024:1280]
        np_ring, npt_ring = ring(S, 2048, 6), ring(R, 3072, 2)
        nqT = ring(X, 0, 2, 256)
        n_out = X[:, 512:768]
        kbd = [H[:, 2048 * f:2048 * (f + 1)] for f in range(2)]
        vpad = [H[:, 4096 + 2048 * f:4096 + 2048 * (f + 1)] for f in range(2)]
        w1_cols, w2_at = 2 * MOE_ALL, 2 * MOE_ALL + 32
        moe_w1, w1_lo, w1_hi = (split(t[:, 0:w1_cols], "p (k n) -> p k n", k=2) for t in (A, A_r, Bw_r))
        router_w = split(Bw[:, w1_cols:w2_at], "p (k n) -> p k n", k=2)
        moe_w2, w2_lo = (split(t[:, w2_at:w2_at + D * MOE_TILES], "p (m n) -> p m n", n=D) for t in (Bw, Bw_r))

        def w2_high(a, h, m):
            return a[:, w1_cols + D * m:w1_cols + D * (m + 1)] if m < 16 else h[:, D * (m + 4):D * (m + 5)]

        moe_act = ring(H, 0, 10) + ring(H, 7168, 2)
        moe_h, h_lo_ring, h_hi_ring = ring(S, 1024, 4), ring(S_r, 1024, 4), ring(S_r, 3072, 4)
        ff0_lo = [split(Bw_r[:, 4096 * i:4096 * (i + 1)], "p (k n) -> p k n", k=2) for i in range(2)]
        gate_hi = split(H_r[:, 4096:8192], "p (k n) -> p k n", k=2)

        def ff0_high(which, i):
            if which == 0:
                return gate_hi[:, :, i * P:(i + 1) * P]
            at = R_r[:, 1632 + 256 * i:1888 + 256 * i] if i < 11 else S_r[:, 768 + 256 * i:1024 + 256 * i]
            return split(at, "p (k n) -> p k n", k=2)

        L2_m_lo = split(A_r[:, 0:4096], "p (f h n) -> p f h n", f=2, h=HEADS)
        x_hi4 = split(S_r[:, 1024:2048], "p (f t) -> p f t", f=2)

        def L2_m_high(h):
            at = A_r[:, 8192 + 256 * h:8448 + 256 * h] if h < 8 else R_r[:, 256 * h - 512:256 * h - 256]
            return split(at, "p (f n) -> p f n", f=2)

        demean = S[:, 4864:4992]
        ff2_gate, ff2_up = (split(Bw_r[:, lo:lo + 1408], "p (k n) -> p k n", k=2) for lo in (0, 1408))
        ff2_down = split(Bw_r[:, 2816:4352], "p (m n) -> p m n", n=D)
        x_hi2, h_hi_ring2 = split(S_r[:, 2560:3584], "p (f t) -> p f t", f=2), ring(S_r, 3584, 3)
        x_hi, x_lo = (split(t[:, 0:1024], "p (f t) -> p f t", f=2) for t in (S_r, X_r))
        yT = ring(R, 0, 2)
        sel = R[:, 1536:1536 + MOE_ALL // 2].bitcast(BF16)
        comb_tok = split(R[:, 3072:3584], "p (b e) -> p b e", b=CB)
        combT = R[:, 3584:3840].bitcast(BF16)
        route_a = split(S[:, 3072:4096], "p (b e j) -> p b e j", b=CB, e=16)
        route_b = split(S[:, 4096:5120], "p (b e j) -> p b e j", b=CB, e=16)

        ld = {k: sem("ld_" + k) for k in (
            "const", "x", "x1", "ctx", "rows", "wq0", "wk0", "wvo0", "fp4_0", "fp4_1", "fp4_2", "L1", "L1rows",
            "L2", "late", "ff2", "moe1")}
        v_chain, tg_ready = sem("v_chain"), sem("tg_ready")
        ones_set, sel_chain, ctxT_mm, ctxT_cp, trig_arg, trig_sin = (
            sem("ones_set"), sem("sel_chain"), sem("ctxT_mm"), sem("ctxT_cp"), sem("trig_arg"), sem("trig_sin"))
        pre_mm, pre_cp = sem("pre_mm"), sem("pre_cp")
        fp4_done, ff2_cast, w8_ready = sem("fp4_done"), sem("ff2_cast"), sem("w8_ready")
        ln_done, xT_mm, xT_cp = sem("ln_done"), sem("xT_mm"), sem("xT_cp")
        y_ready, resid_done, stored = sem("y_ready"), sem("resid_done"), sem("stored")
        k_mm, k_sq, k_cp, k_red, k_rstd, k_scaled_v, k_scaled_g, kT_mm, kT_cp = (
            sem("k_mm"), sem("k_sq"), sem("k_cp"), sem("k_red"), sem("k_rstd"), sem("k_scaled_v"),
            sem("k_scaled_g"), sem("kT_mm"), sem("kT_cp"))
        q_mm, q_cp, q_sq, ss_mm, s_mm, nb, ex, rs, p_norm, pt_mm, pt_cp, ot_mm, ot_cp = (
            sem("q_mm"), sem("q_cp"), sem("q_sq"), sem("ss_mm"), sem("s_mm"), sem("nb"), sem("ex"), sem("rs"),
            sem("p_norm"), sem("pt_mm"), sem("pt_cp"), sem("ot_mm"), sem("ot_cp"))
        centring, wq_mm, wq_cp = sem("centring"), sem("wq_mm"), sem("wq_cp")
        mask_set, gqk_set, ss_read = sem("mask_set"), sem("gqk_set"), sem("ss_read")
        g_mm, u_mm, g_act, h_done, d_mm = sem("g_mm"), sem("u_mm"), sem("g_act"), sem("h_done"), sem("d_mm")
        c_kv, c_tok, c_v, c_tr, c_kT = sem("c_kv"), sem("c_tok"), sem("c_v"), sem("c_tr"), sem("c_kT")
        (n_q, n_tok, n_tr, n_qT, n_kbd_v, n_kbd_g, n_vpad, n_s, n_nb, n_ex, n_rs, n_pn, n_ptm, n_ptc_v, n_ptc_a,
         n_otm, n_otc, vpad_zero) = (
            sem("n_q"), sem("n_tok"), sem("n_tr"), sem("n_qT"), sem("n_kbd_v"), sem("n_kbd_g"), sem("n_vpad"),
            sem("n_s"), sem("n_nb"), sem("n_ex"), sem("n_rs"), sem("n_pn"), sem("n_ptm"), sem("n_ptc_v"),
            sem("n_ptc_a"), sem("n_otm"), sem("n_otc"), sem("vpad_zero"))
        dca_copied = sem("dca_copied")
        dca_mm, dca_tr, dca_norm, dca_ready = sem("dca_mm"), sem("dca_tr"), sem("dca_norm"), sem("dca_ready")
        x_high, x_low, w_high, w_low, h_high, h_low, w0_high, w0_low, m_high, m_low, moe_d, ff2_d, yT_act, yT_dve = (
            sem("x_high"), sem("x_low"), sem("w_high"), sem("w_low"), sem("h_high"), sem("h_low"), sem("w0_high"),
            sem("w0_low"), sem("m_high"), sem("m_low"), sem("moe_d"), sem("ff2_d"),
            sem("yT_act"), sem("yT_dve"))
        r_mm, r_sig, r_comb, r_tr, r_combT = (
            sem("r_mm"), sem("r_sig"), sem("r_comb"), sem("r_tr"), sem("r_combT"))

        NAR = {s: Narrow(s) for s in (2, 6)}

        def turn_bank(n, f):
            if n == 0 or KIND[(n - 1) // 2] in (WIDE, FP8):
                return f
            if KIND[(n - 1) // 2] == NARROW:
                return 2
            return 4 + f
        DCA_V_STEPS = [3, 4, 6, 7, 9, 10, 12, 13]
        WIDE_INDEX = {0: 0, 1: 1, 8: 2, 9: 3}

        block = ctx.enter_context(nc.Block())

        @block.sync
        def _(sp):
            def load(dst, src, what):
                sp.dma_start(dst, src).then_inc(ld[what], 16)

            load(consts[:, :], dram["consts"], "const")
            load(ctx_tok[:, :, :], dram["ctx"].rearrange("b p d -> p b d"), "ctx")
            load(x_sb[:, 0:CB, :], dram["x"][0:CB].rearrange("b p d -> p b d"), "x")
            load(L0_wk, dram["L0_wk"], "wk0")
            load(A[:, 0:4096], dram["L0_wq"], "wq0")
            load(gates[:, 0:4], dram["g_xattn"].partition_broadcast(P), "rows")
            load(gates[:, 4:8], dram["g_ffn"].partition_broadcast(P), "rows")
            load(gqk[:, 0:1], dram["gq"], "rows")
            load(gqk[:, 1:2], dram["gk"], "rows")
            load(qn_col[:, 0:1], dram["qn_w_col"], "rows")
            load(qn_col[:, 1:2], dram["qn_b_col"], "rows")
            load(mask8[:, :], dram["mask"].partition_broadcast(P), "rows")
            load(fside[:, :, :], dram["fside"].rearrange("b p d -> p b d"), "rows")
            load(scales8[:, 0:1], dram["scale"].partition_broadcast(P), "rows")
            load(scales8[:, 1:2], dram["scale1"].partition_broadcast(P), "rows")
            load(Bw[:, 6144:8192], dram["L0_wvT"], "wvo0")
            load(Bw[:, 8192:12288], dram["L0_wo"], "wvo0")
            load(x_sb[:, CB:B, :], dram["x"][CB:B].rearrange("b p d -> p b d"), "x1")
            for p in range(12):
                if p >= 3:
                    sp.wait_ge(fp4_done, 2 * (p - 2))
                name, cols = ("gate", "up", "down")[p // 4], slice(512 * (p % 4), 512 * (p % 4) + 512)
                packed, scale = fp4_slot[p % 3]
                load(packed.bitcast(I32), dram[f"ff0_{name}"][:, cols], f"fp4_{p % 3}")
                load(scale,
                     dram[f"ff0_{name}_s"][:, cols].unsqueeze(1).broadcast_to([8, 16, 512]), f"fp4_{p % 3}")
            sp.wait_ge(fp4_done, 24)
            for dst, name in ((q_bias, "bq"), (kv_bias, "bkv"), (dca_bias, "bkv_dca"), (kn_w, "kn_w"), (kn_b, "kn_b"),
                             
                              (dca_lnw, "kn_dca_w"), (dca_lnb, "kn_dca_b"), (out_bias[2], "bo")):
                load(dst, dram[name].partition_broadcast(P), "L1rows")
            sp.wait_ge(y_ready, 4)
            load(A[:, 0:512], dram["L1_wq"], "L1")
            load(A[:, 512:1024], dram["L1_wkv"], "L1")
            load(A[:, 1024:1536], dram["L1_dca"], "L1")
            load(A[:, 1536:2048], dram["L1_wo"], "L1")
            load(H[:, 0:512], dram["w8"], "L1")
            sp.wait_ge(y_ready, 8)
            load(Bw[:, 0:4096], dram["L2_wqT"], "L2")
            load(Bw[:, 4096:5120], dram["L2_wkT"], "L2")
            load(Bw[:, 5120:6144], dram["L2_wvT"], "L2")
            load(Bw[:, 6144:10240], dram["L2_wo"], "L2")
            sp.wait_ge(resid_done, 12)
            load(down_scale, dram["s_down"].partition_broadcast(P), "late")
            load(out_bias[6], dram["bout"].partition_broadcast(P), "late")
            load(ffn2_scale[:, 0, :], dram["s_gate"], "late")
            load(ffn2_scale[:, 1, :], dram["s_up"], "late")
            sp.wait_ge(pre_mm, 24)
            sp.wait_ge(ln_done, 8)
            load(Bw[:, 0:1408].bitcast(I32), dram["ff2_gate"], "ff2")
            load(Bw[:, 1408:2816].bitcast(I32), dram["ff2_up"], "ff2")
            load(Bw[:, 2816:4352].bitcast(I32), dram["ff2_down"], "ff2")
            load(Bw[:, 4352:4864], dram["L3_wq"], "ff2")
            load(Bw[:, 4864:5376], dram["L3_wkv"], "ff2")
            load(Bw[:, 5376:5888], dram["L3_wo"], "ff2")
            load(Bw[:, w2_at:w2_at + D * MOE_TILES], dram["moe_w2"], "ff2")
            load(Bw[:, w1_cols:w2_at], dram["router"], "ff2")
            sp.wait_ge(y_ready, 20)
            load(A[:, 0:w1_cols], dram["moe_w1"], "moe1")
            for c in range(2):
                for j in range(2):
                    sp.wait_ge(resid_done, 2 * (14 + c) + j + 1)
                    b = CB * c + 2 * j
                    sp.dma_start(out[b:b + 2].rearrange("b p d -> p b d"), x_sb[:, b:b + 2, :]).then_inc(stored, 16)
            sp.wait_ge(stored, 64)

        @block.tensor
        def _(pe):
            def transpose_x(n, f):
                c = n % 2
                pe.wait_ge(ln_done, n + 1)
                for b in range(CB):
                    src = xn[:, c, b, f::2] if n // 2 == 1 else xn[:, c, b, f * P:(f + 1) * P]
                    mm = nc.tensor.transpose(bank[turn_bank(n, f)][:, b * P:(b + 1) * P], src, ident)
                mm.then_inc(xT_mm, 1)

            def keys0(a, b):
                for g in range(4):
                    u = 4 * b + g
                    if u >= 2:
                        pe.wait_ge(k_cp, 16 * a + u - 1)
                    nc.tensor.matmul(bank[2 + u % 2][:, :], ctxT[:, CB * a + b, :], L0_wk[:, 512 * g:512 * g + 512],
                                     start=True, stop=True).then_inc(k_mm, 1)

            def weight_products(which):
                units = [("n", i) for i in range(8)] if which == 0 else [("m", i) for i in range(8)] + [("n", i) for i in range(8)]
                base = 0 if which == 0 else 8
                for u, (kind, i) in enumerate(units):
                    if base + u >= 4:
                        pe.wait_ge(pre_cp, base + u - 3)
                    dst = bank[2 + (base + u) % 4]
                    for j in range(2):
                        h = 2 * i + j
                        if kind == "n":
                            wv = L0_wvT[:, h, :] if which == 0 else L2_wvT[:, h // 2, :]
                            wo = L0_wo[:, h, :] if which == 0 else L2_wo[:, h, :]
                            mm = nc.tensor.matmul(dst[:, j * 256:(j + 1) * 256], wv, wo, start=True, stop=True)
                        else:
                            for f in range(2):
                                mm = nc.tensor.matmul(dst[:, f * 256 + j * 128:f * 256 + (j + 1) * 128],
                                                      L2_wqT[:, h, f * P:(f + 1) * P], L2_wkT[:, h // 2, :],
                                                      start=True, stop=True)
                    mm.then_inc(pre_mm, 1)

            def wide(n):
                a, c, s = WIDE_INDEX[n], n % 2, n // 2
                base = HEADS * a
                if s == 0:
                    if a == 0:
                        pe.wait_ge(ld["wk0"], 16)
                        for b in range(CB):
                            keys0(0, b)
                        for f in range(2):
                            transpose_x(0, f)
                        pe.wait_ge(ld["wvo0"], 32)
                        pe.wait_ge(k_cp, 16)
                        weight_products(0)
                        pe.wait_ge(ones_set, 1)
                        pe.wait_ge(pre_cp, 8)
                        pe.wait_ge(ld["wq0"], 16)
                    pe.wait_ge(k_cp, 16 * a + 16)
                else:
                    pe.wait_ge(pre_cp, 24)
                pe.wait_ge(xT_cp, 2 * n + 2)

                def outputs(batches, some_heads):
                    for b in batches:
                        for h in some_heads:
                            mm = nc.tensor.matmul(bank[6 + b // 2][:, (b % 2) * D:(b % 2 + 1) * D],
                                                  heads[:, h, b * P:(b + 1) * P], out_w[s][:, h, :],
                                                  start=(h == 0 and b % 2 == 0), stop=(h == HEADS - 1),
                                                  skip_group_check=True)
                    return mm

                for i in range(HEADS + 4):
                    if i < HEADS:
                        if i:
                            pe.wait_ge(q_sq if s == 0 else q_cp, base + i)
                        if s != 0:
                            pe.wait_ge(x_low, X_SPLIT[n] + 1)
                            pe.wait_ge(m_low, i + 1)
                        for f in range(2):
                            if s == 0:
                                mm = nc.tensor.matmul(bank[0][:, :], L0_wq[:, f, i * P:(i + 1) * P], xT[:, c, f, :],
                                                      start=(f == 0), stop=(f == 1))
                                continue
                            high, low = L2_m_high(i)[:, f, :], L2_m_lo[:, f, i, :]
                            for q, (weights, x) in enumerate(((high, x_hi4), (low, x_hi4), (high, x_lo))):
                                mm = nc.tensor.matmul(bank[0][:, :], weights, x[:, f, :],
                                                      start=(f == 0 and q == 0), stop=(f == 1 and q == 2))
                        mm.then_inc(q_mm, 1)
                        if s == 0:
                            pe.wait_ge(k_scaled_g if i % 2 else k_scaled_v, 8 * a + i // 2 + 1)
                            if i:
                                pe.wait_ge(kT_cp, base + i)
                            for b in range(CB):
                                mm = nc.tensor.transpose(bank[1][:, b * P:(b + 1) * P],
                                                         heads[:, i, b * P:(b + 1) * P], ident)
                            mm.then_inc(kT_mm, 1)
                    h = i - 1
                    if 0 <= h < HEADS:
                        qT = q_ring[h % 2]
                        if s == 0:
                            pe.wait_ge(q_sq, base + h + 1)
                            if h == 0:
                                pe.wait_ge(resid_done, 2 * n)
                            else:
                                pe.wait_ge(ss_read, base + h)
                            for b in range(CB):
                                mm = nc.tensor.matmul(bank[6][:, b * P:(b + 1) * P],
                                                      q2_ring[h % 2][:, b * P:(b + 1) * P], ones[:, :],
                                                      start=True, stop=True)
                            mm.then_inc(ss_mm, 1)
                            pe.wait_ge(kT_cp, base + h + 1)
                        else:
                            pe.wait_ge(q_cp, base + h + 1)
                        if h >= 2:
                            pe.wait_ge(ex, base + h - 1)
                        for b in range(CB):
                            keys = heads[:, h, b * P:(b + 1) * P] if s == 0 else ctxT[:, CB * c + b, :]
                            mm = nc.tensor.matmul(bank[2 + h % 2][:, b * P:(b + 1) * P], qT[:, b * P:(b + 1) * P],
                                                  keys, start=True, stop=True)
                        mm.then_inc(s_mm, 1)
                    if i > HEADS:
                        if i == HEADS + 1:
                            if s == 0:
                                pe.wait_ge(ss_read, base + HEADS)
                            pe.wait_ge(ot_cp, base + 12)
                        outputs(range(2), range(4 * (i - HEADS - 1), 4 * (i - HEADS)))
                    h = i - 3
                    if 0 <= h < HEADS:
                        pe.wait_ge(p_norm, base + h + 1)
                        if h:
                            pe.wait_ge(pt_cp, base + h)
                        for b in range(CB):
                            mm = nc.tensor.transpose(bank[4][:, b * P:(b + 1) * P],
                                                     p_ring[h % 4][:, b * P:(b + 1) * P], ident)
                        mm.then_inc(pt_mm, 1)
                    h = i - 4
                    if 0 <= h < HEADS:
                        pe.wait_ge(pt_cp, base + h + 1)
                        if h == 0:
                            pe.wait_ge(resid_done, 2 * n)
                        if h >= 2:
                            pe.wait_ge(ot_cp, base + h - 1)
                        for b in range(CB):
                            mm = nc.tensor.matmul(bank[5 + 2 * (h % 2)][:, b * P:(b + 1) * P],
                                                  ctx_tok[:, CB * c + b, :], pt_ring[h % 2][:, b * P:(b + 1) * P],
                                                  start=True, stop=True)
                        mm.then_inc(ot_mm, 1)
                for f in range(2):
                    transpose_x(n + 1, f)
                pe.wait_ge(ot_cp, base + HEADS)
                for b in range(CB):
                    mm = outputs([b], range(12 if b < 2 else 0, HEADS))
                    if b % 2:
                        mm.then_inc(y_ready, 1)
                    if n == 0:
                        keys0(1, b)

            def project_kv(n, j):
                s, c = n // 2 + 1, n % 2
                bt = NAR[s].batch_base + CB * c + j
                if j == 0:
                    pe.wait_ge(ld["L1"] if s == 2 else ld["ff2"], 80 if s == 2 else 128)
                    pe.wait_ge(xT_cp, 2 * n + 2)
                if bt:
                    pe.wait_ge(c_v, bt)
                nc.tensor.matmul(bank[4][:, :], ctxT[:, CB * c + j, :], nkv[s], start=True, stop=True)\
                    .then_inc(c_kv, 1)

            def turn_k(n, j):
                s, c = n // 2 + 1, n % 2
                bt = NAR[s].batch_base + CB * c + j
                pe.wait_ge(c_tok, bt + 1)
                if bt:
                    pe.wait_ge(c_kT, bt)
                if s == 2:
                    pe.wait_ge(dca_ready, B + 2 if c else 2 * j + 2)
                for f in range(2):
                    mm = nc.tensor.transpose(bank[5][:, f * P:(f + 1) * P], k_tok[:, f * P:(f + 1) * P], ident)
                mm.then_inc(c_tr, 1)

            def dca(n, i):
                if n == 2 and i in DCA_V_STEPS:
                    b = DCA_V_STEPS.index(i)
                    if b == 0:
                        pe.wait_ge(ld["L1"], 80)
                        pe.wait_ge(dca_copied, 2)
                    else:
                        pe.wait_ge(dca_ready, b)
                    if b >= 2:
                        pe.wait_ge(c_kT, b // 2)
                    nc.tensor.matmul(bank[5][:, 0:256], dca_ctx8[:, b, :], dca_w[:, 256:512],
                                     start=True, stop=True).then_inc(dca_mm, 1)
                if n == 3 and i == 0:
                    pe.wait_ge(xT_cp, 8)
                    nc.tensor.matmul(bank[5][:, 0:256], dca_ctx, dca_w[:, 0:256], start=True, stop=True)\
                        .then_inc(dca_mm, 1)
                if n == 3 and i == 4:
                    pe.wait_ge(dca_norm, 1)
                    for f in range(2):
                        mm = nc.tensor.transpose(bank[5][:, f * P:(f + 1) * P], dca_tok[:, f * P:(f + 1) * P], ident)
                    mm.then_inc(dca_tr, 1)

            def project(n, t):
                bt = NAR[n // 2].batch_base + t
                if bt:
                    pe.wait_ge(n_tok, bt)
                if t % CB == 0:
                    pe.wait_ge(xT_cp, 2 * n + 2 + 2 * (t // CB))
                for f in range(2):
                    mm = nc.tensor.matmul(bank[1][:, 0:256], xT[:, t // CB, f, (t % CB) * P:(t % CB + 1) * P],
                                          nq[n // 2][:, f, :], start=(f == 0), stop=(f == 1))
                mm.then_inc(n_q, 1)

            def ffn(n):
                s, c = n // 2, n % 2
                base, tiles = FFN_BASE[n], TILES[s]
                pe.wait_ge(x_low, X_SPLIT[n] + 1)
                size = len(tiles)
                for i in range(size + DOWN_LAG):
                    if i < size:
                        pe.wait_ge(w0_low, i + 1)
                        if i >= 2:
                            pe.wait_ge(g_act, base + i - 1)
                            pe.wait_ge(h_done, base + i - 1)
                        for which, counts in enumerate((g_mm, u_mm)):
                            high, low = ff0_high(which, i), ff0_lo[which][:, :, i * P:(i + 1) * P]
                            for f in range(2):
                                for q, (weights, x) in enumerate(((high, x_hi2), (low, x_hi2), (high, x_lo))):
                                    mm = nc.tensor.matmul(bank[2 * which + i % 2][:, :], weights[:, f, :], x[:, f, :],
                                                          start=(f == 0 and q == 0), stop=(f == 1 and q == 2))
                            mm.then_inc(counts, 1)
                    dca(n, i)
                    if n == 2 and i == 1:
                        pe.wait_ge(ld["L1"], 80)
                        pe.wait_ge(centring, 1)
                        for fi in range(2):
                            for fo in range(2):
                                mm = nc.tensor.matmul(bank[4][:, fi * D + fo * P:fi * D + (fo + 1) * P],
                                                      nq[2][:, fo, fi * P:(fi + 1) * P], demean,
                                                      start=True, stop=True)
                        mm.then_inc(wq_mm, 1)
                        pe.wait_ge(wq_cp, 1)
                    j, part = divmod(i - 2, 3)
                    if part == 0 and 1 <= j <= CB:
                        turn_k(n, j - 1)
                    if part == 0 and 0 <= j < CB:
                        project_kv(n, j)
                    if i == size:
                        pe.wait_ge(c_v, NAR[s + 1].batch_base + CB * c + CB)
                        pe.wait_ge(c_kT, NAR[s + 1].batch_base + CB * c + CB)
                        for f in range(2):
                            transpose_x(n + 1, f)
                    m = i - DOWN_LAG
                    if m == size - 1 and c:
                        project(n + 1, 0)
                    if m >= 0:
                        w = tiles[m]
                        pe.wait_ge(h_done, base + m + 1)
                        if m == 0:
                            pe.wait_ge(resid_done, 2 * n)
                        for b in range(CB):
                            mm = nc.tensor.matmul(bank[6 + b // 2][:, (b % 2) * D:(b % 2 + 1) * D],
                                                  h_ring[m % 3][0:w, b * P:(b + 1) * P], ff0_down[0:w, m, :],
                                                  start=(m == 0 and b % 2 == 0), stop=(m == size - 1),
                                                  skip_group_check=True)
                            if m == size - 1 and b % 2:
                                mm.then_inc(y_ready, 1)
                            elif m < size - 1 and b == CB - 1:
                                mm.then_inc(d_mm, 1)

            def moe(n):
                c, k, base, tiles = n % 2, n - 14, FFN_BASE[n], TILES[7]
                size = MOE_TILES
                pe.wait_ge(ld["ff2"], 128)
                pe.wait_ge(xT_cp, 2 * n + 2)
                for b in range(CB):
                    for f in range(2):
                        mm = nc.tensor.matmul(bank[2][:, b * 16:(b + 1) * 16], xT[:, c, f, b * P:(b + 1) * P],
                                              router_w[:, f, :], start=(f == 0), stop=(f == 1))
                mm.then_inc(r_mm, 1)
                for i in range(size + MOE_LEAD + MOE_DOWN_LAG):
                    if i < size:
                        w = tiles[i]
                        if i == 0:
                            pe.wait_ge(x_low, X_SPLIT[n] + 1)
                        pe.wait_ge(w_low, i + 1)
                        if i >= 2:
                            pe.wait_ge(g_act, base + i - 1)
                        for f in range(2):
                            cols = slice(i * P, i * P + w)
                            for q, (weights, x) in enumerate(((w1_hi, x_hi), (w1_lo, x_hi), (w1_hi, x_lo))):
                                mm = nc.tensor.matmul(bank[i % 2][0:w, :], weights[:, f, cols], x[:, f, :],
                                                      start=(f == 0 and q == 0), stop=(f == 1 and q == 2))
                        mm.then_inc(g_mm, 1)
                    m = i - MOE_LEAD
                    if 0 <= m < size:
                        w = tiles[m]
                        if m == 0:
                            pe.wait_ge(r_comb, k + 1)
                            for b in range(CB):
                                mm = nc.tensor.transpose(bank[3][:, b * P:(b + 1) * P], comb_tok[:, b, :], ident)
                            mm.then_inc(r_tr, 1)
                            pe.wait_ge(r_combT, k + 1)
                        if m >= 2:
                            pe.wait_ge(h_done, base + m - 1)
                        nc.tensor.matmul(bank[2 + m % 2][0:w, :], sel[:, m * P:m * P + w], combT[:, :],
                                         start=True, stop=True).then_inc(u_mm, 1)
                    if m == size and n + 1 < STAGES:
                        for f in range(2):
                            transpose_x(n + 1, f)
                    m -= MOE_DOWN_LAG
                    if m >= 0:
                        w = tiles[m]
                        pe.wait_ge(h_low, SPLIT_BASE[n] + m + 1)
                        if m == 0:
                            pe.wait_ge(resid_done, 2 * 14)
                            pe.wait_ge(yT_act, SPLIT[n])
                            pe.wait_ge(yT_dve, SPLIT[n])
                        for f in range(2):
                            cols = slice(f * P, (f + 1) * P)
                            high, low = w2_high(A_r, H_r, m)[0:w, cols], w2_lo[0:w, m, cols]
                            h_hi, h_lo = h_hi_ring[m % 4][0:w, :], h_lo_ring[m % 4][0:w, :]
                            for q, (weights, h) in enumerate(((high, h_hi), (low, h_hi), (high, h_lo))):
                                mm = nc.tensor.matmul(bank[6 + f][:, :], weights, h, start=(m == 0 and q == 0),
                                                      stop=(m == size - 1 and q == 2))
                        mm.then_inc(moe_d, 1)
                pe.wait_ge(xT_cp, 2 * STAGES)
                turn_back(n)

            def turn_back(n):
                pe.wait_ge(yT_act, SPLIT[n] + 1)
                pe.wait_ge(yT_dve, SPLIT[n] + 1)
                pe.wait_ge(resid_done, 2 * n)
                for b in range(CB):
                    for f in range(2):
                        cols = slice((b % 2) * D + f * P, (b % 2) * D + (f + 1) * P)
                        mm = nc.tensor.transpose(bank[Y_BANKS[n][b // 2]][:, cols], yT[f][:, b * P:(b + 1) * P], ident)
                    if b % 2:
                        mm.then_inc(y_ready, 1)

            def ffn2(n):
                c, base, tiles = n % 2, FFN_BASE[n], TILES[5]
                size = len(tiles)
                pe.wait_ge(ff2_cast, 3)
                pe.wait_ge(x_low, X_SPLIT[n] + 1)
                for i in range(size + FF2_DOWN_LAG):
                    if i < size:
                        w = tiles[i]
                        if i >= 2:
                            pe.wait_ge(g_act, base + i - 1)
                            pe.wait_ge(h_done, base + i - 1)
                        if i == 1:
                            pe.wait_ge(resid_done, 2 * n)
                        for at, weights, counts in ((0, ff2_gate, g_mm), (2, ff2_up, u_mm)):
                            for f in range(2):
                                for q, x in enumerate((x_hi2, x_lo)):
                                    mm = nc.tensor.matmul(bank[at + i % 2][0:w, :], weights[:, f, i * P:i * P + w],
                                                          x[:, f, :], start=(f == 0 and q == 0),
                                                          stop=(f == 1 and q == 1))
                            mm.then_inc(counts, 1)
                    if i < CB:
                        project_kv(n, i)
                    m = i - FF2_DOWN_LAG
                    if m == size - 1 and c:
                        project(n + 1, 0)
                    if m >= 0:
                        w = tiles[m]
                        pe.wait_ge(h_low, SPLIT_BASE[n] + m + 1)
                        if m == 0:
                            pe.wait_ge(resid_done, 20)
                            if c:
                                pe.wait_ge(yT_act, 1)
                                pe.wait_ge(yT_dve, 1)
                        for f in range(2):
                            for q, h in enumerate((h_hi_ring2, h_lo_ring)):
                                mm = nc.tensor.matmul(bank[6 + f][:, :], ff2_down[0:w, m, f * P:(f + 1) * P],
                                                      h[m % 3][0:w, :], start=(m == 0 and q == 0),
                                                      stop=(m == size - 1 and q == 1))
                        mm.then_inc(ff2_d, 1)
                    if 1 <= i <= CB:
                        turn_k(n, i - 1)
                    if i == size + 1:
                        pe.wait_ge(c_v, B + CB * c + CB)
                        pe.wait_ge(c_kT, B + CB * c + CB)
                        for f in range(2):
                            transpose_x(n + 1, f)
                pe.wait_ge(xT_cp, 2 * n + 4)
                turn_back(n)

            def fp8(n):
                pe.wait_ge(xT_cp, 2 * n + 2)
                pe.wait_ge(w8_ready, 1)
                pe.wait_ge(resid_done, 2 * n)
                for j in range(2):
                    for b in (2 * j, 2 * j + 1):
                        for f in range(2):
                            mm = nc.tensor.matmul(bank[6 + j][:, (b % 2) * D:(b % 2 + 1) * D],
                                                  xqT[:, f, b * P:(b + 1) * P], w8[:, f, :],
                                                  start=(f == 0), stop=(f == 1))
                    mm.then_inc(y_ready, 1)

            def narrow(n):
                s = n // 2
                na = NAR[s]

                def turn(t):
                    bt = na.batch_base + t
                    pe.wait_ge(n_tok, bt + 1)
                    if bt:
                        pe.wait_ge(n_qT, bt)
                    if t == CB // 2 + 1:
                        pe.wait_ge(xT_cp, 2 * n + 4)
                    for f in range(2):
                        mm = nc.tensor.transpose(bank[2][:, f * P:(f + 1) * P], q_tok[:, f * P:(f + 1) * P], ident)
                    mm.then_inc(n_tr, 1)

                def finish(t):
                    pe.wait_ge(n_otc, na.batch_base + t + 1)
                    for f in range(2):
                        if f == 0 and t % 2 == 0:
                            pe.wait_ge(resid_done, 2 * n + max(t // 2 - 1, 0))
                        mm = nc.tensor.matmul(bank[6 + t // 2 % 2][:, (t % 2) * D:(t % 2 + 1) * D],
                                              n_out[:, f * P:(f + 1) * P], nout[s][:, f, :],
                                              start=(f == 0), stop=(f == 1))
                    if t % 2:
                        mm.then_inc(y_ready, 1)

                steps = list(na.steps())
                turn(0)
                project(n, 1)
                for i in range(len(steps) + OUT_LAG + 1):
                    if i < len(steps):
                        t, f, g, k, gi = steps[i]
                        bt = na.batch_base + t
                        pe.wait_ge(n_qT, bt + 1)
                        if gi >= 2:
                            pe.wait_ge(n_ex, gi - 1)
                        dst = bank[3 + gi % 2]
                        if f == "dca":
                            for ff in range(2):
                                mm = nc.tensor.matmul(dst[:, ff * P:(ff + 1) * P], nqT[bt % 2][:, ff * P:(ff + 1) * P],
                                                      kdca[:, ff, t, :, :], start=True, stop=True)
                        else:
                            who, count = na.spread(t, f)
                            pe.wait_ge(n_kbd_g if who == "gpsimd" else n_kbd_v, count)
                            w = 4 * na.keys
                            mm = nc.tensor.matmul(dst[:, 0:w], nqT[bt % 2][:, f * P:(f + 1) * P],
                                                  kbd[f][:, g * w:(g + 1) * w], start=True, stop=True)
                        mm.then_inc(n_s, 1)
                    if i in na.turn_steps:
                        m, f = na.turn_steps[i]
                        if (m, f) != (1, 0):
                            pe.wait_ge(xT_cp, 2 * (n + m) + f)
                        transpose_x(n + m, f)
                    j = i - OUT_LAG - 1
                    if j >= 0 and steps[j][3] == na.n - 1:
                        finish(steps[j][0])
                    j = i - TURN_LAG
                    if 0 <= j < len(steps):
                        t, f, g, k, gi = steps[j]
                        pe.wait_ge(n_pn, gi + 1)
                        if gi:
                            who, count = na.turned_copy(gi - 1)
                            pe.wait_ge(n_ptc_a if who == "scalar" else n_ptc_v, count)
                        for u in range(2 if f == "dca" else 4):
                            w = P if f == "dca" else na.keys
                            mm = nc.tensor.transpose(bank[5][0:w, u * P:(u + 1) * P],
                                                     np_ring[gi % 6][:, u * w:(u + 1) * w], ident)
                        mm.then_inc(n_ptm, 1)
                    j = i - OUT_LAG
                    if 0 <= j < len(steps):
                        t, f, g, k, gi = steps[j]
                        bt = na.batch_base + t
                        dst = bank[0]
                        who, count = na.turned_copy(gi)
                        pe.wait_ge(n_ptc_a if who == "scalar" else n_ptc_v, count)
                        if k == 0:
                            if bt:
                                pe.wait_ge(n_otc, bt)
                        if f == "dca":
                            for ff in range(2):
                                mm = nc.tensor.matmul(dst[:, ff * P:(ff + 1) * P],
                                                      vdca[:, t, ff * P:(ff + 1) * P],
                                                      npt_ring[gi % 2][:, ff * P:(ff + 1) * P],
                                                      start=False, stop=True, skip_group_check=True)
                        else:
                            pe.wait_ge(n_vpad, 2 * bt + f + 1)
                            for u in range(4):
                                h = 4 * g + u
                                mm = nc.tensor.matmul(dst[:, f * P:(f + 1) * P],
                                                      vpad[f][0:na.keys, h * P:(h + 1) * P],
                                                      npt_ring[gi % 2][0:na.keys, u * P:(u + 1) * P],
                                                      start=(k == 0 and u == 0), stop=(h == na.heads - 1),
                                                      skip_group_check=True)
                        mm.then_inc(n_otm, 1)
                    if i < len(steps) and steps[i][3] == na.q_step and steps[i][0] + 1 < B:
                        turn(steps[i][0] + 1)
                        if steps[i][0] + 2 < B:
                            project(n, steps[i][0] + 2)

            pe.wait_ge(ld["const"], 16)
            pe.wait_ge(ld["ctx"], 16)
            for b in range(B):
                mm = nc.tensor.transpose(bank[4 + b // 4][:, (b % 4) * P:(b % 4 + 1) * P], ctx_tok[:, b, :], ident)
            mm.then_inc(ctxT_mm, 1)
            pe.wait_ge(ctxT_cp, 1)
            for n in range(STAGES):
                kind = KIND[n // 2]
                if n == 7:
                    pe.wait_ge(ld["L2"], 64)
                    weight_products(4)
                if kind == NARROW and n % 2:
                    continue
                if n in (7, 8):
                    for f in range(2):
                        transpose_x(n, f)
                {WIDE: wide, FFN: {1: ffn, 5: ffn2, 7: moe}.get(n // 2), NARROW: narrow, FP8: fp8}[kind](n)

        @block.scalar
        def _(act):
            def copy_xT(n, f):
                act.wait_ge(xT_mm, 2 * n + f + 1)
                dst = xqT[:, f, :] if n // 2 == 3 else xT[:, n % 2, f, :]
                nc.scalar.activation(dst, bank[turn_bank(n, f)][:, :], ACT.Copy).then_inc(xT_cp, 1)

            def high_m(h):
                nc.scalar.activation(L2_m_high(h), L2_m[:, :, h, :], ACT.Copy).then_inc(m_high, 1)

            def copy_products(which):
                base = 0 if which == 0 else 8
                for u in range(8 if which == 0 else 16):
                    act.wait_ge(pre_mm, base + u + 1)
                    src = bank[2 + (base + u) % 4]
                    if which == 4 and u < 8:
                        dst = L2_m[:, :, 2 * u:2 * u + 2, :]
                        src = src[:, :].rearrange("p (f h n) -> p f h n", f=2, h=2)
                    else:
                        dst = out_w[which][:, 2 * (u % 8):2 * (u % 8) + 2, :]
                        src = src[:, :].rearrange("p (h n) -> p h n", h=2)
                    nc.scalar.activation(dst, src, ACT.Copy).then_inc(pre_cp, 1)
                    if which == 4 and u >= 8:
                        if u == 8:
                            act.wait_ge(pre_cp, 16)
                            act.wait_ge(y_ready, 12)
                            act.wait_ge(resid_done, 12)
                        high_m(u - 8)

            def keys0(a, b):
                for g in range(4):
                    u = 4 * b + g
                    act.wait_ge(k_mm, 16 * a + u + 1)
                    if u >= 2:
                        act.wait_ge(k_red, 16 * a + u - 1)
                    src = bank[2 + u % 2][:, :]
                    nc.scalar.activation(q2_ring[u % 2], src, ACT.Square).then_inc(k_sq, 1)
                    nc.scalar.activation(heads[:, 4 * g:4 * g + 4, b * P:(b + 1) * P],
                                         src.rearrange("p (h d) -> p h d", h=4), ACT.Copy).then_inc(k_cp, 1)

            def wide(n):
                a, c, s = WIDE_INDEX[n], n % 2, n // 2
                base = HEADS * a
                if n == 0:
                    for b in range(CB):
                        keys0(0, b)
                    for f in range(2):
                        copy_xT(0, f)
                    copy_products(0)
                    act.wait_ge(ld["rows"], 160)
                    nc.scalar.activation(tg[:, :], gates[:, :], ACT.Tanh).then_inc(tg_ready, 1)
                    act.wait_ge(trig_arg, 1)
                    nc.scalar.activation(trig[:, 4:6, :], trig[:, 2:4, :], ACT.Sin).then_inc(trig_sin, 1)
                if s == 0:
                    act.wait_ge(gqk_set, 1)
                    act.wait_ge(k_red, 16 * a + 16)
                else:
                    if c:
                        act.wait_ge(q_mm, base)
                    act.wait_ge(xT_cp, 2 * n + 2)
                    nc.scalar.activation(x_hi4, xT[:, c, :, :], ACT.Copy).then_inc(x_high, 1)
                for i in range(HEADS + 3):
                    if i < HEADS:
                        act.wait_ge(q_mm, base + i + 1)
                        if i >= 2:
                            act.wait_ge(s_mm, base + i - 1)
                        nc.scalar.activation(q_ring[i % 2], bank[0][:, :], ACT.Copy).then_inc(q_cp, 1)
                        if n == 8 and i + 8 < HEADS:
                            high_m(i + 8)
                        if s == 0:
                            nc.scalar.activation(q2_ring[i % 2], bank[0][:, :], ACT.Square).then_inc(q_sq, 1)
                            act.wait_ge(kT_mm, base + i + 1)
                            nc.scalar.activation(heads[:, i, :], bank[1][:, :], ACT.Copy, scale=gqk[:, 2:3])\
                                .then_inc(kT_cp, 1)
                    h = i - 3
                    if 0 <= h < HEADS:
                        act.wait_ge(pt_mm, base + h + 1)
                        if h >= 2:
                            act.wait_ge(ot_mm, base + h - 1)
                        nc.scalar.activation(pt_ring[h % 2], bank[4][:, :], ACT.Copy).then_inc(pt_cp, 1)
                    h = i - 1
                    if 0 <= h < HEADS:
                        act.wait_ge(nb, base + h + 1)
                        if h >= 4:
                            act.wait_ge(pt_mm, base + h - 3)
                        for b in range(CB):
                            cols = slice(b * P, (b + 1) * P)
                            e = nc.scalar.activation(
                                p_ring[h % 4][:, cols], bank[2 + h % 2][:, cols], ACT.Exp,
                                bias=neg_max[:, h, b:b + 1],
                                scale=q_rstd[:, h, b:b + 1] if s == 0 else float(P) ** -0.5,
                                accum_out=row_sum[:, h, b:b + 1])
                        e.then_inc(ex, 1)
                for f in range(2):
                    copy_xT(n + 1, f)
                if n == 0:
                    for b in range(CB):
                        keys0(1, b)

            def ffn(n):
                s, c = n // 2, n % 2
                base, tiles = FFN_BASE[n], TILES[s]

                def high_weights(i):
                    for which in range(2):
                        m = nc.scalar.activation(ff0_high(which, i), ff0[which][:, :, i * P:(i + 1) * P], ACT.Copy)
                    m.then_inc(w0_high, 1)

                if n == 3:
                    act.wait_ge(u_mm, base)
                act.wait_ge(xT_cp, 2 * n + 2)
                nc.scalar.activation(x_hi2, xT[:, c, :, :], ACT.Copy).then_inc(x_high, 1)
                if n == 2:
                    act.wait_ge(fp4_done, 24)
                    act.wait_ge(y_ready, 4)
                    high_weights(0)
                    high_weights(1)
                for i in range(len(tiles) + 1):
                    if n == 2 and i + 2 < len(tiles):
                        high_weights(i + 2)
                    if i % 3 == 2 and 1 <= (i - 2) // 3 <= CB:
                        copy_kT(s + 1, CB * c + (i - 2) // 3 - 1)
                    if i == len(tiles):
                        break
                    w = tiles[i]
                    act.wait_ge(g_mm, base + i + 1)
                    if i >= 2:
                        act.wait_ge(h_done, base + i - 1)
                    dst = act_ring[i % 2][0:w, :]
                    nc.scalar.activation(dst, bank[i % 2][0:w, :], ACT.Gelu_apprx_tanh).then_inc(g_act, 1)
                    if n == 2 and i == 1:
                        act.wait_ge(wq_mm, 1)
                        nc.scalar.activation(A[:, 0:512], bank[4][:, :], ACT.Copy).then_inc(wq_cp, 1)
                for f in range(2):
                    copy_xT(n + 1, f)

            def copy_kT(s, t):
                act.wait_ge(c_tr, NAR[s].batch_base + t + 1)
                nc.scalar.activation(kT_all[:, t, :, :], bank[5][:, 0:256].rearrange("p (f k) -> p f k", f=2),
                                     ACT.Copy).then_inc(c_kT, 1)

            def ffn2(n):
                c, base, tiles = n % 2, FFN_BASE[n], TILES[5]
                size = len(tiles)
                act.wait_ge(ld["late"], 64)
                if c:
                    act.wait_ge(u_mm, base)
                act.wait_ge(xT_cp, 2 * n + 2)
                nc.scalar.activation(x_hi2, xT[:, c, :, :], ACT.Copy).then_inc(x_high, 1)
                for i in range(size + 1):
                    if 1 <= i <= CB:
                        copy_kT(6, CB * c + i - 1)
                    if i < size:
                        w = tiles[i]
                        act.wait_ge(g_mm, base + i + 1)
                        if i >= 2:
                            act.wait_ge(h_done, base + i - 1)
                        nc.scalar.activation(act_ring[i % 2][0:w, :], bank[i % 2][0:w, :], ACT.Silu,
                                             scale=ffn2_scale[0:w, 0, i:i + 1]).then_inc(g_act, 1)
                    m = i - 1
                    if m >= 0:
                        w = tiles[m]
                        act.wait_ge(h_done, base + m + 1)
                        if size * c + m >= 3:
                            act.wait_ge(ff2_d, size * c + m - 2)
                        nc.scalar.activation(h_hi_ring2[m % 3][0:w, :], h_ring[m % 3][0:w, :], ACT.Copy)\
                            .then_inc(h_high, 1)
                for f in range(2):
                    copy_xT(n + 1, f)
                act.wait_ge(ff2_d, size * (c + 1))
                act.wait_ge(y_ready, 2 * n)
                nc.scalar.activation(yT[0], bank[6][:, :], ACT.Copy).then_inc(yT_act, 1)

            def moe(n):
                c, k, base, tiles = n % 2, n - 14, FFN_BASE[n], TILES[7]
                size = MOE_TILES

                def high_weights(i):
                    w = tiles[i]
                    nc.scalar.activation(w1_hi[:, :, i * P:i * P + w], moe_w1[:, :, i * P:i * P + w], ACT.Copy)
                    nc.scalar.activation(w2_high(A_r, H_r, i), moe_w2[:, i, :], ACT.Copy).then_inc(w_high, 1)

                if k == 0:
                    act.wait_ge(y_ready, 28)
                    act.wait_ge(ld["moe1"], 16)
                    act.wait_ge(ld["ff2"], 128)
                else:
                    act.wait_ge(g_mm, base)
                act.wait_ge(xT_cp, 2 * n + 2)
                nc.scalar.activation(x_hi, xT[:, c, :, :], ACT.Copy).then_inc(x_high, 1)
                if k == 0:
                    high_weights(0)
                    high_weights(1)
                act.wait_ge(r_mm, k + 1)
                nc.scalar.activation(score[:, :, :], bank[2][:, 0:64].rearrange("p (b e) -> p b e", b=CB),
                                     ACT.Sigmoid).then_inc(r_sig, 1)
                for i in range(size + MOE_LEAD):
                    if k == 0 and i + 2 < size:
                        high_weights(i + 2)
                    if i < size:
                        w = tiles[i]
                        act.wait_ge(g_mm, base + i + 1)
                        if i >= 12:
                            act.wait_ge(h_done, base + i - 11)
                        nc.scalar.activation(moe_act[i % 12][0:w, :], bank[i % 2][0:w, :], ACT.Silu)\
                            .then_inc(g_act, 1)
                    m = i - MOE_LEAD
                    if m >= 0:
                        w = tiles[m]
                        act.wait_ge(h_done, base + m + 1)
                        if size * k + m >= 4:
                            act.wait_ge(moe_d, size * k + m - 3)
                        nc.scalar.activation(h_hi_ring[m % 4][0:w, :], moe_h[m % 4][0:w, :], ACT.Copy)\
                            .then_inc(h_high, 1)
                if n + 1 < STAGES:
                    for f in range(2):
                        copy_xT(n + 1, f)
                act.wait_ge(moe_d, size * (k + 1))
                if k:
                    act.wait_ge(y_ready, 2 * n)
                nc.scalar.activation(yT[0], bank[6][:, :], ACT.Copy).then_inc(yT_act, 1)

            def narrow(n):
                s = n // 2
                na = NAR[s]

                def copy_qT(t):
                    bt = na.batch_base + t
                    act.wait_ge(n_tr, bt + 1)
                    if s == 2:
                        nc.scalar.activation(nqT[bt % 2], bank[2][:, 0:256], ACT.Identity, bias=qn_col[:, 1:2],
                                             scale=qn_col[:, 0:1]).then_inc(n_qT, 1)
                    else:
                        nc.scalar.activation(nqT[bt % 2], bank[2][:, 0:256], ACT.Copy).then_inc(n_qT, 1)

                steps = list(na.steps())
                copy_qT(0)
                for i in range(len(steps) + OUT_LAG):
                    j = i - TURN_LAG
                    if 0 <= j < len(steps) and na.turned_copy(steps[j][4])[0] == "scalar":
                        t, f, g, k, gi = steps[j]
                        act.wait_ge(n_ptm, gi + 1)
                        if gi >= 2:
                            act.wait_ge(n_otm, gi - 1)
                        w, m = (P, 256) if f == "dca" else (na.keys, 512)
                        nc.scalar.activation(npt_ring[gi % 2][0:w, 0:m], bank[5][0:w, 0:m], ACT.Copy)\
                            .then_inc(n_ptc_a, 1)
                    if i < len(steps):
                        t, f, g, k, gi = steps[i]
                        act.wait_ge(n_nb, gi + 1)
                        if gi >= 6:
                            act.wait_ge(n_ptm, gi - 5)
                        if f == "dca":
                            nc.scalar.activation(np_ring[gi % 6][:, 0:256], dca_diff, ACT.Exp,
                                                 scale=na.scale).then_inc(n_ex, 1)
                        else:
                            for u in range(4):
                                cols = slice(u * na.keys, (u + 1) * na.keys)
                                e = nc.scalar.activation(np_ring[gi % 6][:, cols], bank[3 + gi % 2][:, cols], ACT.Exp,
                                                         bias=n_max[:, gi % 6, u:u + 1], scale=na.scale,
                                                         accum_out=n_sum[:, gi % 6, u:u + 1])
                            e.then_inc(n_ex, 1)
                    if i in na.turn_steps:
                        m, f = na.turn_steps[i]
                        copy_xT(n + m, f)
                    j = i - OUT_LAG
                    if 0 <= j < len(steps) and steps[j][3] == na.n - 1:
                        t, f, g, k, gi = steps[j]
                        act.wait_ge(n_otm, gi + 1)
                        nc.scalar.activation(n_out, bank[0][:, 0:256], ACT.Copy).then_inc(n_otc, 1)
                    if i < len(steps) and steps[i][3] == na.q_step and steps[i][0] + 1 < B:
                        copy_qT(steps[i][0] + 1)

            act.wait_ge(ctxT_mm, 1)
            for i in range(2):
                m = nc.scalar.activation(ctxT[:, 4 * i:4 * i + 4, :].rearrange("p b k -> p (b k)"), bank[4 + i][:, :],
                                         ACT.Copy)
            m.then_inc(ctxT_cp, 1)
            for n in range(STAGES):
                kind = KIND[n // 2]
                if n == 7:
                    copy_products(4)
                if n in (7, 8):
                    for f in range(2):
                        copy_xT(n, f)
                if kind == NARROW and n % 2 == 0:
                    narrow(n)
                elif kind in (WIDE, FFN):
                    {WIDE: wide, FFN: {1: ffn, 5: ffn2, 7: moe}.get(n // 2)}[kind](n)

        @block.gpsimd
        def _(pool):
            def broadcast(ap, shape):
                return ap.unsqueeze(2).broadcast_to(shape)

            def selection():
                rows = sel.rearrange("p (e j) -> p e j", e=EXPERTS + 1)
                nc.gpsimd.memset(sel, 0.0).then_inc(sel_chain, 1)
                for k in range(3):
                    pool.wait_ge(sel_chain, k + 1)
                    nc.gpsimd.affine_select(out=rows, in_=rows, compare_op=ALU.not_equal, fill=1.0,
                                            base=-(EXPERTS + 1) * k, pattern=[[-1, EXPERTS + 1], [0, MOE_H]],
                                            channel_multiplier=1).then_inc(sel_chain, 1)

            def wide(n):
                a, s = WIDE_INDEX[n], n // 2
                base = HEADS * a
                if s == 0:
                    pool.wait_ge(k_rstd, a + 1)
                    pool.wait_ge(k_cp, 16 * a + 16)
                    for h in range(1, HEADS, 2):
                        v = heads[:, h, :].rearrange("p (b d) -> p b d", b=CB)
                        nc.gpsimd.tensor_tensor(v, v, broadcast(k_ss[:, h, :], [P, CB, P]), ALU.mult)\
                            .then_inc(k_scaled_g, 1)
                def low_m(h):
                    pool.wait_ge(m_high, h + 1)
                    nc.gpsimd.tensor_tensor(L2_m_lo[:, :, h, :], L2_m[:, :, h, :], L2_m_high(h).bitcast(F32),
                                            ALU.subtract).then_inc(m_low, 1)

                if n == 8:
                    for h in range(8):
                        low_m(h)
                for h in range(HEADS):
                    pool.wait_ge(rs, base + h + 1)
                    v = p_ring[h % 4].rearrange("p (b k) -> p b k", b=CB)
                    nc.gpsimd.tensor_tensor(v, v, broadcast(row_sum[:, h, :], [P, CB, P]), ALU.mult)\
                        .then_inc(p_norm, 1)
                    if n == 8 and h + 8 < HEADS:
                        low_m(h + 8)

            def narrow(n):
                s = n // 2
                na = NAR[s]

                def pad_v(t, f):
                    bt = na.batch_base + t
                    if t == 0:
                        pool.wait_ge(c_v, na.batch_base + B)
                    else:
                        pool.wait_ge(n_otm, na.group_base + (t - 1) * na.n + (f + 1) * na.groups)
                    dst = bass.AP(vpad[f].tensor, vpad[f].offset,
                                  [list(vpad[f].ap[0]), [P + na.hd, na.heads], [1, na.hd]])
                    nc.gpsimd.tensor_copy(
                        dst, v_all[:, t, f * P:(f + 1) * P].rearrange("p (h d) -> p h d", d=na.hd))\
                        .then_inc(n_vpad, 1)

                def spread_k(t, f):
                    if t == 0:
                        pool.wait_ge(c_kT, na.batch_base + B)
                    else:
                        pool.wait_ge(n_s, na.group_base + (t - 1) * na.n + (f + 1) * na.groups)
                    shape = [P, na.heads, na.keys]
                    nc.gpsimd.tensor_tensor(
                        kbd[f][:, 0:na.heads * na.keys].rearrange("p (h k) -> p h k", h=na.heads),
                        kT_all[:, t, f, 0:na.keys].unsqueeze(1).broadcast_to(shape),
                        head_mask[s].unsqueeze(2).broadcast_to(shape), ALU.mult).then_inc(n_kbd_g, 1)

                steps = list(na.steps())
                if s == 2:
                    pool.wait_ge(w8_ready, 1)
                own = [f for f in range(2) if na.spread(0, f)[0] == "gpsimd"]
                for f in own:
                    spread_k(0, f)
                if s == 2:
                    pool.wait_ge(y_ready, 8)
                    nc.gpsimd.memset(H[:, 4096:8192], 0.0).then_inc(vpad_zero, 1)
                pool.wait_ge(vpad_zero, 1 if s == 2 else 2)
                pad_v(0, 0)
                pad_v(0, 1)
                for i, (t, f, g, k, gi) in enumerate(steps):
                    pool.wait_ge(n_rs, gi + 1)
                    m, w = (16, 16) if f == "dca" else (4, na.keys)
                    v = np_ring[gi % 6][:, 0:m * w].rearrange("p (h k) -> p h k", h=m)
                    nc.gpsimd.tensor_tensor(v, v, broadcast(n_sum[:, gi % 6, 0:m], [P, m, w]), ALU.mult)\
                        .then_inc(n_pn, 1)
                    for f in range(2):
                        if t and k == (f + 1) * na.groups + OUT_LAG - 1 - na.n:
                            pad_v(t, f)
                    for f in own:
                        if k == min((f + 1) * na.groups, na.n - 1) and t + 1 < B:
                            spread_k(t + 1, f)

            for n in range(STAGES):
                if n in (2, 10):
                    pool.wait_ge(y_ready, 2 * n)
                    if n == 2:
                        for i in range(len(TILES[1])):
                            if i == 2:
                                dca_keys = ctxT[:, :, 112:128]
                                nc.gpsimd.tensor_copy(dca_ctx.rearrange("p (b k) -> p b k", b=B), dca_keys)\
                                    .then_inc(dca_copied, 1)
                                nc.gpsimd.tensor_copy(dca_ctx8.rearrange("p b (r k) -> p b r k", r=8),
                                                      dca_keys.unsqueeze(2).broadcast_to([P, B, 8, 16])).then_inc(dca_copied, 1)
                            pool.wait_ge(w0_high, i + 1)
                            for which in range(2):
                                cols = slice(i * P, (i + 1) * P)
                                m = nc.gpsimd.tensor_tensor(ff0_lo[which][:, :, cols], ff0[which][:, :, cols],
                                                            ff0_high(which, i).bitcast(F32), ALU.subtract)
                            m.then_inc(w0_low, 1)
                if n == 10:
                    nc.gpsimd.memset(H[:, 4096:8192], 0.0).then_inc(vpad_zero, 1)
                    pool.wait_ge(resid_done, 12)
                    selection()
                if KIND[n // 2] == WIDE:
                    wide(n)
                elif KIND[n // 2] == NARROW and n % 2 == 0:
                    narrow(n)
                elif n == 14:
                    for i, w in enumerate(TILES[7]):
                        pool.wait_ge(w_high, i + 1)
                        cols = slice(i * P, i * P + w)
                        nc.gpsimd.tensor_tensor(w1_lo[:, :, cols], moe_w1[:, :, cols], w1_hi[:, :, cols].bitcast(F32),
                                                ALU.subtract)
                        nc.gpsimd.tensor_tensor(w2_lo[:, i, :], moe_w2[:, i, :], w2_high(A_r, H_r, i).bitcast(F32), ALU.subtract)\
                            .then_inc(w_low, 1)

        @block.vector
        def _(dve):
            count = [0]

            def link(ins):
                count[0] += 1
                ins.then_inc(v_chain, 1)
                dve.wait_ge(v_chain, count[0])

            def mark(ins):
                count[0] += 1
                ins.then_inc(v_chain, 1)
                return count[0]

            def tt(o, a, b, op):
                return nc.vector.tensor_tensor(o, a, b, op)

            def ts(o, a, s1, s2, op0, op1=ALU.bypass):
                return nc.vector.tensor_scalar(o, a, s1, s2, op0, op1) if s2 is not None else \
                    nc.vector.tensor_scalar(o, a, s1, None, op0)

            def stt(o, a, s, b, op0, op1):
                return nc.vector.scalar_tensor_tensor(o, a, s, b, op0, op1)

            def rsqrt(dst, v, scale, eps, width, ss_index=0):
                x, y, t = (newton[:, k, 0:width] for k in range(3))
                if ss_index:
                    ts(x, v, scale, eps, ALU.mult, ALU.add).then_inc(ss_read, 1)
                    dve.wait_ge(ss_read, ss_index)
                else:
                    link(ts(x, v, scale, eps, ALU.mult, ALU.add))
                link(ts(t.bitcast(I32), x.bitcast(I32), 1, None, ALU.logical_shift_right))
                link(ts(y.bitcast(I32), t.bitcast(I32), -1.0, RSQRT_SEED, ALU.mult, ALU.add))
                for k in range(3):
                    link(tt(t, y, y, ALU.mult))
                    link(stt(t, t, -0.5, x, ALU.mult, ALU.mult))
                    if k < 2:
                        link(stt(y, t, 1.5, y, ALU.add, ALU.mult))
                return stt(dst, t, 1.5, y, ALU.add, ALU.mult)

            def quantise(v, t, u, scale):
                link(ts(v, v, scale, None, ALU.mult))
                link(ts(t.bitcast(U32), v.bitcast(U32), 0x7F800000, None, ALU.bitwise_and))
                link(ts(t, t, 2.0 ** -6, 1.5 * 2.0 ** 20, ALU.max, ALU.mult))
                link(tt(u, v, t, ALU.add))
                link(tt(v, u, t, ALU.subtract))
                link(ts(t, v, 1.1 * 2.0 ** 119, None, ALU.mult))
                return stt(v, t, 0.0, v, ALU.mult, ALU.add)

            def moments(n, batches=range(CB)):
                lo, hi = batches[0], batches[-1] + 1
                for b in batches:
                    m = mark(nc.vector.bn_stats(stats[:, b, :], x_sb[:, CB * (n % 2) + b, :]))
                dve.wait_ge(v_chain, m)
                for b in batches:
                    m = mark(nc.vector.bn_aggr(mv[:, b, :], stats[:, b, :]))
                dve.wait_ge(v_chain, m)
                link(rsqrt(x_rstd[:, lo:hi], mv[:, lo:hi, 1], 1.0, 1e-5, hi - lo))

            def centre_rows(n, batches=range(CB)):
                c = n % 2
                if n >= 2:
                    dve.wait_ge(xT_mm, 2 * n - 2)
                for b in batches:
                    m = mark(ts(xn[:, c, b, :], x_sb[:, CB * c + b, :], mv[:, b, 0:1], x_rstd[:, b:b + 1],
                                ALU.subtract, ALU.mult))
                dve.wait_ge(v_chain, m)

            def normalise(n):
                centre_rows(n)
                nc.vector.nop().then_inc(ln_done, 1)

            def quantise_rows(n, batches):
                rows = xn[:, n % 2, batches[0]:batches[-1] + 1, :].rearrange("p b d -> p (b d)")
                w = rows.shape[-1]
                link(quantise(rows, q8_tmp[0][:, 0:w], q8_tmp[1][:, 0:w], scales8[:, 0:1]))
                if batches[-1] == CB - 1:
                    nc.vector.nop().then_inc(ln_done, 1)

            def layer_norm(n):
                moments(n)
                normalise(n)

            def residual(n, j):
                s, c = n // 2, n % 2
                dve.wait_ge(y_ready, 2 * n + j + 1)
                x = x_sb[:, CB * c + 2 * j:CB * c + 2 * j + 2, :]
                y = bank[Y_BANKS[n][j] if n in SPLIT else 6 + j][:, :].rearrange("p (b d) -> p b d", b=2)
                gate = tg[:, s // 2 + 4 * (s % 2):s // 2 + 4 * (s % 2) + 1]
                if s == 3:
                    gate = scales8[:, 2:3]
                if s == 5:
                    if j:
                        dve.wait_ge(resid_done, 2 * n + 1)
                    t = R[:, 4096:4608].rearrange("p (b d) -> p b d", b=2)
                    link(tt(t, y, down_scale.unsqueeze(1).broadcast_to([P, 2, D]), ALU.mult))
                    i = stt(x, t, gate, x, ALU.mult, ALU.add)
                elif s in (2, 6):
                    t = X[:, 768:1024]
                    link(ts(t, out_bias[s], gate, None, ALU.mult))
                    link(tt(x, x, t.unsqueeze(1).broadcast_to([P, 2, D]), ALU.add))
                    i = stt(x, y, gate, x, ALU.mult, ALU.add)
                else:
                    i = stt(x, y, gate, x, ALU.mult, ALU.add)
                i.then_inc(resid_done, 1)

            def rsqrt_and_unpack(dst, v, scale, eps, width, ss_index, p, high):
                x, y, t = (newton[:, k, 0:width] for k in range(3))
                packed, block_scale = fp4_slot[p % 3]
                bits, biased = fp4_tmp[0], fp4_tmp[1]
                if not high:
                    dve.wait_ge(ld[f"fp4_{p % 3}"], 32 * (p // 3 + 1))
                ts(x, v, scale, eps, ALU.mult, ALU.add).then_inc(ss_read, 1)
                u0 = mark(ts(bits.bitcast(I32), packed.bitcast(I32), 24 if high else 28, 6,
                             ALU.logical_shift_left, ALU.arith_shift_right))
                dve.wait_ge(ss_read, ss_index)
                r1 = mark(ts(t.bitcast(I32), x.bitcast(I32), 1, None, ALU.logical_shift_right))
                dve.wait_ge(v_chain, u0)
                u1 = mark(ts(bits.bitcast(U32), bits.bitcast(U32), 0x81C00000, None, ALU.bitwise_and))
                dve.wait_ge(v_chain, r1)
                r2 = mark(ts(y.bitcast(I32), t.bitcast(I32), -1.0, RSQRT_SEED, ALU.mult, ALU.add))
                dve.wait_ge(v_chain, u1)
                u2 = mark(ts(biased, bits, 2.0 ** -120, 2.0 ** 126, ALU.add, ALU.mult))
                dve.wait_ge(v_chain, r2)
                r3 = mark(tt(t, y, y, ALU.mult))
                dve.wait_ge(v_chain, u2)
                stt(ff0[p // 4][:, high, 512 * (p % 4):512 * (p % 4) + 512], biased, -64.0, block_scale,
                    ALU.add, ALU.mult).then_inc(fp4_done, 1)
                dve.wait_ge(v_chain, r3)
                link(stt(t, t, -0.5, x, ALU.mult, ALU.mult))
                link(stt(y, t, 1.5, y, ALU.add, ALU.mult))
                link(tt(t, y, y, ALU.mult))
                link(stt(t, t, -0.5, x, ALU.mult, ALU.mult))
                link(stt(y, t, 1.5, y, ALU.add, ALU.mult))
                link(tt(t, y, y, ALU.mult))
                link(stt(t, t, -0.5, x, ALU.mult, ALU.mult))
                link(stt(dst, t, 1.5, y, ALU.add, ALU.mult))
                dve.wait_ge(fp4_done, 2 * p + high + 1)

            def keys0(a, b):
                for g in range(4):
                    u = 4 * b + g
                    dve.wait_ge(k_sq, 16 * a + u + 1)
                    nc.vector.tensor_reduce(k_ss[:, 4 * g:4 * g + 4, b],
                                            q2_ring[u % 2].rearrange("p (h d) -> p h d", h=4), AX, ALU.add)\
                        .then_inc(k_red, 1)

            def scale_keys0(a):
                dve.wait_ge(k_red, 16 * a + 16)
                flat = k_ss[:, :, :].rearrange("p h b -> p (h b)")
                rsqrt(flat, flat, 1.0 / P, 1e-5, 64).then_inc(k_rstd, 1)
                dve.wait_ge(k_rstd, a + 1)
                dve.wait_ge(k_cp, 16 * a + 16)
                for h in range(0, HEADS, 2):
                    v = heads[:, h, :].rearrange("p (b d) -> p b d", b=CB)
                    tt(v, v, k_ss[:, h, :].unsqueeze(2).broadcast_to([P, CB, P]), ALU.mult)\
                        .then_inc(k_scaled_v, 1)

            def wide(n):
                a, c, s = WIDE_INDEX[n], n % 2, n // 2
                base = HEADS * a
                if n == 0:
                    for b in range(CB):
                        keys0(0, b)
                    scale_keys0(0)
                    angles()
                elif n == 8:
                    low_x(8)
                    ts(mask_bias, mask8[:, :], 1.0, NEG, ALU.subtract, ALU.mult).then_inc(mask_set, 1)
                    nc.vector.tensor_reduce(any_valid[:, :], mask8[:, :].rearrange("p (b k) -> p b k", b=B), AX,
                                            ALU.max).then_inc(mask_set, 1)
                    dve.wait_ge(mask_set, 2)
                for i in range(HEADS + 4):
                    h = i - 1
                    if 0 <= h < HEADS:
                        if s == 0:
                            dve.wait_ge(ss_mm, base + h + 1)
                            ss = bank[6][:, :].rearrange("p (b k) -> p b k", b=CB)[:, :, 0]
                            k = HEADS * c + h
                            if k < 24:
                                rsqrt_and_unpack(q_rstd[:, h, :], ss, 1.0 / P, 1e-5, CB, base + h + 1, k // 2, k % 2)
                            else:
                                link(rsqrt(q_rstd[:, h, :], ss, 1.0 / P, 1e-5, CB, base + h + 1))
                    h = i - 2
                    if 0 <= h < HEADS:
                        dve.wait_ge(ex, base + h + 1)
                        if s == 0:
                            nc.vector.reciprocal(row_sum[:, h, :], row_sum[:, h, :]).then_inc(rs, 1)
                        else:
                            link(nc.vector.reciprocal(row_sum[:, h, :], row_sum[:, h, :]))
                            tt(row_sum[:, h, :], row_sum[:, h, :], any_valid[:, CB * c:CB * c + CB], ALU.mult)\
                                .then_inc(rs, 1)
                    h = i - 1
                    if 0 <= h < HEADS:
                        dve.wait_ge(s_mm, base + h + 1)
                        sc = bank[2 + h % 2][:, :]
                        if s != 0:
                            link(tt(sc, sc, mask_bias[:, CT * c:CT * (c + 1)], ALU.add))
                        link(nc.vector.tensor_reduce(neg_max[:, h, :], sc.rearrange("p (b k) -> p b k", b=CB), AX,
                                                     ALU.max))
                        if s == 0:
                            stt(neg_max[:, h, :], neg_max[:, h, :], -1.0, q_rstd[:, h, :], ALU.mult, ALU.mult)\
                                .then_inc(nb, 1)
                        else:
                            ts(neg_max[:, h, :], neg_max[:, h, :], -float(P) ** -0.5, None, ALU.mult)\
                                .then_inc(nb, 1)
                    h = i - 4
                    if 0 <= h < HEADS:
                        dve.wait_ge(ot_mm, base + h + 1)
                        nc.vector.tensor_copy(heads[:, h, :], bank[5 + 2 * (h % 2)][:, :]).then_inc(ot_cp, 1)
                    if i == 4:
                        if n == 0:
                            dve.wait_ge(ld["x1"], 16)
                        moments(n + 1)
                    if i == 8:
                        normalise(n + 1)
                    if n == 0 and i == HEADS:
                        rotations()
                    if n == 9 and i == 10:
                        cast_ff2()

            def cast_ff2():
                dve.wait_ge(ld["ff2"], 128)
                for k, (lo, hi) in enumerate(((0, 1408), (1408, 2816), (2816, 4352))):
                    v = Bw[:, lo:hi]
                    ts(Bw_r[:, lo:hi], v.bitcast(I32), -128.0, None, ALU.add).then_inc(ff2_cast, 1)

            def route_dve(n):
                k = n - 13
                dve.wait_ge(r_sig, k)
                sg = score[:, :, :].rearrange("p b (g j) -> p (b g) j", j=4)
                m, top2, pair = route[:, 0, :], route[:, 1, 0:16], route[:, 1, 16:32]
                first = True
                for u in range(4):
                    for v in range(u + 1, 4):
                        if first:
                            link(tt(top2, sg[:, :, u], sg[:, :, v], ALU.add))
                        else:
                            link(tt(pair, sg[:, :, u], sg[:, :, v], ALU.add))
                            link(tt(top2, top2, pair, ALU.max))
                        first = False

                def in_top2(dst, v, tie, size, ra, rb):
                    shape = [P, CB, size, size]
                    other, own = v.unsqueeze(2).broadcast_to(shape), v.unsqueeze(3).broadcast_to(shape)
                    link(tt(ra, other, own, ALU.is_equal))
                    link(tt(ra, ra, tie.unsqueeze(1).broadcast_to(shape), ALU.mult))
                    link(tt(rb, other, own, ALU.is_gt))
                    link(tt(ra, ra, rb, ALU.add))
                    link(nc.vector.tensor_reduce(dst, ra, AX, ALU.add))
                    link(ts(dst, dst, 2.0, None, ALU.is_lt))

                gsel = route[:, 2, 0:16].rearrange("p (b g) -> p b g", b=CB)
                in_top2(gsel, top2.rearrange("p (b g) -> p b g", b=CB), tie4, 4,
                        route_a[:, :, 0:4, 0:4], route_b[:, :, 0:4, 0:4])
                masked = m.rearrange("p (b e) -> p b e", b=CB)
                link(tt(m.rearrange("p (g j) -> p g j", j=4), sg,
                        route[:, 2, 0:16].unsqueeze(2).broadcast_to([P, 16, 4]), ALU.mult))
                chosen = route[:, 3, :].rearrange("p (b e) -> p b e", b=CB)
                in_top2(chosen, masked, tie16, 16, route_a, route_b)
                link(tt(chosen, chosen, masked, ALU.mult))
                total = route[:, 4, 0:CB]
                link(nc.vector.tensor_reduce(total, chosen, AX, ALU.add))
                link(ts(total, total, 1e-20, None, ALU.add))
                link(nc.vector.reciprocal(total, total))
                if n == 14:
                    link(nc.vector.memset(comb_tok, 0.0))
                    link(nc.vector.memset(comb_tok[:, :, 16:17], 1.0))
                else:
                    dve.wait_ge(r_tr, 1)
                link(tt(chosen, chosen, total.unsqueeze(2).broadcast_to([P, CB, 16]), ALU.mult))
                part = route[:, 5, 0:32].bitcast(BF16).rearrange("p (b e) -> p b e", b=CB)
                for q in range(3):
                    link(nc.vector.tensor_copy(part, chosen))
                    dst = comb_tok[:, :, 17 * q:17 * q + 16]
                    if q < 2:
                        link(nc.vector.tensor_copy(dst, part))
                        link(tt(chosen, chosen, dst, ALU.subtract))
                    else:
                        nc.vector.tensor_copy(dst, part).then_inc(r_comb, 1)
                dve.wait_ge(r_tr, k)
                nc.vector.tensor_copy(combT, bank[3][:, :]).then_inc(r_combT, 1)

            def ffn(n):
                s, c = n // 2, n % 2
                base, tiles = FFN_BASE[n], TILES[s]
                if n == 2:
                    stt(demean, dca_mask, -1.0 / 16, ident, ALU.mult, ALU.add).then_inc(centring, 1)
                    subtract_mean(q_bias.rearrange("p (h d) -> p h d", d=16), newton_wide[:, 0, 0:16], 16)
                for i, w in enumerate(tiles):
                    dve.wait_ge(g_act, base + i + 1)
                    dve.wait_ge(u_mm, base + i + 1)
                    if i >= 3:
                        dve.wait_ge(d_mm, DOWN_BASE[n] + i - 2)
                    up, ga, dst = bank[2 + i % 2][0:w, :], act_ring[i % 2][0:w, :], h_ring[i % 3][0:w, :]
                    tt(dst, up, ga, ALU.mult).then_inc(h_done, 1)
                    j, part = divmod(i - 2, 3)
                    if n == 3 and i == 0:
                        dca_k_norm()
                    if n == 3 and i == 4:
                        dca_k_spread()
                    if n == 2 and i in DCA_V_STEPS:
                        dca_v(DCA_V_STEPS.index(i))
                    if 0 <= j < CB and part < 2:
                        norm_k(c, j, part)
                    if n == 3 and i == 15:
                        quantise_w8()
                    if i == len(tiles) - 3:
                        layer_norm(n + 1)

            def low_x(n):
                dve.wait_ge(xT_cp, 2 * n + 2)
                dve.wait_ge(x_high, X_SPLIT[n] + 1)
                high = x_hi4 if n in (8, 9) else x_hi2 if n < 12 else x_hi
                if n == 9:
                    dve.wait_ge(q_mm, 3 * HEADS)
                if n == 3:
                    dve.wait_ge(u_mm, FFN_BASE[n])
                tt(x_lo, xT[:, n % 2, :, :], high.bitcast(F32), ALU.subtract).then_inc(x_low, 1)

            def ffn2(n):
                c, base, tiles = n % 2, FFN_BASE[n], TILES[5]
                size = len(tiles)
                dve.wait_ge(ld["late"], 64)
                for i in range(size + 1):
                    if i < CB:
                        rope_k(c, i)
                    if i < size:
                        w = tiles[i]
                        dve.wait_ge(g_act, base + i + 1)
                        dve.wait_ge(u_mm, base + i + 1)
                        if size * c + i >= 3:
                            dve.wait_ge(ff2_d, size * c + i - 2)
                        stt(h_ring[i % 3][0:w, :], bank[2 + i % 2][0:w, :], ffn2_scale[0:w, 1, i:i + 1],
                            act_ring[i % 2][0:w, :], ALU.mult, ALU.mult).then_inc(h_done, 1)
                    m = i - 1
                    if m >= 0:
                        w = tiles[m]
                        dve.wait_ge(h_high, SPLIT_BASE[n] + m + 1)
                        tt(h_lo_ring[m % 3][0:w, :], h_ring[m % 3][0:w, :], h_hi_ring2[m % 3][0:w, :].bitcast(F32),
                           ALU.subtract).then_inc(h_low, 1)
                    if i == 0:
                        moments(n + 1)
                    if i == 2:
                        normalise(n + 1)
                dve.wait_ge(ff2_d, size * (c + 1))
                dve.wait_ge(y_ready, 2 * n)
                nc.vector.tensor_copy(yT[1], bank[7][:, :]).then_inc(yT_dve, 1)

            def moe(n):
                c, k, base, tiles = n % 2, n - 14, FFN_BASE[n], TILES[7]
                size = MOE_TILES
                route_dve(n)
                if k:
                    residual(14, 0)
                    residual(14, 1)
                for i in range(size + 1):
                    if i < size:
                        w = tiles[i]
                        dve.wait_ge(g_act, base + i + 1)
                        dve.wait_ge(u_mm, base + i + 1)
                        if size * k + i >= 4:
                            dve.wait_ge(moe_d, size * k + i - 3)
                        tt(moe_h[i % 4][0:w, :], bank[2 + i % 2][0:w, :], moe_act[i % 12][0:w, :], ALU.mult)\
                            .then_inc(h_done, 1)
                    if k == 0 and i == 4:
                        moments(15, (2, 3))
                    if k == 0 and i == 6:
                        centre_rows(15, (2, 3))
                        nc.vector.nop().then_inc(ln_done, 1)
                    m = i - 1
                    if m >= 0:
                        w = tiles[m]
                        dve.wait_ge(h_high, SPLIT_BASE[n] + m + 1)
                        tt(h_lo_ring[m % 4][0:w, :], moe_h[m % 4][0:w, :], h_hi_ring[m % 4][0:w, :].bitcast(F32),
                           ALU.subtract).then_inc(h_low, 1)
                dve.wait_ge(moe_d, size * (k + 1))
                if k:
                    dve.wait_ge(y_ready, 2 * n)
                nc.vector.tensor_copy(yT[1], bank[7][:, :]).then_inc(yT_dve, 1)

            def quantise_w8():
                flat = w8_raw.rearrange("p k n -> p (k n)")
                dve.wait_ge(ld["L1"], 80)
                link(quantise(flat, w8_tmp[0], w8_tmp[1], scales8[:, 1:2]))
                nc.vector.tensor_copy(w8[:, :, :], w8_raw).then_inc(w8_ready, 1)

            def norm_k(c, j, part):
                t = CB * c + j
                v = k_tok.rearrange("p (h d) -> p h d", d=16)
                if part == 0:
                    dve.wait_ge(c_kv, t + 1)
                    if t == 0:
                        dve.wait_ge(ld["L1rows"], 128)
                    else:
                        dve.wait_ge(c_tr, t)
                    kv = bank[4][:, :].rearrange("p (h z d) -> p h z d", z=2, d=16)
                    bias = kv_bias.rearrange("p (h z d) -> p h z d", z=2, d=16)
                    link(tt(v, kv[:, :, 0, :], bias[:, :, 0, :], ALU.add))
                    tt(v_all[:, t, :].rearrange("p (h d) -> p h d", d=16), kv[:, :, 1, :], bias[:, :, 1, :],
                       ALU.add).then_inc(c_v, 1)
                    centre(v, k_tmp.rearrange("p (h d) -> p h d", d=16), 16)
                else:
                    rescale(v, 16, 1e-6, kn_w.unsqueeze(1), kn_b.unsqueeze(1), [P, 16, 16])\
                        .then_inc(c_tok, 1)
                    dve.wait_ge(c_tok, t + 1)

            def rope(dst, tmp, src, b):
                pairs = src.rearrange("p (h q e) -> p h q e", q=4, e=2)
                out_ = tmp.rearrange("p (h q e) -> p h q e", q=4, e=2)
                link(tt(dst.rearrange("p (h q) -> p h q", q=8), src.rearrange("p (h q) -> p h q", q=8),
                        cosx[:, b, :, :].rearrange("p q e -> p (q e)").unsqueeze(1).broadcast_to([P, 32, 8]),
                        ALU.mult))
                for e in range(2):
                    link(tt(out_[:, :, :, e], pairs[:, :, :, 1 - e],
                            sinx[:, b, :, e].unsqueeze(1).broadcast_to([P, 32, 4]), ALU.mult))
                return tt(dst, dst, tmp, ALU.add)

            def rope_k(c, j):
                t = CB * c + j
                dve.wait_ge(c_kv, B + t + 1)
                dve.wait_ge(c_tr, B + t)
                i = rope(k_tok, k_tmp, bank[4][:, 0:256], t)
                i.then_inc(c_tok, 1)
                nc.vector.tensor_copy(v_all[:, t, :], bank[4][:, 256:512]).then_inc(c_v, 1)
                dve.wait_ge(c_tok, B + t + 1)

            def subtract_mean(v, mean, m):
                width = v.shape[-1]
                link(nc.vector.tensor_reduce(mean, v, AX, ALU.add))
                link(ts(mean, mean, -1.0 / width, None, ALU.mult))
                link(tt(v, v, mean.unsqueeze(2).broadcast_to([P, m, width]), ALU.add))

            def square_sum(v, t, total):
                link(tt(t, v, v, ALU.mult))
                link(nc.vector.tensor_reduce(total, t, AX, ALU.add))

            def weigh(v, rstd, w, b, shape):
                link(tt(v, v, rstd.unsqueeze(2).broadcast_to(shape), ALU.mult))
                link(tt(v, v, w.broadcast_to(shape), ALU.mult))
                return tt(v, v, b.broadcast_to(shape), ALU.add)

            def centre(v, t, m):
                mean = newton_wide[:, 0, 0:m]
                subtract_mean(v, mean, m)
                square_sum(v, t, mean)

            def rescale(v, m, eps, w, b, shape):
                mean, rstd = newton_wide[:, 0, 0:m], newton_wide[:, 1, 0:m]
                link(rsqrt(rstd, mean, 1.0 / v.shape[-1], eps, m))
                return weigh(v, rstd, w, b, shape)

            def dca_k_norm():
                dve.wait_ge(dca_mm, B + 1)
                link(tt(dca_tok, bank[5][:, 0:256], dca_bias[:, 0:256], ALU.add))
                v = dca_tok.rearrange("p (h d) -> p h d", d=16)
                centre(v, dca_tmp.rearrange("p (h d) -> p h d", d=16), 16)
                link(rescale(v, 16, 1e-6, dca_lnw.unsqueeze(1), dca_lnb.unsqueeze(1), [P, 16, 16]))
                nc.vector.nop().then_inc(dca_norm, 1)

            def dca_k_spread():
                dve.wait_ge(dca_tr, 1)
                for f in range(2):
                    src = bank[5][:, f * P:(f + 1) * P].rearrange("p (b k) -> p b k", b=B)
                    shape = [P, B, 8, 16]
                    tt(kdca[:, f, :, :, :], src.unsqueeze(2).broadcast_to(shape),
                       head_mask[2].unsqueeze(1).unsqueeze(3).broadcast_to(shape), ALU.mult).then_inc(dca_ready, 1)

            def dca_v(b):
                dve.wait_ge(dca_mm, b + 1)
                link(tt(vdca[:, b, :], bank[5][:, 0:256], dca_bias[:, 256:512], ALU.add))
                v = vdca[:, b, :].rearrange("p (f k) -> p f k", f=2)
                tt(v, v, dca_mask.unsqueeze(1).broadcast_to([P, 2, P]), ALU.mult).then_inc(dca_ready, 1)

            def spread_k(na, t, f):
                if t == 0:
                    dve.wait_ge(c_kT, na.batch_base + B)
                else:
                    dve.wait_ge(n_s, na.group_base + (t - 1) * na.n + (f + 1) * na.groups)
                shape = [P, na.heads, na.keys]
                tt(kbd[f][:, 0:na.heads * na.keys].rearrange("p (h k) -> p h k", h=na.heads),
                   kT_all[:, t, f, 0:na.keys].unsqueeze(1).broadcast_to(shape),
                   head_mask[na.s].unsqueeze(2).broadcast_to(shape), ALU.mult).then_inc(n_kbd_v, 1)

            def tokens(s, t, part):
                bt = NAR[s].batch_base + t
                if part == 0:
                    dve.wait_ge(n_q, bt + 1)
                    if bt:
                        dve.wait_ge(n_tr, bt)
                v = q_tok.rearrange("p (h d) -> p h d", d=16)
                mean, rstd = newton_wide[:, 0, 0:16], newton_wide[:, 1, 0:16]
                if s == 2 and part == 0:
                    link(tt(q_tok, bank[1][:, 0:256], q_bias, ALU.add))
                    square_sum(v, q_tmp.rearrange("p (h d) -> p h d", d=16), mean)
                elif s == 2 and part == 1:
                    link(rsqrt(rstd, mean, 1.0 / 16, 1e-6, 16))
                elif s == 2 and part == 2:
                    tt(v, v, rstd.unsqueeze(2).broadcast_to([P, 16, 16]), ALU.mult).then_inc(n_tok, 1)
                    dve.wait_ge(n_tok, bt + 1)
                elif s == 6 and part == 0:
                    rope(q_tok, q_tmp, bank[1][:, 0:256], t).then_inc(n_tok, 1)
                    dve.wait_ge(n_tok, bt + 1)

            def narrow(n):
                s = n // 2
                na = NAR[s]

                steps = list(na.steps())
                if s == 2:
                    dve.wait_ge(w8_ready, 1)
                own = [f for f in range(2) if na.spread(0, f)[0] == "vector"]
                for i in range(len(steps) + OUT_LAG + 9):
                    if i < len(steps):
                        t, f, g, k, gi = steps[i]
                        dve.wait_ge(n_s, gi + 1)
                        m, w = (16, 16) if f == "dca" else (4, na.keys)
                        sc = bank[3 + gi % 2][:, 0:m * w].rearrange("p (h k) -> p h k", h=m)
                        top = n_max[:, gi % 6, 0:m]
                        link(nc.vector.tensor_reduce(top, sc, AX, ALU.max))
                        if f == "dca":
                            tt(dca_diff.rearrange("p (h k) -> p h k", h=16), sc,
                               top.unsqueeze(2).broadcast_to([P, 16, 16]), ALU.subtract).then_inc(n_nb, 1)
                        else:
                            ts(top, top, -na.scale, None, ALU.mult).then_inc(n_nb, 1)
                    j = i - 1
                    if 0 <= j < len(steps):
                        t, f, g, k, gi = steps[j]
                        dve.wait_ge(n_ex, gi + 1)
                        m = 16 if f == "dca" else 4
                        total = n_sum[:, gi % 6, 0:m]
                        if f == "dca":
                            link(nc.vector.tensor_reduce(
                                total, np_ring[gi % 6][:, 0:256].rearrange("p (h k) -> p h k", h=16), AX, ALU.add))
                        nc.vector.reciprocal(total, total).then_inc(n_rs, 1)
                    for part, later in enumerate((0, 2, 3, 7, 8)):
                        j = i - OUT_LAG - 1 - later
                        if not 0 <= j < len(steps) or steps[j][3] != na.n - 1 or steps[j][0] % 2 == 0:
                            continue
                        t = steps[j][0]
                        m, pair = n + 2 + t // CB, (t % CB - 1, t % CB)
                        if part == 0:
                            residual(n + t // CB, t // 2 % 2)
                        elif part == 1:
                            dve.wait_ge(resid_done, 2 * n + 1 + t // 2)
                            if m == 15 and t == B - 1:
                                low_x(14)
                                continue
                            moments(m, pair)
                        elif part == 2 and not (m == 15 and t == B - 1):
                            centre_rows(m, pair)
                            if s == 6 and pair[1] == CB - 1:
                                nc.vector.nop().then_inc(ln_done, 1)
                        elif s == 2:
                            quantise_rows(m, pair[part - 3:part - 2])
                    if i == 2:
                        moments(n + 1)
                    if i == 4:
                        normalise(n + 1)
                    j = i - TURN_LAG
                    if 0 <= j < len(steps) and na.turned_copy(steps[j][4])[0] == "vector":
                        t, f, g, k, gi = steps[j]
                        dve.wait_ge(n_ptm, gi + 1)
                        if gi >= 2:
                            dve.wait_ge(n_otm, gi - 1)
                        w, m = (P, 256) if f == "dca" else (na.keys, 512)
                        nc.vector.tensor_copy(npt_ring[gi % 2][0:w, 0:m], bank[5][0:w, 0:m]).then_inc(n_ptc_v, 1)
                    if i < len(steps):
                        t, f, g, k, gi = steps[i]
                        if i == 0:
                            tokens(s, 1, 0)
                        later, part = divmod(i + 1, na.n)
                        if later + 1 < B and part <= 3:
                            tokens(s, later + 1, part)
                        if t + 1 < B:
                            for f in own:
                                if k == min((f + 1) * na.groups, na.n - 1):
                                    spread_k(na, t + 1, f)

            def angles():
                dve.wait_ge(ld["rows"], 160)
                ts(gqk[:, 2:3], gqk[:, 0:1], gqk[:, 1:2], float(P) ** -0.5, ALU.mult, ALU.mult).then_inc(gqk_set, 1)
                ang, turns, args = trig[:, 0, :], trig[:, 1, :], trig[:, 2:4, :]
                for half, freq in enumerate((1.0, 0.01)):
                    link(ts(ang.rearrange("p (b q e) -> p b q e", b=B, q=2)[:, :, :, half], fside[:, :, :], freq, None,
                            ALU.mult))
                magic = 1.5 * 2.0 ** 23
                link(ts(turns, ang, 1.0 / 6.283185307179586, magic, ALU.mult, ALU.add))
                link(ts(turns, turns, -magic, None, ALU.add))
                link(stt(ang, turns, -6.28125, ang, ALU.mult, ALU.add))
                link(stt(ang, turns, -(6.283185307179586 - 6.28125), ang, ALU.mult, ALU.add))
                link(ts(args[:, 1, :], ang, 1.5707963267948966, None, ALU.add))
                link(ts(turns, args[:, 1, :], 3.1415925, -6.283185307179586, ALU.is_gt, ALU.mult))
                link(tt(args[:, 1, :], args[:, 1, :], turns, ALU.add))
                link(ts(args[:, 1, :], args[:, 1, :], 3.1415925, -3.1415925, ALU.min, ALU.max))
                ts(args[:, 0, :], ang, 3.1415925, -3.1415925, ALU.min, ALU.max).then_inc(trig_arg, 1)

            def rotations():
                dve.wait_ge(trig_sin, 1)
                sin = trig[:, 4, :].rearrange("p (b q) -> p b q", b=B)
                cos = trig[:, 5, :].rearrange("p (b q) -> p b q", b=B)
                link(nc.vector.tensor_copy(cosx[:, :, :, 0], cos))
                link(nc.vector.tensor_copy(cosx[:, :, :, 1], cos))
                link(ts(sinx[:, :, :, 0], sin, -1.0, None, ALU.mult))
                link(nc.vector.tensor_copy(sinx[:, :, :, 1], sin))
                dve.wait_ge(tg_ready, 1)
                link(nc.vector.reciprocal(scales8[:, 2:4], scales8[:, 0:2]))
                link(tt(scales8[:, 2:3], scales8[:, 2:3], scales8[:, 3:4], ALU.mult))
                link(tt(scales8[:, 2:3], scales8[:, 2:3], tg[:, 5:6], ALU.mult))

            newton_wide = trig[:, 0:2, :]
            nc.vector.memset(ones[:, :], 1.0).then_inc(ones_set, 1)
            dve.wait_ge(ld["x"], 16)
            layer_norm(0)
            for n in range(STAGES):
                kind = KIND[n // 2]
                if n == 2:
                    dve.wait_ge(ld["L1rows"], 128)
                if kind == NARROW:
                    if n % 2 == 0:
                        narrow(n)
                    continue
                if kind == WIDE:
                    wide(n)
                elif n >= 14:
                    moe(n)
                elif kind == FFN:
                    (ffn if n < 4 else ffn2)(n)
                if n == 0:
                    keys0(1, 0)
                    keys0(1, 1)
                    residual(0, 0)
                    keys0(1, 2)
                    keys0(1, 3)
                    scale_keys0(1)
                    residual(0, 1)
                elif n == 14:
                    low_x(15)
                else:
                    if n in (3, 11):
                        for part in range(4):
                            tokens((n + 1) // 2, 0, part)
                    if n == 11:
                        spread_k(NAR[6], 0, 0)
                    if n + 1 in (2, 3, 9, 10, 11):
                        low_x(n + 1)
                    residual(n, 0)
                    residual(n, 1)
                if n == 6:
                    dve.wait_ge(resid_done, 2 * n + 2)
                    layer_norm(8)


def constants(np):
    c = np.zeros((128, 552), np.float32)
    p = np.arange(128)
    c[:, 0:128] = np.eye(128)
    c[:, 128:144] = p[:, None] // 8 == np.arange(16)
    c[:, 144:152] = p[:, None] // 16 == np.arange(8)
    c[:, 152:280] = p[:, None] // 16 == p[None, :] // 16
    for off, size in ((280, 16), (536, 4)):
        e = np.arange(size)
        c[:, off:off + size * size] = (e[None, :] < e[:, None]).reshape(1, -1)
    return c


def kernel(**inputs):
    import numpy as np
    import concourse.bacc as _bacc
    from concourse import mybir as _mybir
    from concourse.bass_utils import run_bass_kernel_spmd as _run

    v = {k: np.asarray(a) for k, a in inputs.items()}

    def by_rows(w, p=128):
        return w.reshape(-1, p, w.shape[-1]).transpose(1, 0, 2).reshape(p, -1)

    def by_pairs(w):
        return np.concatenate([w[:, 0::2], w[:, 1::2]], 1)

    def pad_rows(w, rows):
        return np.concatenate([w, np.zeros((rows - w.shape[0],) + w.shape[1:], w.dtype)], 0)

    def by_heads(w, heads):
        return w.reshape(w.shape[0], heads, -1).transpose(2, 1, 0).reshape(w.shape[1] // heads, -1)

    i = "L0_ffn_"
    host = {
        "consts": constants(np), "x": v["x"], "ctx": v["ctx_1024"], "fside": v["fside_BxSx2_0"],
        "mask": v["mask_BxS2_bf1"].reshape(-1), "g_xattn": v["g_xattn"], "g_ffn": v["g_ffn"],
        "gq": v["L0_xattn_gq"].reshape(128, 1), "gk": v["L0_xattn_gk"].reshape(128, 1),
        "L0_wq": by_rows(v["L0_xattn_Wq"]), "L0_wk": v["L0_xattn_Wk"],
        "L0_wvT": by_heads(v["L0_xattn_Wv"], 16), "L0_wo": by_rows(v["L0_xattn_Wo"]),
        "ff0_gate": by_pairs(v[i + "gate_W_packed"].T), "ff0_gate_s": by_pairs(v[i + "gate_scales"].T),
        "ff0_up": by_pairs(v[i + "up_W_packed"].T), "ff0_up_s": by_pairs(v[i + "up_scales"].T),
        "ff0_down": by_rows(v[i + "down_W_packed"].T), "ff0_down_s": by_rows(v[i + "down_scales"].T, 8),
        "bq": v["L1_xattn_bq"], "bkv": np.concatenate([v["L1_xattn_bk"], v["L1_xattn_bv"]]),
        "bkv_dca": v["L1_xattn_bkv_dca"], "bo": v["L1_xattn_bo"],
        "L1_wq": by_rows(v["L1_xattn_Wq"].T),
        "qn_w_col": np.tile(v["L1_xattn_qn_w"], 8).reshape(128, 1),
        "qn_b_col": np.tile(v["L1_xattn_qn_b"], 8).reshape(128, 1),
        "L1_wkv": np.concatenate([v["L1_xattn_Wk"], v["L1_xattn_Wv"]], 1),
        "L1_dca": v["L1_xattn_Wkv_dca"], "L1_wo": by_rows(v["L1_xattn_Wo"]),
        "w8": by_rows(v["L1_ffn_input2"]), "scale": v["L1_ffn_scale"].reshape(1), "scale1": v["L1_ffn_scale1"].reshape(1),
        "L2_wqT": by_heads(v["L2_xattn_Wq"], 16), "L2_wkT": by_heads(v["L2_xattn_Wk"], 8),
        "L2_wvT": by_heads(v["L2_xattn_Wv"], 8), "L2_wo": by_rows(v["L2_xattn_Wo"]),
        "ff2_gate": by_rows(v["L2_ffn_wq_gate"].T), "ff2_up": by_rows(v["L2_ffn_wq_up"].T),
        "ff2_down": by_rows(pad_rows(v["L2_ffn_wq_down"].T, 768)),
        "s_gate": pad_rows(v["L2_ffn_s_gate"], 768).reshape(6, 128).T,
        "s_up": pad_rows(v["L2_ffn_s_up"], 768).reshape(6, 128).T, "s_down": v["L2_ffn_s_down"],
        "L3_wq": by_rows(v["L3_xattn_Wq"]), "L3_wkv": v["L3_xattn_Wkv"], "L3_wo": by_rows(v["L3_xattn_Wout"]),
        "bout": v["L3_xattn_bout"],
        "moe_w1": by_rows(np.concatenate([v["L3_ffn_w1"], v["L3_ffn_sw1"]]).transpose(1, 0, 2).reshape(256, -1)),
        "moe_w2": by_rows(pad_rows(np.concatenate([v["L3_ffn_w2"], v["L3_ffn_sw2"]]).reshape(-1, 256), 3072)),
        "router": by_rows(v["L3_ffn_gate_w"].T),
    }
    for name in ("kn_w", "kn_b", "kn_dca_w", "kn_dca_b"):
        host[name] = v["L1_xattn_" + name]

    nc = _bacc.Bacc("TRN2", target_bir_lowering=False, num_devices=1)
    arrays, dram = {}, {}
    for name, a in host.items():
        a = np.ascontiguousarray(a)
        arrays["in_" + name] = a
        dram[name] = nc.dram_tensor("in_" + name, a.shape, _mybir.dt.from_np(a.dtype), kind="ExternalInput").ap()
    out = nc.dram_tensor("out_x", (8, 128, 256), _mybir.dt.float32, kind="ExternalOutput").ap()
    build(nc, dram, out)
    r = _run(nc, [arrays], core_ids=[0])
    return r.results[0]["out_x"]
```
